# Optimizing a Trainium2 kernel written in Bass

```python
import numpy as np
import jax
import jax.numpy as jnp

def _softmax(x, axis=-1):
    return jax.nn.softmax(x, axis=axis)

def _gelu(x):
    return jax.nn.gelu(x, approximate=True)

def _silu(x):
    return jax.nn.silu(x)

def _sigmoid(x):
    return jax.nn.sigmoid(x)

def _layernorm(x, axis=-1, eps=1e-05):
    m = jnp.mean(x, axis=axis, keepdims=True)
    v = jnp.var(x, axis=axis, keepdims=True)
    return (x - m) / jnp.sqrt(v + eps)

def _scatter_add(tgt, idx, src, axis=0):
    return tgt.at[idx].add(src)

def _segment_sum(src, seg, n):
    return jax.ops.segment_sum(src, seg, n)
kernel_name = 'mk_adaln_ffn_d2_seqx_r8_902580'

def setup_inputs(seed: int=0):
    np.random.seed(seed)
    _w = jnp.asarray

    def _rec_inputs():
        import jax
        import jax.numpy as jnp
        _rk = jax.random.key(seed)
        x = -0.000125 + 0.9999 * jax.random.normal(jax.random.fold_in(_rk, 1), (32, 32, 512), jnp.float32)
        _lenS = 32 - jax.random.randint(jax.random.fold_in(_rk, 7), (32,), 0, max(1, 32 // 4) + 1, jnp.int32)
        _lenS2 = 32 - jax.random.randint(jax.random.fold_in(_rk, 8), (32,), 0, max(1, 32 // 4) + 1, jnp.int32)
        cond_128 = 0.0061147 + 1.02565 * jax.random.normal(jax.random.fold_in(_rk, 11), (32, 128), jnp.float32)
        fside_S_0 = -0.022604 + 0.987366 * jax.random.normal(jax.random.fold_in(_rk, 12), (32,), jnp.float32)
        return (x, cond_128, fside_S_0)
    x, cond_128, fside_S_0 = _rec_inputs()

    def _L0_cond_setup():
        import jax, jax.numpy as jnp
        import numpy as np
        from jax import lax
        N, C_IN, L = (32, 32, 512)
        C_OUT, K, GROUPS = (32, 9, 4)
        C_DIM, PAD, STRIDE = (128, 4, 1)
        key = jax.random.key(seed)
        k1, k2, k3, k4, k5 = jax.random.split(key, 5)
        x = jax.random.normal(k1, (N, C_IN, L), dtype=jnp.float32)
        c = jax.random.normal(k2, (N, C_DIM), dtype=jnp.float32)
        weight = jax.random.normal(k3, (C_OUT, C_IN // GROUPS, K), dtype=jnp.float32)
        c_weight = jax.random.normal(k4, (C_OUT, C_DIM), dtype=jnp.float32)
        bias = jax.random.normal(k5, (C_OUT,), dtype=jnp.float32)
        return {'x': x, 'c': c, 'weight': weight, 'c_weight': c_weight, 'bias': bias}
    _L0_cond_all = _L0_cond_setup()
    _L0_cond_in = {k: v for k, v in _L0_cond_all.items() if k in ('weight', 'c_weight')}
    del _L0_cond_all

    def _L0_ffn_setup():
        import jax, jax.numpy as jnp
        import numpy as np
        DIM = 512
        INTER = 128
        E = 16
        GROUPS = 4
        LIM = 2
        K = 2
        SHARED_INTER = 2 * INTER
        SCALE = 1.0
        key = jax.random.key(seed)
        ks = jax.random.split(key, 16)

        def n(k, shape, s=0.02):
            return jax.random.normal(k, shape, jnp.float32) * s
        return {'x': jax.random.normal(ks[0], (1, 256, DIM), jnp.float32), 'router_w': n(ks[1], (DIM, E)), 'router_b': n(ks[2], (E,)), 'router_bias': n(ks[3], (E,), 1.0), 'ew1': n(ks[4], (E, DIM, INTER)), 'eb1': n(ks[5], (E, INTER)), 'ew2': n(ks[6], (E, DIM, INTER)), 'eb2': n(ks[7], (E, INTER)), 'ew3': n(ks[8], (E, INTER, DIM)), 'eb3': n(ks[9], (E, DIM)), 'sw1': n(ks[10], (DIM, SHARED_INTER)), 'sb1': n(ks[11], (SHARED_INTER,)), 'sw2': n(ks[12], (DIM, SHARED_INTER)), 'sb2': n(ks[13], (SHARED_INTER,)), 'sw3': n(ks[14], (SHARED_INTER, DIM)), 'sb3': n(ks[15], (DIM,))}
    _L0_ffn_all = _L0_ffn_setup()
    _L0_ffn_in = {k: v for k, v in _L0_ffn_all.items() if k in ('router_w', 'router_b', 'router_bias', 'ew1', 'eb1', 'ew2', 'eb2', 'ew3', 'eb3', 'sw1', 'sb1', 'sw2', 'sb2', 'sw3', 'sb3')}
    del _L0_ffn_all

    def _L1_cond_setup():
        import jax, jax.numpy as jnp
        import numpy as np
        K = 8
        T = 1.0
        D_EMBD = 128
        IN_C = 32
        OUT_C = 32
        BS = 32
        H = 512
        HID = 128
        key = jax.random.key(seed)
        ks = jax.random.split(key, 10)
        s = lambda fan_in: 1.0 / np.sqrt(fan_in)
        return {'x': jax.random.normal(ks[0], (BS, IN_C, H), dtype=jnp.float32), 'embedding': jax.random.normal(ks[1], (BS, D_EMBD), dtype=jnp.float32), 'W0': jax.random.normal(ks[2], (D_EMBD, HID), dtype=jnp.float32) * s(D_EMBD), 'b0': jnp.zeros((HID,), dtype=jnp.float32), 'W1': jax.random.normal(ks[3], (HID, HID), dtype=jnp.float32) * s(HID), 'b1': jnp.zeros((HID,), dtype=jnp.float32), 'W2': jax.random.normal(ks[4], (HID, K), dtype=jnp.float32) * s(HID), 'b2': jnp.zeros((K,), dtype=jnp.float32), 'weight': jax.random.normal(ks[5], (K, OUT_C, IN_C, 1), dtype=jnp.float32) * s(IN_C), 'bias_k': jax.random.normal(ks[6], (K, OUT_C), dtype=jnp.float32) * 0.1}
    _L1_cond_all = _L1_cond_setup()
    _L1_cond_in = {k: v for k, v in _L1_cond_all.items() if k in ('W0', 'b0', 'W1', 'b1', 'W2', 'b2', 'weight', 'bias_k')}
    del _L1_cond_all

    def _L1_ffn_setup():
        import jax, jax.numpy as jnp
        import numpy as np
        B_L, B_H = (4, 8)
        LIN_SLOPE, LIN_INTER, EST_T = (1.0, 0.0, 64.0)
        BATCH, SEQ, IN_F, OUT_F = (4, 256, 512, 512)
        MAX_BITS = 8

        def dequant_kbit(qweight, lut, bit):
            O, I32 = (qweight.shape[1], qweight.shape[2])
            shifts = jnp.arange(32, dtype=jnp.int32)
            idx = jnp.zeros((O, I32 * 32), dtype=jnp.int32)
            for p in range(bit):
                bits = (qweight[p][:, :, None] >> shifts & 1).reshape(O, I32 * 32)
                idx = idx | bits << p
            return jnp.take_along_axis(lut, idx, axis=1)
        key = jax.random.key(seed)
        k = jax.random.split(key, 5)
        x = jax.random.normal(k[0], (BATCH, SEQ, IN_F), dtype=jnp.float32)
        qweight = jax.random.randint(k[1], (MAX_BITS, OUT_F, IN_F // 32), 0, 2147483647, dtype=jnp.int32)
        lut4 = jax.random.normal(k[2], (OUT_F, 2 ** B_L), dtype=jnp.float32) * 0.02
        lut8 = jax.random.normal(k[3], (OUT_F, 2 ** B_H), dtype=jnp.float32) * 0.02
        bias = jax.random.normal(k[4], (OUT_F,), dtype=jnp.float32) * 0.01
        return {'x': x, 'qweight': qweight, 'lut4': lut4, 'lut8': lut8, 'bias': bias}
    _L1_ffn_all = _L1_ffn_setup()
    _L1_ffn_in = {k: v for k, v in _L1_ffn_all.items() if k in ('qweight', 'lut4', 'lut8', 'bias')}
    del _L1_ffn_all
    return {'x': x, 'cond_128': cond_128, 'fside_S_0': fside_S_0, 'L0_cond_weight': _L0_cond_in['weight'], 'L0_cond_c_weight': _L0_cond_in['c_weight'], 'L0_ffn_router_w': _L0_ffn_in['router_w'], 'L0_ffn_router_b': _L0_ffn_in['router_b'], 'L0_ffn_router_bias': _L0_ffn_in['router_bias'], 'L0_ffn_ew1': _L0_ffn_in['ew1'], 'L0_ffn_eb1': _L0_ffn_in['eb1'], 'L0_ffn_ew2': _L0_ffn_in['ew2'], 'L0_ffn_eb2': _L0_ffn_in['eb2'], 'L0_ffn_ew3': _L0_ffn_in['ew3'], 'L0_ffn_eb3': _L0_ffn_in['eb3'], 'L0_ffn_sw1': _L0_ffn_in['sw1'], 'L0_ffn_sb1': _L0_ffn_in['sb1'], 'L0_ffn_sw2': _L0_ffn_in['sw2'], 'L0_ffn_sb2': _L0_ffn_in['sb2'], 'L0_ffn_sw3': _L0_ffn_in['sw3'], 'L0_ffn_sb3': _L0_ffn_in['sb3'], 'L1_cond_W0': _L1_cond_in['W0'], 'L1_cond_b0': _L1_cond_in['b0'], 'L1_cond_W1': _L1_cond_in['W1'], 'L1_cond_b1': _L1_cond_in['b1'], 'L1_cond_W2': _L1_cond_in['W2'], 'L1_cond_b2': _L1_cond_in['b2'], 'L1_cond_weight': _L1_cond_in['weight'], 'L1_cond_bias_k': _L1_cond_in['bias_k'], 'L1_ffn_qweight': _L1_ffn_in['qweight'], 'L1_ffn_lut4': _L1_ffn_in['lut4'], 'L1_ffn_lut8': _L1_ffn_in['lut8'], 'L1_ffn_bias': _L1_ffn_in['bias']}

def reference(x, cond_128, fside_S_0, L0_cond_weight, L0_cond_c_weight, L0_ffn_router_w, L0_ffn_router_b, L0_ffn_router_bias, L0_ffn_ew1, L0_ffn_eb1, L0_ffn_ew2, L0_ffn_eb2, L0_ffn_ew3, L0_ffn_eb3, L0_ffn_sw1, L0_ffn_sb1, L0_ffn_sw2, L0_ffn_sb2, L0_ffn_sw3, L0_ffn_sb3, L1_cond_W0, L1_cond_b0, L1_cond_W1, L1_cond_b1, L1_cond_W2, L1_cond_b2, L1_cond_weight, L1_cond_bias_k, L1_ffn_qweight, L1_ffn_lut4, L1_ffn_lut8, L1_ffn_bias):
    import jax
    import jax.numpy as jnp

    def _L0_cond_ref(x, c, weight, c_weight, bias):
        import jax, jax.numpy as jnp
        import numpy as np
        from jax import lax
        N, C_IN, L = (32, 32, 512)
        C_OUT, K, GROUPS = (32, 9, 4)
        C_DIM, PAD, STRIDE = (128, 4, 1)
        out = lax.conv_general_dilated(x, weight, window_strides=(STRIDE,), padding=[(PAD, PAD)], dimension_numbers=('NCH', 'OIH', 'NCH'), feature_group_count=GROUPS)
        ctx = jnp.einsum('nd,od->no', c, c_weight)
        out = out + ctx[:, :, None] + bias[None, :, None]
        return out

    def _L0_ffn_ref(x, router_w, router_b, router_bias, ew1, eb1, ew2, eb2, ew3, eb3, sw1, sb1, sw2, sb2, sw3, sb3):
        import jax, jax.numpy as jnp
        import numpy as np
        DIM = 512
        INTER = 128
        E = 16
        GROUPS = 4
        LIM = 2
        K = 2
        SHARED_INTER = 2 * INTER
        SCALE = 1.0
        shape = x.shape
        xt = x.reshape(-1, DIM)
        T = xt.shape[0]
        logits = xt @ router_w + router_b
        scores = jax.nn.softmax(logits.astype(jnp.float32), axis=-1) + router_bias
        g = scores.reshape(T, GROUPS, E // GROUPS)
        _, gidx = jax.lax.top_k(g.max(axis=-1), LIM)
        keep = jnp.zeros((T, GROUPS), bool).at[jnp.arange(T)[:, None], gidx].set(True)
        masked = jnp.where(keep[:, :, None], g, -jnp.inf).reshape(T, E)
        _, idx = jax.lax.top_k(masked, K)
        vals = (jnp.take_along_axis(scores, idx, axis=1) * SCALE).astype(x.dtype)
        gate = jnp.zeros((T, E), x.dtype).at[jnp.arange(T)[:, None], idx].add(vals)

        def step(y, p):
            w1, b1, w2, b2, w3, b3, ge = p
            h = jax.nn.silu(xt @ w1 + b1) * (xt @ w2 + b2)
            return (y + ge[:, None] * (h @ w3 + b3), None)
        y, _ = jax.lax.scan(step, jnp.zeros_like(xt), (ew1, eb1, ew2, eb2, ew3, eb3, gate.T))
        z = jax.nn.silu(xt @ sw1 + sb1) * (xt @ sw2 + sb2) @ sw3 + sb3
        return (y + z).reshape(shape)

    def _L1_cond_ref(x, embedding, W0, b0, W1, b1, W2, b2, weight, bias_k):
        import jax, jax.numpy as jnp
        import numpy as np
        K = 8
        T = 1.0
        D_EMBD = 128
        IN_C = 32
        OUT_C = 32
        BS = 32
        H = 512
        HID = 128
        h = jax.nn.gelu(embedding @ W0 + b0, approximate=False)
        h = jax.nn.gelu(h @ W1 + b1, approximate=False)
        att = jax.nn.softmax((h @ W2 + b2) / T, axis=-1)
        agg_w = jnp.einsum('bk,koi->boi', att, weight[..., 0])
        agg_b = att @ bias_k
        out = jnp.einsum('boi,bih->boh', agg_w, x) + agg_b[:, :, None]
        return out

    def _L1_ffn_ref(x, qweight, lut4, lut8, bias):
        import jax, jax.numpy as jnp
        import numpy as np
        B_L, B_H = (4, 8)
        LIN_SLOPE, LIN_INTER, EST_T = (1.0, 0.0, 64.0)
        BATCH, SEQ, IN_F, OUT_F = (4, 256, 512, 512)
        MAX_BITS = 8

        def dequant_kbit(qweight, lut, bit):
            O, I32 = (qweight.shape[1], qweight.shape[2])
            shifts = jnp.arange(32, dtype=jnp.int32)
            idx = jnp.zeros((O, I32 * 32), dtype=jnp.int32)
            for p in range(bit):
                bits = (qweight[p][:, :, None] >> shifts & 1).reshape(O, I32 * 32)
                idx = idx | bits << p
            return jnp.take_along_axis(lut, idx, axis=1)
        e = jnp.linalg.norm(x, axis=-1) * LIN_SLOPE + LIN_INTER
        mask = e > EST_T
        w_l = dequant_kbit(qweight, lut4, B_L)
        w_h = dequant_kbit(qweight, lut8, B_H)
        y_l = jnp.einsum('bsi,oi->bso', x, w_l)
        y_h = jnp.einsum('bsi,oi->bso', x, w_h)
        y = jnp.where(mask[..., None], y_h, y_l) + bias
        return y
    x = x + _L0_ffn_ref(_L0_cond_ref(x, cond_128, L0_cond_weight, L0_cond_c_weight, fside_S_0), L0_ffn_router_w, L0_ffn_router_b, L0_ffn_router_bias, L0_ffn_ew1, L0_ffn_eb1, L0_ffn_ew2, L0_ffn_eb2, L0_ffn_ew3, L0_ffn_eb3, L0_ffn_sw1, L0_ffn_sb1, L0_ffn_sw2, L0_ffn_sb2, L0_ffn_sw3, L0_ffn_sb3)
    x = x + _L1_ffn_ref(_L1_cond_ref(x, cond_128, L1_cond_W0, L1_cond_b0, L1_cond_W1, L1_cond_b1, L1_cond_W2, L1_cond_b2, L1_cond_weight, L1_cond_bias_k), L1_ffn_qweight, L1_ffn_lut4, L1_ffn_lut8, L1_ffn_bias)
    return x

_drawn_inputs = setup_inputs


def setup_inputs(seed=0):
    import zlib

    import numpy as np

    out = dict(_drawn_inputs(seed))
    spreads = {'L1_cond_b0': (0.0, 0.8), 'L1_cond_b1': (0.0, 0.8), 'L1_cond_b2': (0.0, 0.712)}
    factors = {'L0_ffn_router_b': 8.0,
     'L0_ffn_eb1': 25.072,
     'L0_ffn_eb2': 26.781,
     'L0_ffn_eb3': 28.096,
     'L0_ffn_sb1': 54.318,
     'L0_ffn_sb2': 54.557,
     'L0_ffn_sb3': 64.0,
     'L1_cond_bias_k': 43.647,
     'L1_ffn_bias': 64.0}
    for name, (base, spread) in spreads.items():
        noise = np.random.default_rng([zlib.crc32(name.encode()), seed]).standard_normal(out[name].shape)
        drawn = base * np.exp(spread * noise) if base else spread * noise
        out[name] = jnp.asarray(drawn.astype(out[name].dtype))
    for name, factor in factors.items():
        out[name] = (out[name] * factor).astype(out[name].dtype)
    return out
```

```python
from contextlib import ExitStack

import numpy as np

import concourse.bass as bass
from concourse import mybir

F32 = mybir.dt.float32
BF16 = mybir.dt.bfloat16
I32 = mybir.dt.int32
U16 = mybir.dt.uint16
ALU = mybir.AluOpType
ACT = mybir.ActivationFunctionType
X = mybir.AxisListType.X

P = 128
N, C, L = 32, 32, 512
T = N * C
TT = T // P
NT = P // C
TAPS, GROUPS = 9, 4
S = 4
NB = L // S
D = 128
E, INTER, TOPK = 16, 128, 2
EG = 4
MC = 2
KE = 8
KT = KE * C // P
ET = TOPK * T // P + E - 1
O = 512
OI = P // 8
QT = O // OI
G8 = 8
NG = O // G8
RING = 16
CHUNK = RING // 2
PARTS = 3
LT = L // P
BIG = 3.0e38
EST_SQ = 64.0 ** 2 + 2.0 ** -11

SMALL = [("cT", N), ("cwT", C), ("W0", D), ("W1", D), ("W2", KE), ("b0", 1), ("b1", 1), ("sb1", MC), ("sb2", MC),
         ("wk", KT * C), ("rw", S * E), ("convb", C), ("b2", KE), ("bk", C), ("rb", E), ("rbias", E)]
CONST = [("ident", P), ("iota", P), ("rev", E), ("thr", TT), ("tri", E * E), ("blk", NT), ("dmask", C), ("pidx", 1),
         ("tbase", TT), ("ksel", KT * P), ("upper", P), ("mhi", 2 * P), ("mlo", 2 * P), ("mbias", 1), ("ones8", G8)]


def spans(table):
    at, out = 0, {}
    for name, width in table:
        out[name] = slice(at, at + width)
        at += width
    return out, at


SM, SMALL_W = spans(SMALL)
CO, CONST_W = spans(CONST)


def bc(ap, axis, n):
    u = ap.unsqueeze(axis)
    shape = list(u.shape)
    shape[axis] = n
    return u.to_broadcast(shape)


class Region:

    def __init__(self, flat):
        self.flat, self.at = flat, 0

    def __call__(self, shape, dt=F32):
        size = int(np.prod(shape[1:]))
        words = size * mybir.dt.size(dt) // 4
        ap = self.flat[0:shape[0], self.at:self.at + words]
        self.at += words
        assert self.at <= self.flat.shape[1]
        if dt != F32:
            ap = ap.bitcast(dt)
        names = " ".join(f"d{i}" for i in range(len(shape) - 1))
        return ap.rearrange(f"p ({names}) -> p {names}", **{f"d{i}": n for i, n in enumerate(shape[1:])})


def build(nc, A):
    with ExitStack() as ctx:
        def sb(name, shape, dt=F32):
            return ctx.enter_context(nc.sbuf_tensor(name, shape, dt))

        def sem(name):
            return ctx.enter_context(nc.semaphore(name))

        bank = [ctx.enter_context(nc.psum_tensor(f"bank{i}", [P, 512], F32)) for i in range(8)]

        xc_rows = nc.dram_tensor("xc_rows", (T, L), F32, kind="Internal").ap()
        y_slots = nc.dram_tensor("y_slots", (ET * P, L), F32, kind="Internal").ap()

        small = sb("small", [P, SMALL_W])
        const = sb("const", [P, CONST_W])
        sm = {k: small[:, v] for k, v in SM.items()}
        co = {k: const[:, v] for k, v in CO.items()}
        ident = co["ident"]

        x_rows = sb("x_rows", [P, TT, L])
        x4 = sb("x4", [P, N, NB + 2])
        wconv = sb("wconv", [P, 3, P])
        xcT = sb("xcT", [P, S, T])
        xc_stage = sb("xc_stage", [P, 2, L])
        diag = sb("diag", [P, N, C])
        ctxrep = sb("ctxrep", [P, T])
        ctxb = sb("ctxb", [N, C])
        ones = sb("ones", [P, P])
        ones_bf = sb("ones_bf", [P, P], BF16)
        upper_bf = sb("upper_bf", [P, P], BF16)
        h1T = sb("h1T", [D, N])
        h2T = sb("h2T", [D, N])
        att = sb("att", [N, KE])
        attw = sb("attw", [N, KE + 3])
        attT = sb("attT", [KE, N])
        aggb = sb("aggb", [N, C])
        aggbrep = sb("aggbrep", [P, T])
        bd = sb("bd", [P, TT, P])

        w12 = sb("w12", [P, E, S, 2 * INTER])
        w3 = sb("w3", [INTER, E, L])
        sw12 = sb("sw12", [P, S, 4 * INTER])
        sw3 = sb("sw3", [P, MC, L])
        b3x = sb("b3x", [E + 1, L])
        hs = sb("hs", [P, MC, T])

        al = [a.rearrange("p (n i) -> p n i", n=N) for a in (ctxrep[:], bd[:].rearrange("p t k -> p (t k)"))]

        after_conv = Region(x4[:].rearrange("p n b -> p (n b)"))
        score = sb("score", [P, TT, E])
        ra = sb("ra", [P, TT, E])
        rbuf = sb("rbuf", [P, TT, E])
        rc = sb("rc", [P, TT, E])
        masked = sb("masked", [P, TT, E])
        pick = [sb(f"pick{c}", [P, TT, E]) for c in range(TOPK)]
        gpick = [sb(f"gpick{c}", [P, TT, EG]) for c in range(TOPK)]
        gm = sb("gm", [P, TT, EG])
        gt1 = sb("gt1", [P, TT, EG])
        r1 = sb("r1", [P, TT])
        r2 = sb("r2", [P, TT])
        gate = sb("gate", [P, TOPK, TT])
        gate17 = sb("gate17", [P, TT, E + 1])
        gateT = diag[0:E + 1].rearrange("p n c -> p (n c)")
        sel_bf = sb("sel_bf", [P, TT, E], BF16)
        cntj = sb("cntj", [P, E, TT])
        ntile = sb("ntile", [P, E])
        tri_w = after_conv([P, E, E])
        tstart = sb("tstart", [P, E])
        tend = sb("tend", [P, E])
        slot_f = sb("slot_f", [P, TOPK, TT])
        slot_i = sb("slot_i", [P, TOPK, TT], I32)
        sq_i = sb("sq_i", [P, TOPK, TT], I32)
        sr_i = sb("sr_i", [P, TOPK, TT], I32)
        sq_f = sb("sq_f", [P, TOPK, TT])
        sr_f = sb("sr_f", [P, TOPK, TT])
        silu_s = after_conv([P, 2, 512])
        onehot_r = after_conv([P, TOPK, TT, P], BF16)
        onehot_q = after_conv([P, TOPK, TT, 32])
        tok_p = after_conv([P, TOPK, TT, 32], BF16)
        tok_t = after_conv([P, TOPK, TT, 32], BF16)
        tok_of_slot = sb("tok_of_slot", [P, 32], I32)
        eidw = after_conv([P, 32, E])
        eid_f = sb("eid_f", [P, 32])
        expert_of_tile = sb("expert_of_tile", [P, 32], I32)

        after_shared = Region(xcT[:].rearrange("p j t -> p (j t)"))
        xg = [after_shared([P, L]) for _ in range(2)]
        xgT = [after_shared([P, S, P]) for _ in range(2)]
        h12 = [after_shared([P, 2 * INTER]) for _ in range(2)]
        sil = [after_shared([P, INTER]) for _ in range(2)]
        hid = [after_shared([P, INTER]) for _ in range(2)]
        hidT = [after_shared([INTER, P]) for _ in range(2)]
        b12rep = [after_shared([P, 2 * INTER]) for _ in range(2)]
        y_sb = [xc_stage[:, i] for i in range(2)]
        yg = [hs[:].rearrange("p m t -> p (m t)")[:, L * i:L * i + L] for i in range(4)]

        after_al = Region(ctxrep[:])
        qw = after_al([P, QT, L // 32], I32)
        lut4 = after_al([P, NG, G8])
        bits = Region(x4[:].rearrange("p n b -> p (n b)"))([P, RING, L], BF16)
        lut4_parts = Region(diag[:].rearrange("p n c -> p (n c)"))([P, NG, PARTS, G8], BF16)
        match = Region(wconv[:].rearrange("p d m -> p (d m)"))([P, 2, 2, P], BF16)
        after_down = Region(w3[:].rearrange("p e l -> p (e l)"))
        lut8 = [after_down([P, 2, P]) for _ in range(2)]
        hot_hi = [after_down([P, L]) for _ in range(2)]
        hot_lo = [after_down([P, L], BF16) for _ in range(4)]
        prod = [after_down([P, L]) for _ in range(2)]
        xb = after_down([P, TT, L])
        ybias = after_down([P, L])
        after_up = Region(w12[:].rearrange("p e j m -> p (e j m)"))
        wTh = after_up([P, LT, O])
        wTl = after_up([P, LT, O])
        l4rest = [after_up([P, NG, G8]) for _ in range(2)]
        aT = [after_up([P, LT, P]) for _ in range(2)]
        sq = [after_up([P, LT, P]) for _ in range(2)]
        ysel = [after_up([P, L]) for _ in range(2)]
        tmp_pool = after_up([P, L])
        high = [after_up([P, 1], I32) for _ in range(2)]

        s_small = sem("small_loaded")
        s_const = sem("const_loaded")
        s_x4 = [sem(f"x4_loaded{i}") for i in range(4)]
        s_wconv = sem("wconv_loaded")
        s_xrows = sem("x_rows_loaded")
        s_shared = sem("shared_weights_loaded")
        s_b3 = sem("b3_loaded")
        s_w = sem("expert_weights_loaded")
        s_ones = sem("ones_ready")
        s_masks = sem("masks_ready")
        s_ctx = sem("ctx_summed")
        s_diag = sem("ctx_diag_ready")
        s_ctxrep_mm = sem("ctx_spread")
        s_ctxrep = sem("ctx_on_all_partitions")
        s_h1 = sem("att_h1_summed")
        s_h1T = sem("att_h1_ready")
        s_h2 = sem("att_h2_summed")
        s_h2T = sem("att_h2_ready")
        s_attl = sem("att_logits_summed")
        s_attm = sem("att_logits_shifted")
        s_attex = sem("att_exp_ready")
        s_att = sem("att_ready")
        s_attTp = sem("att_turned")
        s_attT = sem("attT_ready")
        s_attrep = sem("att_spread")
        s_al = sem("att_mix_ready")
        s_agg = sem("agg_summed")
        s_aggbrep = sem("aggb_on_all_partitions")
        s_bd = sem("block_diagonal_ready")
        s_conv = sem("conv_summed")
        s_xcT = sem("conv_ready")
        s_turn = sem("conv_turned")
        s_stage = sem("conv_rows_staged")
        s_xcw = [sem(f"conv_rows_written{i}") for i in range(2)]
        s_logit = sem("router_logits_summed")
        s_rm = sem("router_logits_shifted")
        s_rexp = sem("router_exp_ready")
        s_sel = sem("chosen_ready")
        s_gate = sem("gates_ready")
        s_rank = sem("ranks_summed")
        s_hots = sem("slot_onehots_ready")
        s_toks = sem("slot_tokens_summed")
        s_route = sem("routing_ready")
        s_gTp = sem("gates_turned")
        s_gT = sem("gateT_ready")
        s_sup = sem("shared_up_summed")
        s_silu = sem("shared_silu_ready")
        s_hs = sem("shared_hidden_ready")
        s_z = sem("shared_out_summed")
        s_zadd = sem("shared_out_added")
        s_gather = [sem(f"rows_gathered{i}") for i in range(2)]
        s_xTp = sem("rows_turned")
        s_xTe = sem("rows_turned_copied")
        s_b12 = [sem(f"expert_bias_loaded{i}") for i in range(2)]
        s_up = sem("expert_up_summed")
        s_hb = sem("expert_bias_added")
        s_hsilu = sem("expert_silu_ready")
        s_hg = sem("expert_hidden_ready")
        s_hTp = sem("expert_hidden_turned")
        s_hTe = sem("expert_hidden_turned_copied")
        s_down = sem("expert_down_summed")
        s_ye = sem("expert_out_copied")
        s_yw = [sem(f"expert_out_written{i}") for i in range(2)]
        s_back = [sem(f"out_rows_gathered{i}") for i in range(4)]
        s_comb = sem("out_rows_added")
        s_q = sem("packed_bits_loaded")
        s_l4 = sem("lut4_loaded")
        s_l4p = sem("lut4_split")
        s_match = sem("match_weights_ready")
        s_bits = sem("bit_chunks_ready")
        s_lut8 = [sem(f"lut8_loaded{i}") for i in range(2)]
        s_m = sem("nibbles_matched")
        s_hi = sem("high_onehot_ready")
        s_lo = sem("low_onehot_ready")
        s_G = sem("table_rows_summed")
        s_prod = sem("values_chosen")
        s_s3 = sem("weights_turned")
        s_wev = sem("weights_copied")
        s_ybias = sem("ybias_loaded")
        s_pool = sem("pool_chain")
        s_xb = sem("residual_bias_ready")
        s_amm = sem("linear_input_summed")
        s_aT = sem("linear_input_ready")
        s_sq = sem("squares_ready")
        s_norm = sem("norms_summed")
        s_high = sem("precision_chosen")
        s_ymm = sem("linear_summed")
        s_ylc = sem("low_result_copied")
        s_ysel = sem("result_chosen")
        s_yout = sem("result_ready")
        s_out = [sem(f"result_written{i}") for i in range(2)]
        s_v = sem("vector_chain")
        s_a = sem("scalar_chain")

        def over_tiles(eng, step, last):
            for kk in range(2):
                step(kk, 0)
                step(kk, 1)
            with eng.Fori(2, (ET - 1) // 2) as kk:
                step(kk, 0)
                step(kk, 1)
            for k in range(ET - 1, last + 1):
                step(k // 2, k % 2)

        def over_groups(eng, step):
            for i in range(4):
                step(0, i)
            with eng.Fori(1, NG // 4 - 1) as u:
                for i in range(4):
                    step(u, i)
            for i in range(4):
                step(NG // 4 - 1, i)

        block = ctx.enter_context(nc.Block())

        @block.sync
        def _(sp):
            sp.dma_start(small[:], A["small"]).then_inc(s_small, 16)
            sp.dma_start(wconv[:], A["wconv"]).then_inc(s_wconv, 16)
            for i in range(4):
                sp.dma_start(x4[:, 8 * i:8 * i + 8, :], A["x4"][:, 8 * i:8 * i + 8, :]).then_inc(s_x4[i], 16)
            sp.dma_start(sw12[:], A["sw12"]).then_inc(s_shared, 16)
            sp.dma_start(sw3[:], A["sw3"]).then_inc(s_shared, 16)
            sp.dma_start(b3x[:], A["b3x"]).then_inc(s_b3, 16)
            sp.dma_start(x_rows[:], A["x_rows"]).then_inc(s_xrows, 16)
            for e in range(0, E, 2):
                sp.wait_ge(s_stage, e // 2 + 1)
                sp.dma_start(w12[:, e:e + 2], A["w12"][:, e:e + 2]).then_inc(s_w, 16)
                sp.dma_start(w3[:, e:e + 2], A["w3"][:, e:e + 2]).then_inc(s_w, 16)
            sp.wait_ge(s_agg, 1)
            sp.dma_start(qw, A["q"]).then_inc(s_q, 16)
            sp.dma_start(lut4, A["lut4"]).then_inc(s_l4, 16)
            sp.wait_ge(s_route, 1)
            sp.wait_ge(s_sup, 2 * MC)

            def step(kk, par):
                k = 2 * kk + par
                if not isinstance(k, int) or k < ET:
                    if not isinstance(k, int) or k >= 2:
                        sp.wait_ge(s_hb, k - 1)
                    e = sp.value_load(expert_of_tile[0:1, bass.ds(k, 1)], min_val=0, max_val=E - 1)
                    sp.dma_start(b12rep[par], A["b12"][bass.ds(e, 1), :].partition_broadcast(P)).then_inc(s_b12[par], 16)
                if not isinstance(k, int) or k >= 2:
                    sp.wait_ge(s_ye, k - 1)
                    sp.dma_start(y_slots[bass.ds((k - 2) * P, P), :], y_sb[par]).then_inc(s_yw[par], 16)

            over_tiles(sp, step, ET + 1)

            sp.wait_ge(s_down, ET)
            sp.dma_start(ybias, A["ybias"].partition_broadcast(P)).then_inc(s_ybias, 16)

            def tables(u, par):
                t = 2 * u + par
                if not isinstance(t, int) or t >= 2:
                    sp.wait_ge(s_G, 2 * t - 2)
                sp.dma_start(lut8[par], A["lut8"][bass.ds(t, 1)].rearrange("a p g m -> p (a g) m")).then_inc(s_lut8[par], 16)

            tables(0, 0)
            tables(0, 1)
            with sp.Fori(1, QT // 2) as u:
                tables(u, 0)
                tables(u, 1)
            for t in range(TT):
                sp.wait_ge(s_yout, t + 1)
                sp.dma_start(A["out"][P * t:P * t + P, :], ysel[t % 2]).then_inc(s_out[t % 2], 16)
            for i in range(2):
                sp.wait_ge(s_out[i], 16 * TT // 2)

        @block.gpsimd
        def _(pool):
            nc.gpsimd.memset(ones[:], 1.0).then_inc(s_ones, 1)
            nc.gpsimd.memset(ones_bf[:], 1.0).then_inc(s_ones, 1)
            nc.gpsimd.memset(gate17[:], 1.0).then_inc(s_ones, 1)
            pool.wait_ge(s_const, 16)
            nc.gpsimd.tensor_copy(upper_bf[:], co["upper"]).then_inc(s_masks, 1)
            pool.wait_ge(s_route, 2)
            pool.wait_ge(s_sup, 2 * MC)

            for i in range(2):
                pool.wait_ge(s_xcw[i], 16 * TT // 2)
            for k in range(ET):
                if k >= 2:
                    pool.wait_ge(s_xTp, k - 1)
                nc.gpsimd.indirect_dma_start(xg[k % 2], None, xc_rows,
                                             bass.IndirectOffsetOnAxis(tok_of_slot[:, k:k + 1], 0)).then_inc(s_gather[k % 2], 16)
            pool.wait_ge(s_yw[0], 16 * ((ET + 1) // 2))
            pool.wait_ge(s_yw[1], 16 * (ET // 2))
            pool.wait_ge(s_down, ET)
            pool.wait_ge(s_zadd, TT)
            pool.wait_ge(s_ybias, 16)
            chain = 0

            def gather_back(n):
                t, c = n // TOPK, n % TOPK
                nc.gpsimd.indirect_dma_start(yg[n % 4], None, y_slots,
                                             bass.IndirectOffsetOnAxis(slot_i[:, c, t:t + 1], 0)).then_inc(s_back[n % 4], 16)

            for n in range(4):
                gather_back(n)
            for t in range(TT):
                for c in range(TOPK):
                    n = TOPK * t + c
                    pool.wait_ge(s_back[n % 4], 16 * (n // 4 + 1))
                    nc.gpsimd.tensor_scalar(yg[n % 4], yg[n % 4], gate[:, c, t:t + 1], None, ALU.mult).then_inc(s_pool, 1)
                    chain += 1
                    pool.wait_ge(s_pool, chain)
                    if n >= 1:
                        pool.wait_ge(s_comb, n)
                    nc.gpsimd.tensor_tensor(x_rows[:, t], x_rows[:, t], yg[n % 4], ALU.add).then_inc(s_comb, 1)
                    if n + 4 < TOPK * TT:
                        pool.wait_ge(s_comb, n + 1)
                        gather_back(n + 4)
                pool.wait_ge(s_comb, TOPK * (t + 1))
                nc.gpsimd.tensor_tensor(xb[:, t], x_rows[:, t], ybias, ALU.add).then_inc(s_xb, 1)

        @block.scalar
        def _(act):
            act.dma_start(const[:], A["const"]).then_inc(s_const, 16)
            act.wait_ge(s_small, 16)
            act.wait_ge(s_h1, 1)
            nc.scalar.activation(h1T[:], bank[6][:, 0:N], ACT.Gelu, bias=sm["b0"]).then_inc(s_h1T, 1)
            act.wait_ge(s_h2, 1)
            nc.scalar.activation(h2T[:], bank[6][:, 0:N], ACT.Gelu, bias=sm["b1"]).then_inc(s_h2T, 1)
            for h in range(2):
                act.wait_ge(s_ctxrep_mm, h + 1)
                nc.scalar.activation(ctxrep[:, 512 * h:512 * h + 512], bank[4 + 3 * h][:], ACT.Copy).then_inc(s_ctxrep, 1)

            def stage_rows(t):
                act.wait_ge(s_turn, t + 1)
                if t >= 2:
                    act.wait_ge(s_xcw[t % 2], 16 * (t // 2))
                nc.scalar.activation(xc_stage[:, t % 2], bank[2 + t % 2][:], ACT.Copy).then_inc(s_stage, 1)
                act.wait_ge(s_stage, t + 1)
                act.dma_start(xc_rows[P * t:P * t + P, :], xc_stage[:, t % 2]).then_inc(s_xcw[t % 2], 16)

            for t in range(4):
                stage_rows(t)
            act.wait_ge(s_attm, 1)
            nc.scalar.activation(att[:], attw[:, 0:KE], ACT.Exp, accum_out=attw[:, KE + 1:KE + 2]).then_inc(s_attex, 1)
            for t in range(4, TT):
                stage_rows(t)
            act.wait_ge(s_attTp, 1)
            nc.scalar.activation(attT[:], bank[6][0:KE, 0:N], ACT.Copy).then_inc(s_attT, 1)
            act.wait_ge(s_rm, 1)
            nc.scalar.activation(ra[:], rbuf[:], ACT.Exp).then_inc(s_rexp, 1)

            def shared_silu(n):
                act.wait_ge(s_sup, n + 1)
                if n >= 2:
                    act.wait_ge(s_hs, n - 1)
                nc.scalar.activation(silu_s[:, n % 2], bank[2 * (n % 2)][:], ACT.Silu,
                                     bias=sm["sb1"][:, n % MC:n % MC + 1]).then_inc(s_silu, 1)

            shared_silu(0)
            shared_silu(1)
            for h in range(2):
                act.wait_ge(s_agg, h + 2)
                nc.scalar.activation(aggbrep[:, 512 * h:512 * h + 512], bank[6 + h][:], ACT.Copy).then_inc(s_aggbrep, 1)
            shared_silu(2)
            for h in range(2):
                act.wait_ge(s_gTp, h + 1)
                nc.scalar.activation(gateT[:, 512 * h:512 * h + 512], bank[5 - h][0:E + 1, :], ACT.Copy).then_inc(s_gT, 1)
            shared_silu(3)

            def turned_rows(kk, par):
                k = 2 * kk + par
                act.wait_ge(s_xTp, k + 1)
                if not isinstance(k, int) or k >= 2:
                    act.wait_ge(s_up, k - 1)
                nc.scalar.activation(xgT[par].rearrange("p j t -> p (j t)"), bank[par][:], ACT.Copy).then_inc(s_xTe, 1)

            def step(kk, par):
                k = 2 * kk + par
                if not isinstance(k, int) or k + 1 < ET:
                    turned_rows(kk + par, 1 - par)
                if not isinstance(k, int) or k >= 2:
                    act.wait_ge(s_down, k - 1)
                    if not isinstance(k, int) or k >= 4:
                        act.wait_ge(s_yw[par], 16 * (kk - 1))
                    nc.scalar.activation(y_sb[par], bank[5 + par][:], ACT.Copy).then_inc(s_ye, 1)
                if not isinstance(k, int) or k < ET:
                    act.wait_ge(s_hb, k + 1)
                    if not isinstance(k, int) or k >= 2:
                        act.wait_ge(s_hg, k - 1)
                    nc.scalar.activation(sil[par], h12[par][:, 0:INTER], ACT.Silu).then_inc(s_hsilu, 1)

            turned_rows(0, 0)
            over_tiles(act, step, ET + 1)

            def step(u, i):
                g = 4 * u + i
                static = isinstance(g, int)
                act.wait_ge(s_m, g + 1)
                if not static or g >= 2:
                    act.wait_ge(s_G, g - 1)
                nc.scalar.activation(hot_hi[i % 2], bank[i % 2][:], ACT.Relu, bias=co["mbias"]).then_inc(s_hi, 1)
                if not static or g >= 4:
                    act.wait_ge(s_s3, g - 3)
                nc.scalar.activation(hot_lo[i], bank[2 + i % 2][:], ACT.Relu, bias=co["mbias"]).then_inc(s_lo, 1)

            act.wait_ge(s_down, ET)
            over_groups(act, step)

            act.wait_ge(s_aT, 1)
            nc.scalar.activation(sq[0].rearrange("p j t -> p (j t)"), aT[0].rearrange("p j t -> p (j t)"),
                                 ACT.Square).then_inc(s_sq, 1)
            for t in range(TT):
                if t + 1 < TT:
                    act.wait_ge(s_aT, t + 2)
                    if t >= 1:
                        act.wait_ge(s_norm, t)
                    nc.scalar.activation(sq[(t + 1) % 2].rearrange("p j t -> p (j t)"),
                                         aT[(t + 1) % 2].rearrange("p j t -> p (j t)"), ACT.Square).then_inc(s_sq, 1)
                act.wait_ge(s_ymm, 2 * t + 1)
                if t >= 2:
                    act.wait_ge(s_out[t % 2], 16 * (t // 2))
                nc.scalar.activation(ysel[t % 2], bank[5 + t % 2][:], ACT.Copy).then_inc(s_ylc, 1)

        @block.vector
        def _(dve):
            chain = [0]

            def link(ins):
                chain[0] += 1
                ins.then_inc(s_v, 1)
                dve.wait_ge(s_v, chain[0])

            v = nc.vector
            dve.wait_ge(s_small, 16)
            dve.wait_ge(s_const, 16)
            dve.wait_ge(s_ctx, 1)
            link(v.tensor_tensor(ctxb[:], bank[5][0:N, 0:C], sm["convb"][0:N], ALU.add))
            v.tensor_tensor(diag[0:N], bc(ctxb[:], 1, N), bc(ident[0:N, 0:N], 2, C), ALU.mult).then_inc(s_diag, 1)

            def conv_out(t):
                dve.wait_ge(s_conv, t + 1)
                if t == 0:
                    dve.wait_ge(s_ctxrep, 2)
                cr = ctxrep[:, P * t:P * t + P].rearrange("p (n c) -> p n c", n=NT)
                v.tensor_tensor(
                    xcT[:, :, P * t:P * t + P].rearrange("p j (n c) -> p n j c", n=NT),
                    bank[t % 2][:].rearrange("p (n j c) -> p n j c", n=NT, j=S),
                    bc(cr, 2, S), ALU.add).then_inc(s_xcT, 1)

            for t in range(4):
                conv_out(t)
            dve.wait_ge(s_attl, 1)
            link(v.tensor_tensor(attw[:, 0:KE], bank[5][0:N, 0:KE], sm["b2"][0:N], ALU.add))
            link(v.tensor_reduce(attw[:, KE:KE + 1], attw[:, 0:KE], X, ALU.max))
            v.tensor_scalar(attw[:, 0:KE], attw[:, 0:KE], attw[:, KE:KE + 1], None, ALU.subtract).then_inc(s_attm, 1)
            for t in range(4, TT):
                conv_out(t)
            dve.wait_ge(s_attex, 1)
            link(v.reciprocal(attw[:, KE + 2:KE + 3], attw[:, KE + 1:KE + 2]))
            v.tensor_scalar(att[:], att[:], attw[:, KE + 2:KE + 3], None, ALU.mult).then_inc(s_att, 1)

            dve.wait_ge(s_logit, 1)
            link(v.tensor_tensor(score[:], bank[4][:, 0:TT * E].rearrange("p (t e) -> p t e", t=TT),
                                 bc(sm["rb"], 1, TT), ALU.add))
            link(v.tensor_reduce(r1[:], score[:], X, ALU.max))
            v.tensor_tensor(rbuf[:], score[:], bc(r1[:], 2, E), ALU.subtract).then_inc(s_rm, 1)

            dve.wait_ge(s_attrep, 2)
            for k in range(KT):
                v.tensor_tensor(al[k], bc(bank[5][:, N * k:N * k + N], 2, C), bc(co["dmask"], 1, N),
                                ALU.mult).then_inc(s_al, 1)
            link(v.tensor_copy(aggb[:], bank[6][0:N, 0:C]))
            v.tensor_tensor(diag[0:N], bc(aggb[:], 1, N), bc(ident[0:N, 0:N], 2, C), ALU.mult).then_inc(s_al, 1)

            dve.wait_ge(s_rexp, 1)
            link(v.tensor_reduce(r1[:], ra[:], X, ALU.add))
            link(v.reciprocal(r2[:], r1[:]))
            link(v.tensor_tensor(rbuf[:], ra[:], bc(r2[:], 2, E), ALU.mult))
            link(v.tensor_tensor(score[:], rbuf[:], bc(sm["rbias"], 1, TT), ALU.add))

            def first_max(out, m, n, a, b):
                link(v.tensor_reduce(r1[:], m, X, ALU.max))
                link(v.tensor_tensor(a, m, bc(r1[:], 2, n), ALU.is_equal))
                link(v.tensor_tensor(b, a, bc(co["rev"][:, 0:n], 1, TT), ALU.mult))
                link(v.tensor_reduce(r2[:], b, X, ALU.max))
                link(v.tensor_tensor(out, b, bc(r2[:], 2, n), ALU.is_equal))

            g4 = score[:].rearrange("p t (g k) -> p t g k", g=EG)
            link(v.tensor_reduce(gm[:], g4, X, ALU.max))
            first_max(gpick[0][:], gm[:], EG, ra[:, :, 0:EG], rc[:, :, 0:EG])
            link(v.scalar_tensor_tensor(gm[:], gpick[0][:], -BIG, gm[:], ALU.mult, ALU.add))
            first_max(gpick[1][:], gm[:], EG, ra[:, :, 0:EG], rc[:, :, 0:EG])
            link(v.tensor_tensor(gt1[:], gpick[0][:], gpick[1][:], ALU.add))
            link(v.tensor_scalar(gt1[:], gt1[:], BIG, -BIG, ALU.mult, ALU.add))
            link(v.tensor_tensor(masked[:].rearrange("p t (g k) -> p t g k", g=EG), g4, bc(gt1[:], 3, E // EG), ALU.add))
            first_max(pick[0][:], masked[:], E, ra[:], rc[:])
            link(v.scalar_tensor_tensor(masked[:], pick[0][:], -BIG, masked[:], ALU.mult, ALU.add))
            first_max(pick[1][:], masked[:], E, ra[:], rc[:])
            link(v.tensor_tensor(rbuf[:], pick[0][:], pick[1][:], ALU.add))
            v.tensor_copy(sel_bf[:], rbuf[:]).then_inc(s_sel, 1)
            dve.wait_ge(s_ones, 3)
            v.tensor_tensor(gate17[:, :, 0:E], rbuf[:], score[:], ALU.mult).then_inc(s_gate, 1)
            for c in range(TOPK):
                link(v.tensor_tensor(ra[:], pick[c][:], score[:], ALU.mult))
                link(v.tensor_reduce(gate[:, c], ra[:], X, ALU.add))

            dve.wait_ge(s_agg, 1)
            for t in range(TT):
                last = v.tensor_tensor(bd[:, t].rearrange("p (n c) -> p n c", n=NT),
                                       bc(bank[5][:, C * t:C * t + C], 1, NT), bc(co["blk"], 2, C), ALU.mult)
            last.then_inc(s_bd, 1)

            def shared_hidden(n):
                half, m = n // MC, n % MC
                dve.wait_ge(s_silu, n + 1)
                v.scalar_tensor_tensor(hs[:, m, 512 * half:512 * half + 512], bank[2 * (n % 2) + 1][:],
                                       sm["sb2"][:, m:m + 1], silu_s[:, n % 2], ALU.add, ALU.mult).then_inc(s_hs, 1)

            shared_hidden(0)
            shared_hidden(1)

            dve.wait_ge(s_rank, 2)
            link(v.tensor_tensor(cntj[:], bc(bank[6][:, 0:E], 2, TT), bc(co["thr"], 1, E), ALU.is_gt))
            link(v.tensor_reduce(ntile[:], cntj[:], X, ALU.add))
            link(v.tensor_tensor(tri_w[:], bc(ntile[:], 1, E), co["tri"].rearrange("p (a b) -> p a b", a=E), ALU.mult))
            link(v.tensor_reduce(tstart[:], tri_w[:], X, ALU.add))
            link(v.tensor_tensor(tend[:], tstart[:], ntile[:], ALU.add))
            link(v.tensor_scalar(tstart[:], tstart[:], float(P), None, ALU.mult))
            link(v.tensor_tensor(ra[:], bank[7][:, 0:TT * E].rearrange("p (t e) -> p t e", t=TT),
                                 bc(tstart[:], 1, TT), ALU.add))
            for c in range(TOPK):
                link(v.tensor_tensor(rc[:], pick[c][:], ra[:], ALU.mult))
                link(v.tensor_reduce(slot_f[:, c], rc[:], X, ALU.add))
            link(v.tensor_copy(slot_i[:], slot_f[:]))
            link(v.tensor_scalar(sq_i[:], slot_i[:], 7, None, ALU.logical_shift_right))
            link(v.tensor_scalar(sr_i[:], slot_i[:], P - 1, None, ALU.bitwise_and))
            link(v.tensor_copy(sq_f[:], sq_i[:]))
            link(v.tensor_copy(sr_f[:], sr_i[:]))
            for c in range(TOPK):
                link(v.tensor_tensor(onehot_r[:, c], bc(co["iota"], 1, TT), bc(sr_f[:, c], 2, P), ALU.is_equal))
                link(v.tensor_tensor(onehot_q[:, c], bc(co["iota"][:, 0:32], 1, TT), bc(sq_f[:, c], 2, 32), ALU.is_equal))
                v.tensor_scalar(tok_p[:, c], onehot_q[:, c], co["pidx"], None, ALU.mult).then_inc(s_hots, 1)
                v.tensor_tensor(tok_t[:, c], onehot_q[:, c], bc(co["tbase"], 2, 32), ALU.mult).then_inc(s_hots, 1)
            link(v.tensor_tensor(eidw[:], bc(tend[:], 1, 32), bc(co["iota"][:, 0:32], 2, E), ALU.is_le))
            link(v.tensor_reduce(eid_f[:], eidw[:], X, ALU.add))
            v.tensor_scalar(expert_of_tile[:], eid_f[:], float(E - 1), None, ALU.min).then_inc(s_route, 1)
            shared_hidden(2)
            shared_hidden(3)
            dve.wait_ge(s_toks, 1)
            v.tensor_copy(tok_of_slot[:], bank[4][:, 0:32]).then_inc(s_route, 1)
            dve.wait_ge(s_xrows, 16)
            for t in range(TT):
                dve.wait_ge(s_z, t + 1)
                v.tensor_tensor(x_rows[:, t], x_rows[:, t], bank[t % 4][:], ALU.add).then_inc(s_zadd, 1)

            def step(kk, par):
                k = 2 * kk + par
                if not isinstance(k, int) or k >= 1:
                    dve.wait_ge(s_hTp, k)
                    if not isinstance(k, int) or k >= 3:
                        dve.wait_ge(s_down, k - 2)
                    v.tensor_copy(hidT[1 - par], bank[4][:, 0:P]).then_inc(s_hTe, 1)
                if not isinstance(k, int) or k < ET:
                    dve.wait_ge(s_up, k + 1)
                    dve.wait_ge(s_b12[par], 16 * (kk + 1))
                    if not isinstance(k, int) or k >= 2:
                        dve.wait_ge(s_hg, k - 1)
                    v.tensor_tensor(h12[par], bank[2 + par][:, 0:2 * INTER], b12rep[par], ALU.add).then_inc(s_hb, 1)
                    dve.wait_ge(s_hsilu, k + 1)
                    v.tensor_tensor(hid[par], sil[par], h12[par][:, INTER:2 * INTER], ALU.mult).then_inc(s_hg, 1)

            over_tiles(dve, step, ET)

            def make_bits(c):
                if c >= 2:
                    dve.wait_ge(s_m, 2 * CHUNK * (c - 1))
                halves = qw[:, CHUNK * c:CHUNK * c + CHUNK].rearrange("p t w -> p (t w)").bitcast(U16)
                halves = halves.rearrange("p (t h) -> p t h", h=2)
                out = bits.bitcast(U16).rearrange("p t (w s) -> p (t w) s", s=32)
                at = (c % 2) * CHUNK * L // 32
                for b in range(32):
                    move = (14 - b % 16, ALU.logical_shift_left) if b % 16 < 15 else (1, ALU.logical_shift_right)
                    last = v.tensor_scalar(out[:, at:at + CHUNK * L // 32, b], halves[:, :, b // 16], move[0], 0x4000,
                                           move[1], ALU.bitwise_and)
                last.then_inc(s_bits, 1)

            dve.wait_ge(s_q, 16)
            dve.wait_ge(s_l4, 16)
            dve.wait_ge(s_up, ET)
            v.tensor_copy(match[:, 0].rearrange("p a m -> p (a m)"), co["mhi"]).then_inc(s_match, 1)
            v.tensor_copy(match[:, 1].rearrange("p a m -> p (a m)"), co["mlo"]).then_inc(s_match, 1)
            make_bits(0)
            link(v.tensor_copy(lut4_parts[:, :, 0], lut4))
            link(v.tensor_tensor(l4rest[0], lut4, lut4_parts[:, :, 0], ALU.subtract))
            link(v.tensor_copy(lut4_parts[:, :, 1], l4rest[0]))
            link(v.tensor_tensor(l4rest[1], l4rest[0], lut4_parts[:, :, 1], ALU.subtract))
            v.tensor_copy(lut4_parts[:, :, 2], l4rest[1]).then_inc(s_l4p, 1)
            make_bits(1)

            def step(u, i):
                g = 4 * u + i
                static = isinstance(g, int)
                dve.wait_ge(s_G, g + 1)
                dve.wait_ge(s_lo, g + 1)
                if not static or g >= 2:
                    dve.wait_ge(s_s3, g - 1)
                v.tensor_tensor(prod[i % 2], hot_lo[i], bank[4 + i % 2][:], ALU.mult).then_inc(s_prod, 1)
                if i % 2 == 0 and (not static or g >= 2):
                    copy_weights(2 * u + i // 2 - 1, (i // 2 + 1) % 2)

            def copy_weights(t, par):
                dve.wait_ge(s_s3, 2 * t + 2)
                from_ps = bank[6 + par][:, 0:256].rearrange("p (a c) -> p a c", c=32)
                v.tensor_copy(wTh[:, :, bass.ds(OI * t, OI)].rearrange("p i (g c) -> p i g c", g=2),
                              from_ps[:, :, 0:G8].rearrange("p (i g) c -> p i g c", g=2))
                v.tensor_reduce(wTl[:, :, bass.ds(OI * t, OI)].rearrange("p i (g c) -> p i g c", g=2),
                                from_ps[:, :, G8:32].rearrange("p (i g) (k c) -> p i g c k", g=2, k=PARTS),
                                X, ALU.add).then_inc(s_wev, 1)

            for i in range(4):
                step(0, i)
            for c in range(4):
                lo, hi = max(1, 4 * c), min(4 * c + 4, NG // 4 - 1)
                with dve.Fori(lo, hi) as u:
                    for i in range(4):
                        step(u, i)
                if c < 2:
                    make_bits(c + 2)
            for i in range(4):
                step(NG // 4 - 1, i)
            copy_weights(QT - 1, 1)

            def linear_in(t):
                dve.wait_ge(s_amm, t + 1)
                if t >= 2:
                    dve.wait_ge(s_ymm, 2 * t - 2)
                v.tensor_tensor(aT[t % 2], bank[t % 2][:].rearrange("p (j k) -> p j k", j=LT),
                                bc(aggbrep[:, P * t:P * t + P], 1, LT), ALU.add).then_inc(s_aT, 1)

            linear_in(0)
            for t in range(TT):
                dve.wait_ge(s_norm, t + 1)
                v.tensor_scalar(high[t % 2], bank[2][:, 0:1], EST_SQ, None, ALU.is_gt).then_inc(s_high, 1)
                if t + 1 < TT:
                    linear_in(t + 1)
                dve.wait_ge(s_ylc, t + 1)
                dve.wait_ge(s_ymm, 2 * t + 2)
                dve.wait_ge(s_high, t + 1)
                v.copy_predicated(ysel[t % 2], high[t % 2].to_broadcast([P, L]), bank[3 + t % 2][:]).then_inc(s_ysel, 1)
                dve.wait_ge(s_ysel, t + 1)
                dve.wait_ge(s_xb, t + 1)
                v.tensor_tensor(ysel[t % 2], ysel[t % 2], xb[:, t], ALU.add).then_inc(s_yout, 1)

        @block.tensor
        def _(pe):
            mm = nc.tensor.matmul
            pe.wait_ge(s_small, 16)
            mm(bank[5][0:N, 0:C], sm["cT"], sm["cwT"], start=True, stop=True).then_inc(s_ctx, 1)
            mm(bank[6][:, 0:N], sm["W0"], sm["cT"], start=True, stop=True).then_inc(s_h1, 1)
            pe.wait_ge(s_h1T, 1)
            mm(bank[6][:, 0:N], sm["W1"], h1T[:], start=True, stop=True).then_inc(s_h2, 1)
            pe.wait_ge(s_ones, 3)
            pe.wait_ge(s_diag, 1)
            for h in range(2):
                mm(bank[4 + 3 * h][:], ones[0:N, :], diag[0:N, 16 * h:16 * h + 16, :].rearrange("p n c -> p (n c)"),
                   start=True, stop=True).then_inc(s_ctxrep_mm, 1)
            pe.wait_ge(s_wconv, 16)

            def conv(t):
                pe.wait_ge(s_x4[t // 2], 16)
                if t >= 2:
                    pe.wait_ge(s_xcT, t - 1)
                for k in range(NT):
                    for d in range(3):
                        last = mm(bank[t % 2][:, P * k:P * k + P], x4[:, NT * t + k, d:d + NB], wconv[:, d],
                                  start=(d == 0), stop=(d == 2))
                last.then_inc(s_conv, 1)

            def turn(t):
                pe.wait_ge(s_xcT, t + 1)
                if t == 0:
                    pe.wait_ge(s_const, 16)
                    pe.wait_ge(s_ctxrep, 1)
                if t >= 2:
                    pe.wait_ge(s_stage, t - 1)
                for j in range(S):
                    last = nc.tensor.transpose(bank[2 + t % 2][:, P * j:P * j + P], xcT[:, j, P * t:P * t + P], ident)
                last.then_inc(s_turn, 1)
                for j in range(S):
                    last = mm(bank[4][:, E * t:E * t + E], xcT[:, j, P * t:P * t + P], sm["rw"][:, E * j:E * j + E],
                              start=(j == 0), stop=(j == S - 1))
                if t == TT - 1:
                    last.then_inc(s_logit, 1)

            for t in range(TT):
                conv(t)
                if t >= 1:
                    turn(t - 1)
                if t == 3:
                    pe.wait_ge(s_h2T, 1)
                    mm(bank[5][0:N, 0:KE], h2T[:], sm["W2"], start=True, stop=True).then_inc(s_attl, 1)
            turn(TT - 1)

            def shared_up(n):
                half, m = n // MC, n % MC
                if n == 0:
                    pe.wait_ge(s_shared, 32)
                if n == 1:
                    pe.wait_ge(s_stage, TT)
                if n >= 2:
                    pe.wait_ge(s_hs, n - 1)
                for w in range(2):
                    for j in range(S):
                        last = mm(bank[2 * (n % 2) + w][:], sw12[:, j, 256 * w + P * m:256 * w + P * m + P],
                                  xcT[:, j, 512 * half:512 * half + 512], start=(j == 0), stop=(j == S - 1))
                last.then_inc(s_sup, 1)

            def shared_down(t):
                pe.wait_ge(s_hs, 2 if t < 4 else 4)
                if t < 4:
                    pe.wait_ge(s_gT, 2)
                else:
                    pe.wait_ge(s_zadd, t - 3)
                for m in range(MC):
                    mm(bank[t % 4][:], hs[:, m, P * t:P * t + P], sw3[:, m], start=(m == 0), stop=False)
                mm(bank[t % 4][:], gateT[:, P * t:P * t + P], b3x[:], start=False, stop=True).then_inc(s_z, 1)

            shared_up(0)
            pe.wait_ge(s_att, 1)
            nc.tensor.transpose(bank[6][0:KE, 0:N], att[:], ident[0:N, 0:N]).then_inc(s_attTp, 1)
            pe.wait_ge(s_attT, 1)
            for k in range(KT):
                mm(bank[5][:, N * k:N * k + N], co["ksel"][0:KE, P * k:P * k + P], attT[:], start=True, stop=True)
            last = mm(bank[6][0:N, 0:C], attT[:], sm["bk"][0:KE], start=True, stop=True)
            last.then_inc(s_attrep, 2)
            shared_up(1)
            pe.wait_ge(s_al, 3)
            for t in range(TT):
                for k in range(KT):
                    last = mm(bank[5][:, C * t:C * t + C], al[k][:, NT * t:NT * t + NT, :].rearrange("p n i -> p (n i)"),
                              sm["wk"][:, C * k:C * k + C], start=(k == 0), stop=(k == KT - 1))
            last.then_inc(s_agg, 1)
            for h in range(2):
                mm(bank[6 + h][:], ones[0:N, :], diag[0:N, 16 * h:16 * h + 16, :].rearrange("p n c -> p (n c)"),
                   start=True, stop=True).then_inc(s_agg, 1)
            pe.wait_ge(s_sel, 1)
            pe.wait_ge(s_masks, 1)
            pe.wait_ge(s_aggbrep, 2)
            sel = sel_bf[:].rearrange("p t e -> p (t e)")
            mm(bank[7][:, 0:TT * E], upper_bf[:], sel, start=True, stop=False)
            for t in range(1, TT):
                last = mm(bank[7][:, t * E:TT * E], ones_bf[:], sel[:, 0:(TT - t) * E], start=False, stop=(t == TT - 1))
            last.then_inc(s_rank, 1)
            for t in range(TT):
                last = mm(bank[6][:, 0:E], ones_bf[:], sel[:, t * E:t * E + E], start=(t == 0), stop=(t == TT - 1))
            last.then_inc(s_rank, 1)
            shared_up(2)
            pe.wait_ge(s_gate, 1)
            pe.wait_ge(s_bd, 1)
            for h in range(2):
                for t in range(4 * h, 4 * h + 4):
                    last = nc.tensor.transpose(bank[5 - h][0:E + 1, P * (t % 4):P * (t % 4) + P], gate17[:, t], ident)
                last.then_inc(s_gTp, 1)
            shared_up(3)
            pe.wait_ge(s_b3, 16)
            pe.wait_ge(s_hs, 4)
            for t in range(4):
                shared_down(t)
            pe.wait_ge(s_hots, 4)
            n = 0
            for c in range(TOPK):
                for t in range(TT):
                    for part in (tok_p, tok_t):
                        last = mm(bank[4][:, 0:32], onehot_r[:, c, t], part[:, c, t],
                                  start=(n == 0), stop=(n == 2 * TOPK * TT - 1))
                        n += 1
            last.then_inc(s_toks, 1)
            for t in range(4, TT):
                shared_down(t)

            pe.wait_ge(s_w, 16 * E)
            pe.wait_ge(s_zadd, TT)
            pe.wait_ge(s_route, 2)

            def turn_rows(kk, par):
                k = 2 * kk + par
                pe.wait_ge(s_gather[par], 16 * (kk + 1))
                if not isinstance(k, int) or k >= 2:
                    pe.wait_ge(s_xTe, k - 1)
                for j in range(S):
                    last = nc.tensor.transpose(bank[par][:, P * j:P * j + P], xg[par][:, P * j:P * j + P], ident)
                last.then_inc(s_xTp, 1)

            def expert_of(k):
                return pe.value_load(expert_of_tile[0:1, bass.ds(k, 1)], min_val=0, max_val=E - 1)

            def step(kk, par):
                k = 2 * kk + par
                if not isinstance(k, int) or k >= 2:
                    e_down = expert_of(k - 2)
                if not isinstance(k, int) or k < ET:
                    e_up = expert_of(k)
                if not isinstance(k, int) or k + 1 < ET:
                    turn_rows(kk + par, 1 - par)
                if not isinstance(k, int) or k >= 2:
                    pe.wait_ge(s_hTe, k - 1)
                    if not isinstance(k, int) or k >= 4:
                        pe.wait_ge(s_ye, k - 3)
                    mm(bank[5 + par][:], hidT[par], w3[:, bass.ds(e_down, 1), :].rearrange("p a l -> p (a l)"),
                       start=True, stop=True).then_inc(s_down, 1)
                if not isinstance(k, int) or 1 <= k <= ET:
                    pe.wait_ge(s_hg, k)
                    nc.tensor.transpose(bank[4][:, 0:P], hid[1 - par], ident).then_inc(s_hTp, 1)
                if not isinstance(k, int) or k < ET:
                    pe.wait_ge(s_xTe, k + 1)
                    if not isinstance(k, int) or k >= 2:
                        pe.wait_ge(s_hb, k - 1)
                    for j in range(S):
                        last = mm(bank[2 + par][:, 0:2 * INTER], xgT[par][:, j],
                                  w12[:, bass.ds(e_up, 1), j, :].rearrange("p a m -> p (a m)"),
                                  start=(j == 0), stop=(j == S - 1))
                    last.then_inc(s_up, 1)

            turn_rows(0, 0)
            over_tiles(pe, step, ET + 1)

            pe.wait_ge(s_ye, ET)
            pe.wait_ge(s_match, 2)

            def match_nibbles(g, t, par, buf):
                static = isinstance(g, int)
                if par == 0:
                    pe.wait_ge(s_bits, t // CHUNK + 1)
                if not static or g >= 2:
                    pe.wait_ge(s_lo, g - 1)
                    pe.wait_ge(s_hi, g - 1)
                for half in range(2):
                    last = mm(bank[2 * half + buf][:], match[:, half, par], bits[:, bass.ds(t % RING, 1), :].rearrange("p a i -> p (a i)"),
                              start=True, stop=True)
                last.then_inc(s_m, 1)

            def turn_weights(g, t, par, i):
                static = isinstance(g, int)
                pe.wait_ge(s_prod, g + 1)
                if par == 0 and (not static or t >= 2):
                    pe.wait_ge(s_wev, t - 1)
                out = bank[6 + i // 2]
                for j in range(LT):
                    at = 32 * (2 * j + par)
                    mm(out[:, at:at + G8], prod[i % 2][:, P * j:P * j + P], co["ones8"], start=True, stop=True)
                    last = mm(out[:, at + G8:at + 32], hot_lo[i][:, P * j:P * j + P],
                              lut4_parts[:, bass.ds(g, 1)].rearrange("p a k c -> p (a k c)"), start=True, stop=True)
                last.then_inc(s_s3, 1)

            def step(u, i):
                g = 4 * u + i
                static = isinstance(g, int)
                if not static or g + 1 < NG:
                    n = i + 1
                    match_nibbles(4 * u + n, 2 * u + n // 2, n % 2, n % 2)
                pe.wait_ge(s_hi, g + 1)
                pe.wait_ge(s_lut8[i // 2], 16 * (u + 1))
                if not static or g >= 2:
                    pe.wait_ge(s_prod, g - 1)
                mm(bank[4 + i % 2][:], lut8[i // 2][:, i % 2], hot_hi[i % 2], start=True, stop=True).then_inc(s_G, 1)
                if not static or g >= 1:
                    w = 4 * u + i - 1
                    turn_weights(w, (2 * u - 1) if i == 0 else 2 * u + (i - 1) // 2, (i - 1) % 2, (i - 1) % 4)

            match_nibbles(0, 0, 0, 0)
            pe.wait_ge(s_l4p, 1)
            over_groups(pe, step)
            turn_weights(NG - 1, QT - 1, 1, 3)

            def linear_in(t):
                pe.wait_ge(s_comb, TOPK * (t + 1))
                if t >= 2:
                    pe.wait_ge(s_aT, t - 1)
                for j in range(LT):
                    last = mm(bank[t % 2][:, P * j:P * j + P], x_rows[:, t, P * j:P * j + P], bd[:, t], start=True, stop=True)
                last.then_inc(s_amm, 1)

            pe.wait_ge(s_wev, QT)
            linear_in(0)
            for t in range(TT):
                if t + 1 < TT:
                    linear_in(t + 1)
                pe.wait_ge(s_aT, t + 1)
                if t >= 2:
                    pe.wait_ge(s_ylc, t - 1)
                    pe.wait_ge(s_ysel, t - 1)
                for b, w in ((5, wTl), (3, wTh)):
                    for j in range(LT):
                        last = mm(bank[b + t % 2][:], aT[t % 2][:, j], w[:, j], start=(j == 0), stop=(j == LT - 1))
                    last.then_inc(s_ymm, 1)
                    if b == 5:
                        pe.wait_ge(s_sq, t + 1)
                        if t >= 1:
                            pe.wait_ge(s_high, t)
                        for j in range(LT):
                            last = mm(bank[2][:, 0:1], sq[t % 2][:, j], ones[:, 0:1], start=(j == 0), stop=(j == LT - 1))
                        last.then_inc(s_norm, 1)


def conv_weights(w):
    out = np.zeros((S, C, 3, S, C), w.dtype)
    pad, per = TAPS // 2, C // GROUPS
    for o in range(C):
        g = o // per
        for j in range(S):
            for k in range(TAPS):
                rel = j + k - pad
                out[rel % S, g * per:(g + 1) * per, rel // S + 1, j, o] = w[o, :, k]
    return out.reshape(P, 3, P)


def packed(table, parts, dtype=np.float32):
    at, width = spans(table)
    out = np.zeros((P, width), dtype)
    for name, a in parts.items():
        a = a.reshape(a.shape[0], -1)
        out[:a.shape[0], at[name].start:at[name].start + a.shape[1]] = a
    return out


def constants():
    p = np.arange(P)
    bits = lambda x, k: x >> k & 1
    match = np.zeros((2, P, 2, P), np.float32)
    for half in range(2):
        for plane in range(4):
            for par in range(2):
                for o in range(G8):
                    row = (4 * half + plane) * OI + par * G8 + o
                    match[half, row, par, 16 * o:16 * o + 16] = np.where(bits(np.arange(16), plane), 0.5, -0.5)
    ksel = np.zeros((KE, KT, KE // KT, C), np.float32)
    for k in range(KE):
        ksel[k, k // (KE // KT), k % (KE // KT)] = 1
    ones = np.array([bin(x).count("1") for x in range(16)])
    return packed(CONST, {
        "ident": np.eye(P), "iota": np.tile(p, (P, 1)), "rev": np.tile(E - np.arange(E), (P, 1)),
        "thr": np.tile(P * np.arange(TT), (P, 1)), "tri": np.tile(np.tri(E, k=-1).reshape(-1), (P, 1)),
        "blk": p[:, None] // C == np.arange(NT), "dmask": p[:, None] % C == np.arange(C), "pidx": p[:, None],
        "tbase": np.tile(P * np.arange(TT), (P, 1)), "ksel": ksel, "upper": p[:, None] < p,
        "mlo": match[0], "mhi": match[1], "mbias": 1 - ones[p % 16][:, None], "ones8": p[:, None] // 16 == np.arange(G8)})


def layout(i):
    a = {k: np.ascontiguousarray(v) for k, v in i.items()}
    rep = lambda v, n=P: np.broadcast_to(v, (n,) + v.shape)
    x4 = np.zeros((S, C, N, NB + 2), a["x"].dtype)
    x4[..., 1:NB + 1] = a["x"].reshape(N, C, NB, S).transpose(3, 1, 0, 2)
    blocks = lambda w: w.reshape(w.shape[:-2] + (NB, S, w.shape[-1]))
    ew12 = np.concatenate([blocks(a["L0_ffn_ew1"]), blocks(a["L0_ffn_ew2"])], -1)
    sw12 = np.concatenate([blocks(a["L0_ffn_sw1"]), blocks(a["L0_ffn_sw2"])], -1)
    q = a["L1_ffn_qweight"]
    lut8 = np.zeros((NG, G8, 16, G8, 16), a["L1_ffn_lut8"].dtype)
    lut4 = np.zeros((G8, 16, NG, G8), a["L1_ffn_lut4"].dtype)
    l8 = a["L1_ffn_lut8"].reshape(NG, G8, 16, 16)
    l4 = a["L1_ffn_lut4"].reshape(NG, G8, 16)
    for o in range(G8):
        lut8[:, o, :, o, :] = l8[:, o]
        lut4[o, :, :, o] = l4[:, o].T
    small = packed(SMALL, {
        "cT": a["cond_128"].T, "cwT": a["L0_cond_c_weight"].T, "W0": a["L1_cond_W0"], "W1": a["L1_cond_W1"],
        "W2": a["L1_cond_W2"], "b0": a["L1_cond_b0"][:, None], "b1": a["L1_cond_b1"][:, None],
        "sb1": a["L0_ffn_sb1"].reshape(MC, P).T, "sb2": a["L0_ffn_sb2"].reshape(MC, P).T,
        "wk": a["L1_cond_weight"][..., 0].reshape(KT, KE // KT, C, C).transpose(1, 3, 0, 2).reshape(P, KT, C),
        "rw": blocks(a["L0_ffn_router_w"]), "convb": rep(a["fside_S_0"], N), "b2": rep(a["L1_cond_b2"], N),
        "bk": a["L1_cond_bias_k"], "rb": rep(a["L0_ffn_router_b"]), "rbias": rep(a["L0_ffn_router_bias"])})
    return {
        "small": small, "const": constants(), "x4": x4.reshape(P, N, NB + 2), "wconv": conv_weights(a["L0_cond_weight"]),
        "x_rows": a["x"].reshape(TT, P, L).transpose(1, 0, 2), "w12": ew12.transpose(1, 0, 2, 3),
        "w3": a["L0_ffn_ew3"].transpose(1, 0, 2), "sw12": sw12, "sw3": a["L0_ffn_sw3"].reshape(MC, P, L).transpose(1, 0, 2),
        "b3x": np.concatenate([a["L0_ffn_eb3"], a["L0_ffn_sb3"][None]]),
        "b12": np.concatenate([a["L0_ffn_eb1"], a["L0_ffn_eb2"]], -1),
        "q": q.reshape(8, QT, OI, L // 32).transpose(0, 2, 1, 3).reshape(P, QT, L // 32),
        "lut8": lut8.reshape(QT, 2, P, P).transpose(0, 2, 1, 3), "lut4": lut4.reshape(P, NG, G8), "ybias": a["L1_ffn_bias"],
    }


def kernel(**inputs):
    import concourse.bacc as bacc
    from concourse.bass_utils import run_bass_kernel_spmd

    nc = bacc.Bacc("TRN2", target_bir_lowering=False, num_devices=1)
    arrays, A = {}, {}
    for name, a in layout(inputs).items():
        a = np.ascontiguousarray(a)
        arrays[f"in_{name}"] = a
        A[name] = nc.dram_tensor(f"in_{name}", a.shape, mybir.dt.from_np(a.dtype), kind="ExternalInput").ap()
    A["out"] = nc.dram_tensor("out", (T, L), F32, kind="ExternalOutput").ap()
    build(nc, A)
    r = run_bass_kernel_spmd(nc, [arrays], core_ids=[0])
    return r.results[0]["out"].reshape(N, C, L)
```

```python
from contextlib import ExitStack

import numpy as np

import concourse.bass as bass
from concourse import mybir

F32 = mybir.dt.float32
BF16 = mybir.dt.bfloat16
F32R = mybir.dt.float32r
I32 = mybir.dt.int32
U16 = mybir.dt.uint16
ALU = mybir.AluOpType
ACT = mybir.ActivationFunctionType
X = mybir.AxisListType.X

P = 128
N, C, L = 32, 32, 512
T = N * C
TT = T // P
NT = P // C
TAPS, GROUPS = 9, 4
S = 4
NB = L // S
D = 128
E, INTER, TOPK = 16, 128, 2
EG = 4
MC = 2
KE = 8
KT = KE * C // P
ET = TOPK * T // P + E - 1
O = 512
OI = P // 8
QT = O // OI
G8 = 8
NG = O // G8
RING = 16
CHUNK = RING // 2
PARTS = 3
HALVES = 2
BLOCK = P // G8
NBLOCK = NG // BLOCK
LT = L // P
BIG = 3.0e38
EST_SQ = 64.0 ** 2 + 2.0 ** -11

SMALL = [("cT", N), ("cwT", C), ("W0", D), ("W1", D), ("W2", KE), ("b0", 1), ("b1", 1), ("sb1", MC), ("sb2", MC),
         ("wk", KT * C), ("rw", S * E), ("convb", C), ("b2", KE), ("bk", C), ("rb", E), ("rbias", E)]
CONST = [("ident", P), ("iota", P), ("rev", E), ("thr", TT), ("tri", E * E), ("blk", NT), ("dmask", C), ("pidx", 1),
         ("tbase", TT), ("ksel", KT * P), ("upper", P), ("mhi", 2 * P), ("mlo", 2 * P), ("mbias", 1), ("ones8", G8)]


def spans(table):
    at, out = 0, {}
    for name, width in table:
        out[name] = slice(at, at + width)
        at += width
    return out, at


SM, SMALL_W = spans(SMALL)
CO, CONST_W = spans(CONST)


def bc(ap, axis, n):
    u = ap.unsqueeze(axis)
    shape = list(u.shape)
    shape[axis] = n
    return u.to_broadcast(shape)


class Region:

    def __init__(self, flat, at=0):
        self.flat, self.at = flat, at

    def __call__(self, shape, dt=F32):
        size = int(np.prod(shape[1:]))
        words = size * mybir.dt.size(dt) // 4
        ap = self.flat[0:shape[0], self.at:self.at + words]
        self.at += words
        assert self.at <= self.flat.shape[1]
        if dt != self.flat.dtype:
            ap = ap.bitcast(dt)
        names = " ".join(f"d{i}" for i in range(len(shape) - 1))
        return ap.rearrange(f"p ({names}) -> p {names}", **{f"d{i}": n for i, n in enumerate(shape[1:])})


def build(nc, A):
    with ExitStack() as ctx:
        def sb(name, shape, dt=F32):
            return ctx.enter_context(nc.sbuf_tensor(name, shape, dt))

        def sem(name):
            return ctx.enter_context(nc.semaphore(name))

        psum = ctx.enter_context(nc.psum_tensor("psum", [P, 8, 512], F32))
        bank = [psum[:, i] for i in range(8)]

        xc_rows = nc.dram_tensor("xc_rows", (T, L), F32, kind="Internal").ap()
        y_slots = nc.dram_tensor("y_slots", (ET * P, L), F32, kind="Internal").ap()

        small = sb("small", [P, SMALL_W])
        const = sb("const", [P, CONST_W])
        sm = {k: small[:, v] for k, v in SM.items()}
        co = {k: const[:, v] for k, v in CO.items()}
        ident = co["ident"]

        x_rows = sb("x_rows", [P, TT, L])
        x4 = sb("x4", [P, N, NB + 2])
        wconv = sb("wconv", [P, 3, P])
        xcT = sb("xcT", [P, S, T])
        xc_stage = sb("xc_stage", [P, 2, L])
        diag = sb("diag", [P, N, C])
        ctxrep = sb("ctxrep", [P, T])
        ctxb = sb("ctxb", [N, C])
        ones = sb("ones", [P, P])
        ones_bf = sb("ones_bf", [P, P], BF16)
        upper_bf = sb("upper_bf", [P, P], BF16)
        h1T = sb("h1T", [D, N])
        h2T = sb("h2T", [D, N])
        att = sb("att", [N, KE])
        attw = sb("attw", [N, KE + 3])
        attT = sb("attT", [KE, N])
        aggb = sb("aggb", [N, C])
        aggbrep = sb("aggbrep", [P, T])
        bd = sb("bd", [P, TT, P])

        w12_at = nc.sbuf_base
        w12 = sb("w12", [P, E, S, 2 * INTER])
        w3 = sb("w3", [INTER, E, L])
        sw12 = sb("sw12", [P, S, 4 * INTER])
        sw3 = sb("sw3", [P, MC, L])
        b3x = sb("b3x", [E + 1, L])
        hs = sb("hs", [P, MC, T])

        al = [a.rearrange("p (n i) -> p n i", n=N) for a in (ctxrep[:], bd[:].rearrange("p t k -> p (t k)"))]

        after_conv = Region(x4[:].rearrange("p n b -> p (n b)"))
        score = sb("score", [P, TT, E])
        ra = sb("ra", [P, TT, E])
        rbuf = sb("rbuf", [P, TT, E])
        rc = sb("rc", [P, TT, E])
        masked = sb("masked", [P, TT, E])
        pick = [sb(f"pick{c}", [P, TT, E]) for c in range(TOPK)]
        gpick = [sb(f"gpick{c}", [P, TT, EG]) for c in range(TOPK)]
        gm = sb("gm", [P, TT, EG])
        gt1 = sb("gt1", [P, TT, EG])
        r1 = sb("r1", [P, TT])
        r2 = sb("r2", [P, TT])
        gate = sb("gate", [P, TOPK, TT])
        gate17 = sb("gate17", [P, TT, E + 1])
        gateT = diag[0:E + 1].rearrange("p n c -> p (n c)")
        sel_bf = sb("sel_bf", [P, TT, E], BF16)
        cntj = sb("cntj", [P, E, TT])
        ntile = sb("ntile", [P, E])
        tri_w = after_conv([P, E, E])
        tstart = sb("tstart", [P, E])
        tend = sb("tend", [P, E])
        slot_f = sb("slot_f", [P, TOPK, TT])
        slot_i = sb("slot_i", [P, TOPK, TT], I32)
        sq_i = sb("sq_i", [P, TOPK, TT], I32)
        sr_i = sb("sr_i", [P, TOPK, TT], I32)
        sq_f = sb("sq_f", [P, TOPK, TT])
        sr_f = sb("sr_f", [P, TOPK, TT])
        silu_s = after_conv([P, 2, 512])
        onehot_r = after_conv([P, TOPK, TT, P], BF16)
        onehot_q = after_conv([P, TOPK, TT, 32])
        tok_p = after_conv([P, TOPK, TT, 32], BF16)
        tok_t = after_conv([P, TOPK, TT, 32], BF16)
        tok_of_slot = sb("tok_of_slot", [P, 32], I32)
        eidw = after_conv([P, 32, E])
        eid_f = sb("eid_f", [P, 32])
        expert_of_tile = sb("expert_of_tile", [P, 32], I32)

        after_shared = Region(xcT[:].rearrange("p j t -> p (j t)"))
        xg = [after_shared([P, L]) for _ in range(2)]
        xgT = [after_shared([P, S, P]) for _ in range(2)]
        h12 = [after_shared([P, 2 * INTER]) for _ in range(2)]
        sil = [after_shared([P, INTER]) for _ in range(2)]
        hid = [after_shared([P, INTER]) for _ in range(2)]
        hidT = [after_shared([INTER, P]) for _ in range(2)]
        b12rep = [after_shared([P, 2 * INTER]) for _ in range(2)]
        y_sb = [xc_stage[:, i] for i in range(2)]
        yg = [hs[:].rearrange("p m t -> p (m t)")[:, L * i:L * i + L] for i in range(4)]

        after_al = Region(ctxrep[:])
        qw = after_al([P, QT, L // 32], I32)
        lut4 = after_al([P, NG, G8])
        bits = Region(x4[:].rearrange("p n b -> p (n b)"))([P, RING, L], BF16)
        lut4_parts = Region(diag[:].rearrange("p n c -> p (n c)"))([P, NG, PARTS, G8], BF16)
        match = Region(wconv[:].rearrange("p d m -> p (d m)"))([P, 2, 2, P], BF16)
        rounded_words = HALVES * (2 * 2 * P + 2 * L + 2 * LT * P + 2 * LT * O) + 2 * L + 2 * P
        rounded = Region(nc.alloc_sbuf_tensor_at("rounded", [P, rounded_words], F32R, offset=w12_at)[:])
        after_up = Region(w12[:].rearrange("p e j m -> p (e j m)"), rounded_words)
        lut8 = [after_up([P, 2, P]) for _ in range(2)]
        lut8_halves = [rounded([P, HALVES, 2, P], F32R) for _ in range(2)]
        place = rounded([P, 2 * P - G8], F32R)
        hot_hi = [rounded([P, L], F32R) for _ in range(2)]
        hot_lo = [after_up([P, L], BF16) for _ in range(4)]
        prod = [rounded([P, HALVES, L], F32R) for _ in range(2)]
        wTh = rounded([P, HALVES, LT, O], F32R)
        wTl = rounded([P, HALVES, LT, O], F32R)
        after_down = Region(w3[:].rearrange("p e l -> p (e l)"))
        xb = after_down([P, TT, L])
        ybias = after_down([P, L])
        w_rows = after_down([P, NBLOCK, L])
        aT_halves = [rounded([P, HALVES, LT, P], F32R) for _ in range(2)]
        sq = [after_down([P, LT, P]) for _ in range(2)]
        high = [after_down([P, 1], I32) for _ in range(2)]
        after_tiles = Region(xcT[:].rearrange("p j t -> p (j t)"))
        wTl_sum = after_tiles([P, LT, O])
        aT = [after_tiles([P, LT, P]) for _ in range(2)]
        ysel = [after_tiles([P, L]) for _ in range(2)]

        s_small = sem("small_loaded")
        s_const = sem("const_loaded")
        s_x4 = [sem(f"x4_loaded{i}") for i in range(4)]
        s_wconv = sem("wconv_loaded")
        s_xrows = sem("x_rows_loaded")
        s_shared = sem("shared_weights_loaded")
        s_b3 = sem("b3_loaded")
        s_w = sem("expert_weights_loaded")
        s_ones = sem("ones_ready")
        s_masks = sem("masks_ready")
        s_ctx = sem("ctx_summed")
        s_diag = sem("ctx_diag_ready")
        s_ctxrep_mm = sem("ctx_spread")
        s_ctxrep = sem("ctx_on_all_partitions")
        s_h1 = sem("att_h1_summed")
        s_h1T = sem("att_h1_ready")
        s_h2 = sem("att_h2_summed")
        s_h2T = sem("att_h2_ready")
        s_attl = sem("att_logits_summed")
        s_attm = sem("att_logits_shifted")
        s_attex = sem("att_exp_ready")
        s_att = sem("att_ready")
        s_attTp = sem("att_turned")
        s_attT = sem("attT_ready")
        s_attrep = sem("att_spread")
        s_al = sem("att_mix_ready")
        s_agg = sem("agg_summed")
        s_aggbrep = sem("aggb_on_all_partitions")
        s_bd = sem("block_diagonal_ready")
        s_conv = sem("conv_summed")
        s_xcT = sem("conv_ready")
        s_turn = sem("conv_turned")
        s_stage = sem("conv_rows_staged")
        s_xcw = [sem(f"conv_rows_written{i}") for i in range(2)]
        s_logit = sem("router_logits_summed")
        s_rm = sem("router_logits_shifted")
        s_rexp = sem("router_exp_ready")
        s_sel = sem("chosen_ready")
        s_gate = sem("gates_ready")
        s_rank = sem("ranks_summed")
        s_hots = sem("slot_onehots_ready")
        s_toks = sem("slot_tokens_summed")
        s_route = sem("routing_ready")
        s_gTp = sem("gates_turned")
        s_gT = sem("gateT_ready")
        s_sup = sem("shared_up_summed")
        s_silu = sem("shared_silu_ready")
        s_hs = sem("shared_hidden_ready")
        s_z = sem("shared_out_summed")
        s_zadd = sem("shared_out_added")
        s_gather = [sem(f"rows_gathered{i}") for i in range(2)]
        s_xTp = sem("rows_turned")
        s_xTe = sem("rows_turned_copied")
        s_b12 = [sem(f"expert_bias_loaded{i}") for i in range(2)]
        s_up = sem("expert_up_summed")
        s_hb = sem("expert_bias_added")
        s_hsilu = sem("expert_silu_ready")
        s_hg = sem("expert_hidden_ready")
        s_hTp = sem("expert_hidden_turned")
        s_hTe = sem("expert_hidden_turned_copied")
        s_down = sem("expert_down_summed")
        s_ye = sem("expert_out_copied")
        s_yw = [sem(f"expert_out_written{i}") for i in range(2)]
        s_back = [sem(f"out_rows_gathered{i}") for i in range(4)]
        s_comb = sem("out_rows_added")
        s_q = sem("packed_bits_loaded")
        s_l4 = sem("lut4_loaded")
        s_l4p = sem("lut4_split")
        s_match = sem("match_weights_ready")
        s_bits = sem("bit_chunks_ready")
        s_lut8 = [sem(f"lut8_loaded{i}") for i in range(2)]
        s_l8hi = sem("table_rounded")
        s_l8 = sem("table_halves_ready")
        s_place = sem("placing_ones_ready")
        s_mh = sem("high_nibbles_matched")
        s_ml = sem("low_nibbles_matched")
        s_hi = sem("high_onehot_ready")
        s_lo = sem("low_onehot_ready")
        s_G = sem("table_rows_summed")
        s_prod = sem("values_chosen")
        s_wblock = sem("weight_rows_summed")
        s_wrows = sem("weight_rows_bank_free")
        s_wl = sem("low_weights_summed")
        s_wlfree = sem("low_weights_bank_free")
        s_wTp = sem("weights_turned")
        s_whi = sem("weights_rounded")
        s_wlo = sem("weight_rests_ready")
        s_aThi = sem("linear_input_rounded")
        s_aTlo = sem("linear_input_rest_ready")
        s_ybias = sem("ybias_loaded")
        s_pool = sem("pool_chain")
        s_xb = sem("residual_bias_ready")
        s_amm = sem("linear_input_summed")
        s_aT = sem("linear_input_ready")
        s_sq = sem("squares_ready")
        s_norm = sem("norms_summed")
        s_high = sem("precision_chosen")
        s_ymm = sem("linear_summed")
        s_ylc = sem("low_result_copied")
        s_ysel = sem("result_chosen")
        s_yout = sem("result_ready")
        s_out = [sem(f"result_written{i}") for i in range(2)]
        s_v = sem("vector_chain")
        s_a = sem("scalar_chain")

        def over_tiles(eng, step, last):
            for kk in range(2):
                step(kk, 0)
                step(kk, 1)
            with eng.Fori(2, (ET - 1) // 2) as kk:
                step(kk, 0)
                step(kk, 1)
            for k in range(ET - 1, last + 1):
                step(k // 2, k % 2)

        block = ctx.enter_context(nc.Block())

        @block.sync
        def _(sp):
            sp.dma_start(small[:], A["small"]).then_inc(s_small, 16)
            sp.dma_start(wconv[:], A["wconv"]).then_inc(s_wconv, 16)
            for i in range(4):
                sp.dma_start(x4[:, 8 * i:8 * i + 8, :], A["x4"][:, 8 * i:8 * i + 8, :]).then_inc(s_x4[i], 16)
            sp.dma_start(sw12[:], A["sw12"]).then_inc(s_shared, 16)
            sp.dma_start(sw3[:], A["sw3"]).then_inc(s_shared, 16)
            sp.dma_start(b3x[:], A["b3x"]).then_inc(s_b3, 16)
            sp.dma_start(x_rows[:], A["x_rows"]).then_inc(s_xrows, 16)
            for e in range(0, E, 2):
                sp.wait_ge(s_stage, e // 2 + 1)
                sp.dma_start(w12[:, e:e + 2], A["w12"][:, e:e + 2]).then_inc(s_w, 16)
                sp.dma_start(w3[:, e:e + 2], A["w3"][:, e:e + 2]).then_inc(s_w, 16)
                if e == 8:
                    sp.wait_ge(s_agg, 1)
                    sp.dma_start(qw, A["q"]).then_inc(s_q, 16)
                    sp.dma_start(lut4, A["lut4"]).then_inc(s_l4, 16)
            sp.wait_ge(s_route, 1)
            sp.wait_ge(s_sup, 2 * MC)

            def step(kk, par):
                k = 2 * kk + par
                if not isinstance(k, int) or k < ET:
                    if not isinstance(k, int) or k >= 2:
                        sp.wait_ge(s_hb, k - 1)
                    e = sp.value_load(expert_of_tile[0:1, bass.ds(k, 1)], min_val=0, max_val=E - 1)
                    sp.dma_start(b12rep[par], A["b12"][bass.ds(e, 1), :].partition_broadcast(P)).then_inc(s_b12[par], 16)
                if not isinstance(k, int) or k >= 2:
                    sp.wait_ge(s_ye, k - 1)
                    sp.dma_start(y_slots[bass.ds((k - 2) * P, P), :], y_sb[par]).then_inc(s_yw[par], 16)

            over_tiles(sp, step, ET + 1)

            sp.wait_ge(s_up, ET)

            def tables(u, par):
                t = 2 * u + par
                if not isinstance(t, int) or t >= 2:
                    sp.wait_ge(s_l8, t - 1)
                sp.dma_start(lut8[par], A["lut8"][bass.ds(t, 1)].rearrange("a p g m -> p (a g) m")).then_inc(s_lut8[par], 16)

            tables(0, 0)
            tables(0, 1)
            sp.wait_ge(s_down, ET)
            sp.dma_start(ybias, A["ybias"].partition_broadcast(P)).then_inc(s_ybias, 16)
            with sp.Fori(1, QT // 2) as u:
                tables(u, 0)
                tables(u, 1)
            for t in range(TT):
                sp.wait_ge(s_yout, t + 1)
                sp.dma_start(A["out"][P * t:P * t + P, :], ysel[t % 2]).then_inc(s_out[t % 2], 16)
            for i in range(2):
                sp.wait_ge(s_out[i], 16 * TT // 2)

        @block.gpsimd
        def _(pool):
            nc.gpsimd.memset(ones[:], 1.0).then_inc(s_ones, 1)
            nc.gpsimd.memset(ones_bf[:], 1.0).then_inc(s_ones, 1)
            nc.gpsimd.memset(gate17[:], 1.0).then_inc(s_ones, 1)
            pool.wait_ge(s_const, 16)
            nc.gpsimd.tensor_copy(upper_bf[:], co["upper"]).then_inc(s_masks, 1)
            pool.wait_ge(s_route, 2)
            pool.wait_ge(s_sup, 2 * MC)

            for i in range(2):
                pool.wait_ge(s_xcw[i], 16 * TT // 2)
            for k in range(ET):
                if k >= 2:
                    pool.wait_ge(s_xTp, k - 1)
                nc.gpsimd.indirect_dma_start(xg[k % 2], None, xc_rows,
                                             bass.IndirectOffsetOnAxis(tok_of_slot[:, k:k + 1], 0)).then_inc(s_gather[k % 2], 16)
            pool.wait_ge(s_yw[0], 16 * ((ET + 1) // 2))
            pool.wait_ge(s_yw[1], 16 * (ET // 2))
            pool.wait_ge(s_down, ET)
            pool.wait_ge(s_zadd, TT)
            pool.wait_ge(s_ybias, 16)
            chain = 0

            def gather_back(n):
                t, c = n // TOPK, n % TOPK
                nc.gpsimd.indirect_dma_start(yg[n % 4], None, y_slots,
                                             bass.IndirectOffsetOnAxis(slot_i[:, c, t:t + 1], 0)).then_inc(s_back[n % 4], 16)

            for n in range(4):
                gather_back(n)
            for t in range(TT):
                for c in range(TOPK):
                    n = TOPK * t + c
                    pool.wait_ge(s_back[n % 4], 16 * (n // 4 + 1))
                    nc.gpsimd.tensor_scalar(yg[n % 4], yg[n % 4], gate[:, c, t:t + 1], None, ALU.mult).then_inc(s_pool, 1)
                    chain += 1
                    pool.wait_ge(s_pool, chain)
                    if n >= 1:
                        pool.wait_ge(s_comb, n)
                    nc.gpsimd.tensor_tensor(x_rows[:, t], x_rows[:, t], yg[n % 4], ALU.add).then_inc(s_comb, 1)
                    if n + 4 < TOPK * TT:
                        pool.wait_ge(s_comb, n + 1)
                        gather_back(n + 4)
                pool.wait_ge(s_comb, TOPK * (t + 1))
                nc.gpsimd.tensor_tensor(xb[:, t], x_rows[:, t], ybias, ALU.add).then_inc(s_xb, 1)

        @block.scalar
        def _(act):
            act.dma_start(const[:], A["const"]).then_inc(s_const, 16)
            act.wait_ge(s_small, 16)
            act.wait_ge(s_h1, 1)
            nc.scalar.activation(h1T[:], bank[6][:, 0:N], ACT.Gelu, bias=sm["b0"]).then_inc(s_h1T, 1)
            act.wait_ge(s_h2, 1)
            nc.scalar.activation(h2T[:], bank[6][:, 0:N], ACT.Gelu, bias=sm["b1"]).then_inc(s_h2T, 1)
            for h in range(2):
                act.wait_ge(s_ctxrep_mm, h + 1)
                nc.scalar.activation(ctxrep[:, 512 * h:512 * h + 512], bank[4 + 3 * h], ACT.Copy).then_inc(s_ctxrep, 1)

            def stage_rows(t):
                act.wait_ge(s_turn, t + 1)
                if t >= 2:
                    act.wait_ge(s_xcw[t % 2], 16 * (t // 2))
                nc.scalar.activation(xc_stage[:, t % 2], bank[2 + t % 2], ACT.Copy).then_inc(s_stage, 1)
                act.wait_ge(s_stage, t + 1)
                act.dma_start(xc_rows[P * t:P * t + P, :], xc_stage[:, t % 2]).then_inc(s_xcw[t % 2], 16)

            for t in range(4):
                stage_rows(t)
            act.wait_ge(s_attm, 1)
            nc.scalar.activation(att[:], attw[:, 0:KE], ACT.Exp, accum_out=attw[:, KE + 1:KE + 2]).then_inc(s_attex, 1)
            for t in range(4, TT):
                stage_rows(t)
            act.wait_ge(s_attTp, 1)
            nc.scalar.activation(attT[:], bank[6][0:KE, 0:N], ACT.Copy).then_inc(s_attT, 1)
            act.wait_ge(s_rm, 1)
            nc.scalar.activation(ra[:], rbuf[:], ACT.Exp).then_inc(s_rexp, 1)

            def shared_silu(n):
                act.wait_ge(s_sup, n + 1)
                if n >= 2:
                    act.wait_ge(s_hs, n - 1)
                nc.scalar.activation(silu_s[:, n % 2], bank[2 * (n % 2)], ACT.Silu,
                                     bias=sm["sb1"][:, n % MC:n % MC + 1]).then_inc(s_silu, 1)

            shared_silu(0)
            shared_silu(1)
            for h in range(2):
                act.wait_ge(s_agg, h + 2)
                nc.scalar.activation(aggbrep[:, 512 * h:512 * h + 512], bank[6 + h], ACT.Copy).then_inc(s_aggbrep, 1)
            shared_silu(2)
            for h in range(2):
                act.wait_ge(s_gTp, h + 1)
                nc.scalar.activation(gateT[:, 512 * h:512 * h + 512], bank[5 - h][0:E + 1, :], ACT.Copy).then_inc(s_gT, 1)
            shared_silu(3)

            def turned_rows(kk, par):
                k = 2 * kk + par
                act.wait_ge(s_xTp, k + 1)
                if not isinstance(k, int) or k >= 2:
                    act.wait_ge(s_up, k - 1)
                nc.scalar.activation(xgT[par].rearrange("p j t -> p (j t)"), bank[par], ACT.Copy).then_inc(s_xTe, 1)

            def step(kk, par):
                k = 2 * kk + par
                if not isinstance(k, int) or k + 1 < ET:
                    turned_rows(kk + par, 1 - par)
                if not isinstance(k, int) or k >= 2:
                    act.wait_ge(s_down, k - 1)
                    if not isinstance(k, int) or k >= 4:
                        act.wait_ge(s_yw[par], 16 * (kk - 1))
                    nc.scalar.activation(y_sb[par], bank[5 + par], ACT.Copy).then_inc(s_ye, 1)
                if not isinstance(k, int) or k < ET:
                    act.wait_ge(s_hb, k + 1)
                    if not isinstance(k, int) or k >= 2:
                        act.wait_ge(s_hg, k - 1)
                    nc.scalar.activation(sil[par], h12[par][:, 0:INTER], ACT.Silu).then_inc(s_hsilu, 1)

            turned_rows(0, 0)
            over_tiles(act, step, ET + 1)

            def round_table(t, u, par):
                act.wait_ge(s_lut8[par], 16 * (u + 1))
                nc.scalar.activation(lut8_halves[par][:, 0], lut8[par], ACT.Copy).then_inc(s_l8hi, 1)

            def step(r, i, tables=True):
                g = BLOCK * r + i
                act.wait_ge(s_mh, g + 1)
                nc.scalar.activation(hot_hi[i % 2], bank[0], ACT.Relu, bias=co["mbias"]).then_inc(s_hi, 1)
                act.wait_ge(s_ml, g + 1)
                nc.scalar.activation(hot_lo[i % 4], bank[1], ACT.Relu, bias=co["mbias"]).then_inc(s_lo, 1)
                if i % 2 == 1 and tables:
                    t = BLOCK // 2 * r + (i + 1) // 2
                    round_table(t, BLOCK // 4 * r + (i + 1) // 4, (i + 1) // 2 % 2)

            def copy_rows(r):
                act.wait_ge(s_wblock, r + 1)
                nc.scalar.activation(w_rows[:, bass.ds(r, 1)].rearrange("p a l -> p (a l)"), bank[6],
                                     ACT.Copy).then_inc(s_wrows, 1)

            act.wait_ge(s_up, ET)
            round_table(0, 0, 0)
            step(0, 0)
            step(0, 1)
            with act.Fori(0, NBLOCK - 1) as r:
                for i in range(2, BLOCK + 2):
                    step(r, i)
                copy_rows(r)
            for i in range(2, BLOCK):
                step(NBLOCK - 1, i, tables=i < BLOCK - 1)
            act.wait_ge(s_wlfree, QT + 1)
            nc.scalar.activation(wTl[:, 0], wTl_sum, ACT.Copy).then_inc(s_whi, 1)
            copy_rows(NBLOCK - 1)
            for j in range(LT):
                act.wait_ge(s_wTp, j + 1)
                nc.scalar.activation(wTh[:, 0, j], bank[5 - j], ACT.Copy).then_inc(s_whi, 1)

            def round_input(t):
                act.wait_ge(s_aT, t + 1)
                if t >= 2:
                    act.wait_ge(s_ymm, 2 * t - 2)
                nc.scalar.activation(aT_halves[t % 2][:, 0], aT[t % 2], ACT.Copy).then_inc(s_aThi, 1)

            round_input(0)
            act.wait_ge(s_aT, 1)
            nc.scalar.activation(sq[0].rearrange("p j t -> p (j t)"), aT[0].rearrange("p j t -> p (j t)"),
                                 ACT.Square).then_inc(s_sq, 1)
            for t in range(TT):
                if t + 1 < TT:
                    round_input(t + 1)
                    if t >= 1:
                        act.wait_ge(s_norm, t)
                    nc.scalar.activation(sq[(t + 1) % 2].rearrange("p j t -> p (j t)"),
                                         aT[(t + 1) % 2].rearrange("p j t -> p (j t)"), ACT.Square).then_inc(s_sq, 1)
                act.wait_ge(s_ymm, 2 * t + 1)
                if t >= 2:
                    act.wait_ge(s_out[t % 2], 16 * (t // 2))
                nc.scalar.activation(ysel[t % 2], bank[6 + t % 2], ACT.Copy).then_inc(s_ylc, 1)

        @block.vector
        def _(dve):
            chain = [0]

            def link(ins):
                chain[0] += 1
                ins.then_inc(s_v, 1)
                dve.wait_ge(s_v, chain[0])

            v = nc.vector
            dve.wait_ge(s_small, 16)
            dve.wait_ge(s_const, 16)
            dve.wait_ge(s_ctx, 1)
            link(v.tensor_tensor(ctxb[:], bank[5][0:N, 0:C], sm["convb"][0:N], ALU.add))
            v.tensor_tensor(diag[0:N], bc(ctxb[:], 1, N), bc(ident[0:N, 0:N], 2, C), ALU.mult).then_inc(s_diag, 1)

            def conv_out(t):
                dve.wait_ge(s_conv, t + 1)
                if t == 0:
                    dve.wait_ge(s_ctxrep, 2)
                cr = ctxrep[:, P * t:P * t + P].rearrange("p (n c) -> p n c", n=NT)
                v.tensor_tensor(
                    xcT[:, :, P * t:P * t + P].rearrange("p j (n c) -> p n j c", n=NT),
                    bank[t % 2].rearrange("p (n j c) -> p n j c", n=NT, j=S),
                    bc(cr, 2, S), ALU.add).then_inc(s_xcT, 1)

            for t in range(4):
                conv_out(t)
            dve.wait_ge(s_attl, 1)
            link(v.tensor_tensor(attw[:, 0:KE], bank[5][0:N, 0:KE], sm["b2"][0:N], ALU.add))
            link(v.tensor_reduce(attw[:, KE:KE + 1], attw[:, 0:KE], X, ALU.max))
            v.tensor_scalar(attw[:, 0:KE], attw[:, 0:KE], attw[:, KE:KE + 1], None, ALU.subtract).then_inc(s_attm, 1)
            for t in range(4, TT):
                conv_out(t)
            dve.wait_ge(s_attex, 1)
            link(v.reciprocal(attw[:, KE + 2:KE + 3], attw[:, KE + 1:KE + 2]))
            v.tensor_scalar(att[:], att[:], attw[:, KE + 2:KE + 3], None, ALU.mult).then_inc(s_att, 1)

            v.tensor_copy(match[:, 0].rearrange("p a m -> p (a m)"), co["mhi"]).then_inc(s_match, 1)
            v.tensor_copy(match[:, 1].rearrange("p a m -> p (a m)"), co["mlo"]).then_inc(s_match, 1)

            dve.wait_ge(s_logit, 1)
            link(v.tensor_tensor(score[:], bank[4][:, 0:TT * E].rearrange("p (t e) -> p t e", t=TT),
                                 bc(sm["rb"], 1, TT), ALU.add))
            link(v.tensor_reduce(r1[:], score[:], X, ALU.max))
            v.tensor_tensor(rbuf[:], score[:], bc(r1[:], 2, E), ALU.subtract).then_inc(s_rm, 1)

            dve.wait_ge(s_attrep, 2)
            for k in range(KT):
                v.tensor_tensor(al[k], bc(bank[5][:, N * k:N * k + N], 2, C), bc(co["dmask"], 1, N),
                                ALU.mult).then_inc(s_al, 1)
            link(v.tensor_copy(aggb[:], bank[6][0:N, 0:C]))
            v.tensor_tensor(diag[0:N], bc(aggb[:], 1, N), bc(ident[0:N, 0:N], 2, C), ALU.mult).then_inc(s_al, 1)

            dve.wait_ge(s_rexp, 1)
            link(v.tensor_reduce(r1[:], ra[:], X, ALU.add))
            link(v.reciprocal(r2[:], r1[:]))
            link(v.tensor_tensor(rbuf[:], ra[:], bc(r2[:], 2, E), ALU.mult))
            link(v.tensor_tensor(score[:], rbuf[:], bc(sm["rbias"], 1, TT), ALU.add))

            def first_max(out, m, n, a, b):
                link(v.tensor_reduce(r1[:], m, X, ALU.max))
                link(v.tensor_tensor(a, m, bc(r1[:], 2, n), ALU.is_equal))
                link(v.tensor_tensor(b, a, bc(co["rev"][:, 0:n], 1, TT), ALU.mult))
                link(v.tensor_reduce(r2[:], b, X, ALU.max))
                link(v.tensor_tensor(out, b, bc(r2[:], 2, n), ALU.is_equal))

            g4 = score[:].rearrange("p t (g k) -> p t g k", g=EG)
            link(v.tensor_reduce(gm[:], g4, X, ALU.max))
            first_max(gpick[0][:], gm[:], EG, ra[:, :, 0:EG], rc[:, :, 0:EG])
            link(v.scalar_tensor_tensor(gm[:], gpick[0][:], -BIG, gm[:], ALU.mult, ALU.add))
            first_max(gpick[1][:], gm[:], EG, ra[:, :, 0:EG], rc[:, :, 0:EG])
            link(v.tensor_tensor(gt1[:], gpick[0][:], gpick[1][:], ALU.add))
            link(v.tensor_scalar(gt1[:], gt1[:], BIG, -BIG, ALU.mult, ALU.add))
            link(v.tensor_tensor(masked[:].rearrange("p t (g k) -> p t g k", g=EG), g4, bc(gt1[:], 3, E // EG), ALU.add))
            first_max(pick[0][:], masked[:], E, ra[:], rc[:])
            link(v.scalar_tensor_tensor(masked[:], pick[0][:], -BIG, masked[:], ALU.mult, ALU.add))
            first_max(pick[1][:], masked[:], E, ra[:], rc[:])
            link(v.tensor_tensor(rbuf[:], pick[0][:], pick[1][:], ALU.add))
            v.tensor_copy(sel_bf[:], rbuf[:]).then_inc(s_sel, 1)
            dve.wait_ge(s_ones, 3)
            v.tensor_tensor(gate17[:, :, 0:E], rbuf[:], score[:], ALU.mult).then_inc(s_gate, 1)
            for c in range(TOPK):
                link(v.tensor_tensor(ra[:], pick[c][:], score[:], ALU.mult))
                link(v.tensor_reduce(gate[:, c], ra[:], X, ALU.add))

            dve.wait_ge(s_agg, 1)
            for t in range(TT):
                last = v.tensor_tensor(bd[:, t].rearrange("p (n c) -> p n c", n=NT),
                                       bc(bank[5][:, C * t:C * t + C], 1, NT), bc(co["blk"], 2, C), ALU.mult)
            last.then_inc(s_bd, 1)

            def shared_hidden(n):
                half, m = n // MC, n % MC
                dve.wait_ge(s_silu, n + 1)
                v.scalar_tensor_tensor(hs[:, m, 512 * half:512 * half + 512], bank[2 * (n % 2) + 1],
                                       sm["sb2"][:, m:m + 1], silu_s[:, n % 2], ALU.add, ALU.mult).then_inc(s_hs, 1)

            shared_hidden(0)
            shared_hidden(1)

            dve.wait_ge(s_rank, 2)
            link(v.tensor_tensor(cntj[:], bc(bank[6][:, 0:E], 2, TT), bc(co["thr"], 1, E), ALU.is_gt))
            link(v.tensor_reduce(ntile[:], cntj[:], X, ALU.add))
            link(v.tensor_tensor(tri_w[:], bc(ntile[:], 1, E), co["tri"].rearrange("p (a b) -> p a b", a=E), ALU.mult))
            link(v.tensor_reduce(tstart[:], tri_w[:], X, ALU.add))
            link(v.tensor_tensor(tend[:], tstart[:], ntile[:], ALU.add))
            link(v.tensor_scalar(tstart[:], tstart[:], float(P), None, ALU.mult))
            link(v.tensor_tensor(ra[:], bank[7][:, 0:TT * E].rearrange("p (t e) -> p t e", t=TT),
                                 bc(tstart[:], 1, TT), ALU.add))
            for c in range(TOPK):
                link(v.tensor_tensor(rc[:], pick[c][:], ra[:], ALU.mult))
                link(v.tensor_reduce(slot_f[:, c], rc[:], X, ALU.add))
            link(v.tensor_copy(slot_i[:], slot_f[:]))
            link(v.tensor_scalar(sq_i[:], slot_i[:], 7, None, ALU.logical_shift_right))
            link(v.tensor_scalar(sr_i[:], slot_i[:], P - 1, None, ALU.bitwise_and))
            link(v.tensor_copy(sq_f[:], sq_i[:]))
            link(v.tensor_copy(sr_f[:], sr_i[:]))
            for c in range(TOPK):
                link(v.tensor_tensor(onehot_r[:, c], bc(co["iota"], 1, TT), bc(sr_f[:, c], 2, P), ALU.is_equal))
                link(v.tensor_tensor(onehot_q[:, c], bc(co["iota"][:, 0:32], 1, TT), bc(sq_f[:, c], 2, 32), ALU.is_equal))
                v.tensor_scalar(tok_p[:, c], onehot_q[:, c], co["pidx"], None, ALU.mult).then_inc(s_hots, 1)
                v.tensor_tensor(tok_t[:, c], onehot_q[:, c], bc(co["tbase"], 2, 32), ALU.mult).then_inc(s_hots, 1)
            link(v.tensor_tensor(eidw[:], bc(tend[:], 1, 32), bc(co["iota"][:, 0:32], 2, E), ALU.is_le))
            link(v.tensor_reduce(eid_f[:], eidw[:], X, ALU.add))
            v.tensor_scalar(expert_of_tile[:], eid_f[:], float(E - 1), None, ALU.min).then_inc(s_route, 1)
            shared_hidden(2)
            shared_hidden(3)
            dve.wait_ge(s_toks, 1)
            v.tensor_copy(tok_of_slot[:], bank[4][:, 0:32]).then_inc(s_route, 1)
            dve.wait_ge(s_xrows, 16)
            for t in range(TT):
                dve.wait_ge(s_z, t + 1)
                v.tensor_tensor(x_rows[:, t], x_rows[:, t], bank[t % 4], ALU.add).then_inc(s_zadd, 1)

            def step(kk, par):
                k = 2 * kk + par
                if not isinstance(k, int) or k >= 1:
                    dve.wait_ge(s_hTp, k)
                    if not isinstance(k, int) or k >= 3:
                        dve.wait_ge(s_down, k - 2)
                    v.tensor_copy(hidT[1 - par], bank[4][:, 0:P]).then_inc(s_hTe, 1)
                if not isinstance(k, int) or k < ET:
                    dve.wait_ge(s_up, k + 1)
                    dve.wait_ge(s_b12[par], 16 * (kk + 1))
                    if not isinstance(k, int) or k >= 2:
                        dve.wait_ge(s_hg, k - 1)
                    v.tensor_tensor(h12[par], bank[2 + par][:, 0:2 * INTER], b12rep[par], ALU.add).then_inc(s_hb, 1)
                    dve.wait_ge(s_hsilu, k + 1)
                    v.tensor_tensor(hid[par], sil[par], h12[par][:, INTER:2 * INTER], ALU.mult).then_inc(s_hg, 1)

            def make_bit(c, n):
                move = (14 - n % 16, ALU.logical_shift_left) if n % 16 < 15 else (1, ALU.logical_shift_right)
                halves = qw[:, bass.ds(CHUNK * c, CHUNK)].rearrange("p t w -> p (t w)").bitcast(U16)
                halves = halves.rearrange("p (t h) -> p t h", h=2)
                out = bits[:, bass.ds(CHUNK * (c % 2), CHUNK)].bitcast(U16).rearrange("p t (w s) -> p (t w) s", s=32)
                ins = v.tensor_scalar(out[:, :, n], halves[:, :, n // 16], move[0], 0x4000, move[1], ALU.bitwise_and)
                if n == 31:
                    ins.then_inc(s_bits, 1)

            dve.wait_ge(s_q, 16)
            for n in range(32):
                make_bit(0, n)
                make_bit(1, n)
            dve.wait_ge(s_l4, 16)
            for k in range(PARTS):
                link(v.tensor_copy(lut4_parts[:, :, k], lut4))
                if k < PARTS - 1:
                    link(v.tensor_tensor(lut4, lut4, lut4_parts[:, :, k], ALU.subtract))

            over_tiles(dve, step, ET)

            link(v.tensor_scalar(place, co["pidx"].to_broadcast([P, 2 * P - G8]), 0.0, None, ALU.mult))
            v.tensor_copy(place[:, P - G8:P], co["ones8"]).then_inc(s_place, 1)

            def split_table(t, par):
                dve.wait_ge(s_l8hi, t + 1)
                v.tensor_tensor(lut8_halves[par][:, 1], lut8[par], lut8_halves[par][:, 0].bitcast(F32),
                                ALU.subtract).then_inc(s_l8, 1)

            def copy_weights(t):
                dve.wait_ge(s_wl, t + 1)
                v.tensor_reduce(wTl_sum[:, :, bass.ds(OI * t, OI)].rearrange("p i (g c) -> p i g c", g=2),
                                bank[7][:, 0:LT * 2 * PARTS * G8].rearrange("p (i g k c) -> p i g c k", g=2, k=PARTS, c=G8),
                                X, ALU.add).then_inc(s_wlfree, 1)

            def step(r, i):
                g = BLOCK * r + i
                t = BLOCK // 2 * r + i // 2
                dve.wait_ge(s_G, g + 1)
                dve.wait_ge(s_lo, g + 1)
                v.tensor_tensor(prod[i % 2], bc(hot_lo[i % 4], 1, HALVES), psum[:, 2 + 2 * (i % 2):4 + 2 * (i % 2)],
                                ALU.mult).then_inc(s_prod, 1)
                if i % 2 == 1:
                    copy_weights(t)
                elif not isinstance(g, int) or t + 1 < QT:
                    split_table(t + 1, (i // 2 + 1) % 2)

            v.memset(r1[:], 0.0).then_inc(s_wrows, 1)
            v.memset(r2[:], 0.0).then_inc(s_wlfree, 1)
            split_table(0, 0)
            for i in range(BLOCK):
                step(0, i)
            with dve.Fori(1, NBLOCK - 1) as r:
                dve.wait_ge(s_ml, BLOCK * r)
                for i in range(BLOCK):
                    step(r, i)
                    for n in range(3 * i, min(3 * i + 3, 32)):
                        make_bit(r + 1, n)
            for i in range(BLOCK):
                step(NBLOCK - 1, i)
            dve.wait_ge(s_whi, 1)
            dve.wait_ge(s_wlfree, QT + 1)
            v.tensor_tensor(wTl[:, 1], wTl_sum, wTl[:, 0].bitcast(F32), ALU.subtract).then_inc(s_wlo, 1)
            for j in range(LT):
                dve.wait_ge(s_whi, j + 2)
                v.tensor_tensor(wTh[:, 1, j], bank[5 - j], wTh[:, 0, j].bitcast(F32), ALU.subtract).then_inc(s_wlo, 1)

            def linear_in(t):
                dve.wait_ge(s_amm, t + 1)
                if t >= 2:
                    dve.wait_ge(s_aTlo, t - 1)
                    dve.wait_ge(s_sq, t - 1)
                v.tensor_tensor(aT[t % 2], bank[t % 2].rearrange("p (j k) -> p j k", j=LT),
                                bc(aggbrep[:, P * t:P * t + P], 1, LT), ALU.add).then_inc(s_aT, 1)
                dve.wait_ge(s_aThi, t + 1)
                v.tensor_tensor(aT_halves[t % 2][:, 1], aT[t % 2], aT_halves[t % 2][:, 0].bitcast(F32),
                                ALU.subtract).then_inc(s_aTlo, 1)

            linear_in(0)
            for t in range(TT):
                dve.wait_ge(s_norm, t + 1)
                v.tensor_scalar(high[t % 2], bank[5][:, 0:1], EST_SQ, None, ALU.is_gt).then_inc(s_high, 1)
                if t + 1 < TT:
                    linear_in(t + 1)
                dve.wait_ge(s_ylc, t + 1)
                dve.wait_ge(s_ymm, 2 * t + 2)
                dve.wait_ge(s_high, t + 1)
                v.copy_predicated(ysel[t % 2], high[t % 2].to_broadcast([P, L]), bank[3 + t % 2]).then_inc(s_ysel, 1)
                dve.wait_ge(s_ysel, t + 1)
                dve.wait_ge(s_xb, t + 1)
                v.tensor_tensor(ysel[t % 2], ysel[t % 2], xb[:, t], ALU.add).then_inc(s_yout, 1)

        @block.tensor
        def _(pe):
            mm = nc.tensor.matmul
            pe.wait_ge(s_small, 16)
            mm(bank[5][0:N, 0:C], sm["cT"], sm["cwT"], start=True, stop=True).then_inc(s_ctx, 1)
            mm(bank[6][:, 0:N], sm["W0"], sm["cT"], start=True, stop=True).then_inc(s_h1, 1)
            pe.wait_ge(s_h1T, 1)
            mm(bank[6][:, 0:N], sm["W1"], h1T[:], start=True, stop=True).then_inc(s_h2, 1)
            pe.wait_ge(s_ones, 3)
            pe.wait_ge(s_diag, 1)
            for h in range(2):
                mm(bank[4 + 3 * h], ones[0:N, :], diag[0:N, 16 * h:16 * h + 16, :].rearrange("p n c -> p (n c)"),
                   start=True, stop=True).then_inc(s_ctxrep_mm, 1)
            pe.wait_ge(s_wconv, 16)

            def conv(t):
                pe.wait_ge(s_x4[t // 2], 16)
                if t >= 2:
                    pe.wait_ge(s_xcT, t - 1)
                for k in range(NT):
                    for d in range(3):
                        last = mm(bank[t % 2][:, P * k:P * k + P], x4[:, NT * t + k, d:d + NB], wconv[:, d],
                                  start=(d == 0), stop=(d == 2))
                last.then_inc(s_conv, 1)

            def turn(t):
                pe.wait_ge(s_xcT, t + 1)
                if t == 0:
                    pe.wait_ge(s_const, 16)
                    pe.wait_ge(s_ctxrep, 1)
                if t >= 2:
                    pe.wait_ge(s_stage, t - 1)
                for j in range(S):
                    last = nc.tensor.transpose(bank[2 + t % 2][:, P * j:P * j + P], xcT[:, j, P * t:P * t + P], ident)
                last.then_inc(s_turn, 1)
                for j in range(S):
                    last = mm(bank[4][:, E * t:E * t + E], xcT[:, j, P * t:P * t + P], sm["rw"][:, E * j:E * j + E],
                              start=(j == 0), stop=(j == S - 1))
                if t == TT - 1:
                    last.then_inc(s_logit, 1)

            for t in range(TT):
                conv(t)
                if t >= 1:
                    turn(t - 1)
                if t == 3:
                    pe.wait_ge(s_h2T, 1)
                    mm(bank[5][0:N, 0:KE], h2T[:], sm["W2"], start=True, stop=True).then_inc(s_attl, 1)
            turn(TT - 1)

            def shared_up(n):
                half, m = n // MC, n % MC
                if n == 0:
                    pe.wait_ge(s_shared, 32)
                if n == 1:
                    pe.wait_ge(s_stage, TT)
                if n >= 2:
                    pe.wait_ge(s_hs, n - 1)
                for w in range(2):
                    for j in range(S):
                        last = mm(bank[2 * (n % 2) + w], sw12[:, j, 256 * w + P * m:256 * w + P * m + P],
                                  xcT[:, j, 512 * half:512 * half + 512], start=(j == 0), stop=(j == S - 1))
                last.then_inc(s_sup, 1)

            def shared_down(t):
                pe.wait_ge(s_hs, 2 if t < 4 else 4)
                if t < 4:
                    pe.wait_ge(s_gT, 2)
                else:
                    pe.wait_ge(s_zadd, t - 3)
                for m in range(MC):
                    mm(bank[t % 4], hs[:, m, P * t:P * t + P], sw3[:, m], start=(m == 0), stop=False)
                mm(bank[t % 4], gateT[:, P * t:P * t + P], b3x[:], start=False, stop=True).then_inc(s_z, 1)

            shared_up(0)
            pe.wait_ge(s_att, 1)
            nc.tensor.transpose(bank[6][0:KE, 0:N], att[:], ident[0:N, 0:N]).then_inc(s_attTp, 1)
            pe.wait_ge(s_attT, 1)
            for k in range(KT):
                mm(bank[5][:, N * k:N * k + N], co["ksel"][0:KE, P * k:P * k + P], attT[:], start=True, stop=True)
            last = mm(bank[6][0:N, 0:C], attT[:], sm["bk"][0:KE], start=True, stop=True)
            last.then_inc(s_attrep, 2)
            shared_up(1)
            pe.wait_ge(s_al, 3)
            for t in range(TT):
                for k in range(KT):
                    last = mm(bank[5][:, C * t:C * t + C], al[k][:, NT * t:NT * t + NT, :].rearrange("p n i -> p (n i)"),
                              sm["wk"][:, C * k:C * k + C], start=(k == 0), stop=(k == KT - 1))
            last.then_inc(s_agg, 1)
            for h in range(2):
                mm(bank[6 + h], ones[0:N, :], diag[0:N, 16 * h:16 * h + 16, :].rearrange("p n c -> p (n c)"),
                   start=True, stop=True).then_inc(s_agg, 1)
            pe.wait_ge(s_sel, 1)
            pe.wait_ge(s_masks, 1)
            pe.wait_ge(s_aggbrep, 2)
            sel = sel_bf[:].rearrange("p t e -> p (t e)")
            mm(bank[7][:, 0:TT * E], upper_bf[:], sel, start=True, stop=False)
            for t in range(1, TT):
                last = mm(bank[7][:, t * E:TT * E], ones_bf[:], sel[:, 0:(TT - t) * E], start=False, stop=(t == TT - 1))
            last.then_inc(s_rank, 1)
            for t in range(TT):
                last = mm(bank[6][:, 0:E], ones_bf[:], sel[:, t * E:t * E + E], start=(t == 0), stop=(t == TT - 1))
            last.then_inc(s_rank, 1)
            shared_up(2)
            pe.wait_ge(s_gate, 1)
            pe.wait_ge(s_bd, 1)
            for h in range(2):
                for t in range(4 * h, 4 * h + 4):
                    last = nc.tensor.transpose(bank[5 - h][0:E + 1, P * (t % 4):P * (t % 4) + P], gate17[:, t], ident)
                last.then_inc(s_gTp, 1)
            shared_up(3)
            pe.wait_ge(s_b3, 16)
            pe.wait_ge(s_hs, 4)
            for t in range(4):
                shared_down(t)
            pe.wait_ge(s_hots, 4)
            n = 0
            for c in range(TOPK):
                for t in range(TT):
                    for part in (tok_p, tok_t):
                        last = mm(bank[4][:, 0:32], onehot_r[:, c, t], part[:, c, t],
                                  start=(n == 0), stop=(n == 2 * TOPK * TT - 1))
                        n += 1
            last.then_inc(s_toks, 1)
            for t in range(4, TT):
                shared_down(t)

            pe.wait_ge(s_w, 16 * E)
            pe.wait_ge(s_zadd, TT)
            pe.wait_ge(s_route, 2)

            def turn_rows(kk, par):
                k = 2 * kk + par
                pe.wait_ge(s_gather[par], 16 * (kk + 1))
                if not isinstance(k, int) or k >= 2:
                    pe.wait_ge(s_xTe, k - 1)
                for j in range(S):
                    last = nc.tensor.transpose(bank[par][:, P * j:P * j + P], xg[par][:, P * j:P * j + P], ident)
                last.then_inc(s_xTp, 1)

            def expert_of(k):
                return pe.value_load(expert_of_tile[0:1, bass.ds(k, 1)], min_val=0, max_val=E - 1)

            def step(kk, par):
                k = 2 * kk + par
                if not isinstance(k, int) or k >= 2:
                    e_down = expert_of(k - 2)
                if not isinstance(k, int) or k < ET:
                    e_up = expert_of(k)
                if not isinstance(k, int) or k + 1 < ET:
                    turn_rows(kk + par, 1 - par)
                if not isinstance(k, int) or k >= 2:
                    pe.wait_ge(s_hTe, k - 1)
                    if not isinstance(k, int) or k >= 4:
                        pe.wait_ge(s_ye, k - 3)
                    mm(bank[5 + par], hidT[par], w3[:, bass.ds(e_down, 1), :].rearrange("p a l -> p (a l)"),
                       start=True, stop=True).then_inc(s_down, 1)
                if not isinstance(k, int) or 1 <= k <= ET:
                    pe.wait_ge(s_hg, k)
                    nc.tensor.transpose(bank[4][:, 0:P], hid[1 - par], ident).then_inc(s_hTp, 1)
                if not isinstance(k, int) or k < ET:
                    pe.wait_ge(s_xTe, k + 1)
                    if not isinstance(k, int) or k >= 2:
                        pe.wait_ge(s_hb, k - 1)
                    for j in range(S):
                        last = mm(bank[2 + par][:, 0:2 * INTER], xgT[par][:, j],
                                  w12[:, bass.ds(e_up, 1), j, :].rearrange("p a m -> p (a m)"),
                                  start=(j == 0), stop=(j == S - 1))
                    last.then_inc(s_up, 1)

            turn_rows(0, 0)
            over_tiles(pe, step, ET + 1)

            def match_high(g, t, par):
                if par == 0:
                    pe.wait_ge(s_bits, t // CHUNK + 1)
                if not isinstance(g, int) or g >= 1:
                    pe.wait_ge(s_hi, g)
                mm(bank[0], match[:, 0, par], bits[:, bass.ds(t % RING, 1), :].rearrange("p a i -> p (a i)"),
                   start=True, stop=True).then_inc(s_mh, 1)

            def match_low(g, t, par):
                if not isinstance(g, int) or g >= 1:
                    pe.wait_ge(s_lo, g)
                mm(bank[1], match[:, 1, par], bits[:, bass.ds(t % RING, 1), :].rearrange("p a i -> p (a i)"),
                   start=True, stop=True).then_inc(s_ml, 1)

            def look_up(g, t, i):
                pe.wait_ge(s_hi, g + 1)
                if i % 2 == 0:
                    pe.wait_ge(s_l8, t + 1)
                for h in range(HALVES):
                    last = mm(bank[2 + 2 * (i % 2) + h], lut8_halves[i // 2 % 2][:, h, i % 2], hot_hi[i % 2],
                              start=True, stop=True)
                last.then_inc(s_G, 1)

            def step(r, i):
                g = BLOCK * r + i
                t = BLOCK // 2 * r + i // 2
                more = lambda n: not isinstance(g, int) or g + n < NG
                if more(2):
                    match_high(g + 2, t + 1, i % 2)
                if more(1):
                    look_up(g + 1, BLOCK // 2 * r + (i + 1) // 2, (i + 1) % BLOCK)
                if more(2):
                    match_low(g + 2, t + 1, i % 2)
                pe.wait_ge(s_lo, g + 1)
                if i % 2 == 0:
                    pe.wait_ge(s_wlfree, t + 1)
                for j in range(LT):
                    at = PARTS * G8 * (2 * j + i % 2)
                    last = mm(bank[7][:, at:at + PARTS * G8], hot_lo[i % 4][:, P * j:P * j + P],
                              lut4_parts[:, bass.ds(g, 1)].rearrange("p a k c -> p (a k c)"), start=True, stop=True)
                if i % 2 == 1:
                    last.then_inc(s_wl, 1)
                pe.wait_ge(s_prod, g + 1)
                if i == 0:
                    pe.wait_ge(s_wrows, r + 1)
                for h in range(HALVES):
                    last = mm(bank[6], place[:, P - G8 - G8 * i:2 * P - G8 - G8 * i], prod[i % 2][:, h],
                              start=(i == 0 and h == 0), stop=(i == BLOCK - 1 and h == HALVES - 1))
                if i == BLOCK - 1:
                    last.then_inc(s_wblock, 1)

            pe.wait_ge(s_match, 2)
            match_high(0, 0, 0)
            match_low(0, 0, 0)
            match_high(1, 0, 1)
            look_up(0, 0, 0)
            match_low(1, 0, 1)
            pe.wait_ge(s_ye, ET)
            pe.wait_ge(s_place, 1)
            with pe.Fori(0, NBLOCK - 1) as r:
                for i in range(BLOCK):
                    step(r, i)
            for i in range(BLOCK):
                step(NBLOCK - 1, i)
            pe.wait_ge(s_wrows, NBLOCK + 1)
            for j in range(LT):
                for r in range(NBLOCK):
                    last = nc.tensor.transpose(bank[5 - j][:, P * r:P * r + P], w_rows[:, r, P * j:P * j + P], ident)
                last.then_inc(s_wTp, 1)

            def linear_in(t):
                pe.wait_ge(s_comb, TOPK * (t + 1))
                if t >= 2:
                    pe.wait_ge(s_aT, t - 1)
                for j in range(LT):
                    last = mm(bank[t % 2][:, P * j:P * j + P], x_rows[:, t, P * j:P * j + P], bd[:, t], start=True, stop=True)
                last.then_inc(s_amm, 1)

            linear_in(0)
            for t in range(TT):
                if t + 1 < TT:
                    linear_in(t + 1)
                pe.wait_ge(s_aTlo, t + 1)
                if t >= 2:
                    pe.wait_ge(s_ylc, t - 1)
                    pe.wait_ge(s_ysel, t - 1)
                for b, w, ready in ((6, wTl, 1), (3, wTh, 1 + LT)):
                    pe.wait_ge(s_wlo, ready)
                    terms = [(j, ha, hw) for j in range(LT) for ha, hw in ((1, 0), (0, 1), (0, 0))]
                    for n, (j, ha, hw) in enumerate(terms):
                        last = mm(bank[b + t % 2], aT_halves[t % 2][:, ha, j], w[:, hw, j],
                                  start=(n == 0), stop=(n == len(terms) - 1))
                    last.then_inc(s_ymm, 1)
                    if b == 6:
                        pe.wait_ge(s_sq, t + 1)
                        if t == 0:
                            pe.wait_ge(s_wlo, 2)
                        else:
                            pe.wait_ge(s_high, t)
                        for j in range(LT):
                            last = mm(bank[5][:, 0:1], sq[t % 2][:, j], ones[:, 0:1], start=(j == 0), stop=(j == LT - 1))
                        last.then_inc(s_norm, 1)


def conv_weights(w):
    out = np.zeros((S, C, 3, S, C), w.dtype)
    pad, per = TAPS // 2, C // GROUPS
    for o in range(C):
        g = o // per
        for j in range(S):
            for k in range(TAPS):
                rel = j + k - pad
                out[rel % S, g * per:(g + 1) * per, rel // S + 1, j, o] = w[o, :, k]
    return out.reshape(P, 3, P)


def packed(table, parts, dtype=np.float32):
    at, width = spans(table)
    out = np.zeros((P, width), dtype)
    for name, a in parts.items():
        a = a.reshape(a.shape[0], -1)
        out[:a.shape[0], at[name].start:at[name].start + a.shape[1]] = a
    return out


def constants():
    p = np.arange(P)
    bits = lambda x, k: x >> k & 1
    match = np.zeros((2, P, 2, P), np.float32)
    for half in range(2):
        for plane in range(4):
            for par in range(2):
                for o in range(G8):
                    row = (4 * half + plane) * OI + par * G8 + o
                    match[half, row, par, 16 * o:16 * o + 16] = np.where(bits(np.arange(16), plane), 0.5, -0.5)
    ksel = np.zeros((KE, KT, KE // KT, C), np.float32)
    for k in range(KE):
        ksel[k, k // (KE // KT), k % (KE // KT)] = 1
    ones = np.array([bin(x).count("1") for x in range(16)])
    return packed(CONST, {
        "ident": np.eye(P), "iota": np.tile(p, (P, 1)), "rev": np.tile(E - np.arange(E), (P, 1)),
        "thr": np.tile(P * np.arange(TT), (P, 1)), "tri": np.tile(np.tri(E, k=-1).reshape(-1), (P, 1)),
        "blk": p[:, None] // C == np.arange(NT), "dmask": p[:, None] % C == np.arange(C), "pidx": p[:, None],
        "tbase": np.tile(P * np.arange(TT), (P, 1)), "ksel": ksel, "upper": p[:, None] < p,
        "mlo": match[0], "mhi": match[1], "mbias": 1 - ones[p % 16][:, None], "ones8": p[:, None] // 16 == np.arange(G8)})


def layout(i):
    a = {k: np.ascontiguousarray(v) for k, v in i.items()}
    rep = lambda v, n=P: np.broadcast_to(v, (n,) + v.shape)
    x4 = np.zeros((S, C, N, NB + 2), a["x"].dtype)
    x4[..., 1:NB + 1] = a["x"].reshape(N, C, NB, S).transpose(3, 1, 0, 2)
    blocks = lambda w: w.reshape(w.shape[:-2] + (NB, S, w.shape[-1]))
    ew12 = np.concatenate([blocks(a["L0_ffn_ew1"]), blocks(a["L0_ffn_ew2"])], -1)
    sw12 = np.concatenate([blocks(a["L0_ffn_sw1"]), blocks(a["L0_ffn_sw2"])], -1)
    q = a["L1_ffn_qweight"]
    lut8 = np.zeros((NG, G8, 16, G8, 16), a["L1_ffn_lut8"].dtype)
    lut4 = np.zeros((G8, 16, NG, G8), a["L1_ffn_lut4"].dtype)
    l8 = a["L1_ffn_lut8"].reshape(NG, G8, 16, 16)
    l4 = a["L1_ffn_lut4"].reshape(NG, G8, 16)
    for o in range(G8):
        lut8[:, o, :, o, :] = l8[:, o]
        lut4[o, :, :, o] = l4[:, o].T
    small = packed(SMALL, {
        "cT": a["cond_128"].T, "cwT": a["L0_cond_c_weight"].T, "W0": a["L1_cond_W0"], "W1": a["L1_cond_W1"],
        "W2": a["L1_cond_W2"], "b0": a["L1_cond_b0"][:, None], "b1": a["L1_cond_b1"][:, None],
        "sb1": a["L0_ffn_sb1"].reshape(MC, P).T, "sb2": a["L0_ffn_sb2"].reshape(MC, P).T,
        "wk": a["L1_cond_weight"][..., 0].reshape(KT, KE // KT, C, C).transpose(1, 3, 0, 2).reshape(P, KT, C),
        "rw": blocks(a["L0_ffn_router_w"]), "convb": rep(a["fside_S_0"], N), "b2": rep(a["L1_cond_b2"], N),
        "bk": a["L1_cond_bias_k"], "rb": rep(a["L0_ffn_router_b"]), "rbias": rep(a["L0_ffn_router_bias"])})
    return {
        "small": small, "const": constants(), "x4": x4.reshape(P, N, NB + 2), "wconv": conv_weights(a["L0_cond_weight"]),
        "x_rows": a["x"].reshape(TT, P, L).transpose(1, 0, 2), "w12": ew12.transpose(1, 0, 2, 3),
        "w3": a["L0_ffn_ew3"].transpose(1, 0, 2), "sw12": sw12, "sw3": a["L0_ffn_sw3"].reshape(MC, P, L).transpose(1, 0, 2),
        "b3x": np.concatenate([a["L0_ffn_eb3"], a["L0_ffn_sb3"][None]]),
        "b12": np.concatenate([a["L0_ffn_eb1"], a["L0_ffn_eb2"]], -1),
        "q": q.reshape(8, QT, OI, L // 32).transpose(0, 2, 1, 3).reshape(P, QT, L // 32),
        "lut8": lut8.reshape(QT, 2, P, P).transpose(0, 2, 1, 3), "lut4": lut4.reshape(P, NG, G8), "ybias": a["L1_ffn_bias"],
    }


def kernel(**inputs):
    import concourse.bacc as bacc
    from concourse.bass_utils import run_bass_kernel_spmd

    nc = bacc.Bacc("TRN2", target_bir_lowering=False, num_devices=1)
    arrays, A = {}, {}
    for name, a in layout(inputs).items():
        a = np.ascontiguousarray(a)
        arrays[f"in_{name}"] = a
        A[name] = nc.dram_tensor(f"in_{name}", a.shape, mybir.dt.from_np(a.dtype), kind="ExternalInput").ap()
    A["out"] = nc.dram_tensor("out", (T, L), F32, kind="ExternalOutput").ap()
    build(nc, A)
    r = run_bass_kernel_spmd(nc, [arrays], core_ids=[0])
    return r.results[0]["out"].reshape(N, C, L)
```

```python
from contextlib import ExitStack

import numpy as np

import concourse.bass as bass
from concourse import mybir

F32 = mybir.dt.float32
BF16 = mybir.dt.bfloat16
F32R = mybir.dt.float32r
I32 = mybir.dt.int32
U8 = mybir.dt.uint8
F8 = mybir.dt.float8e4
ALU = mybir.AluOpType
ACT = mybir.ActivationFunctionType
X = mybir.AxisListType.X

P = 128
N, C, L = 32, 32, 512
T = N * C
TT = T // P
NT = P // C
TAPS, GROUPS = 9, 4
S = 4
NB = L // S
D = 128
E, INTER, TOPK = 16, 128, 2
EG = 4
MC = 2
KE = 8
KT = KE * C // P
ET = TOPK * T // P + E - 1
TILE_LOOPS = (ET - 1) // 4 - 1
O = 512
OI = P // 8
QT = O // OI
G8 = 8
NG = O // G8
BITS_LOOP = (QT - 1) // TILE_LOOPS
BITS_FIRST = QT - BITS_LOOP * TILE_LOOPS
PARTS = 3
HALVES = 2
BLOCK = P // G8
NBLOCK = NG // BLOCK
LT = L // P
BIG = 3.0e38
EST_SQ = 64.0 ** 2 + 2.0 ** -11

SMALL = [("cT", N), ("cwT", C), ("W0", D), ("W1", D), ("W2", KE), ("b0", 1), ("b1", 1), ("sb1", MC), ("sb2", MC),
         ("wk", KT * C), ("rw", S * E), ("convb", C), ("b2", KE), ("bk", C), ("rb", E), ("rbias", E)]
CONST = [("ident", P), ("iota", P), ("rev", E), ("thr", TT), ("tri", E * E), ("blk", NT), ("dmask", C), ("pidx", 1),
         ("tbase", TT), ("ksel", KT * P), ("upper", P), ("mhi", 2 * P), ("mlo", 2 * P), ("mbias", 1), ("ones8", G8)]


def spans(table):
    at, out = 0, {}
    for name, width in table:
        out[name] = slice(at, at + width)
        at += width
    return out, at


SM, SMALL_W = spans(SMALL)
CO, CONST_W = spans(CONST)


def bc(ap, axis, n):
    u = ap.unsqueeze(axis)
    shape = list(u.shape)
    shape[axis] = n
    return u.to_broadcast(shape)


class Region:

    def __init__(self, flat, at=0):
        self.flat, self.at = flat, at

    def __call__(self, shape, dt=F32):
        size = int(np.prod(shape[1:]))
        words = size * mybir.dt.size(dt) // 4
        ap = self.flat[0:shape[0], self.at:self.at + words]
        self.at += words
        assert self.at <= self.flat.shape[1]
        if dt != self.flat.dtype:
            ap = ap.bitcast(dt)
        names = " ".join(f"d{i}" for i in range(len(shape) - 1))
        return ap.rearrange(f"p ({names}) -> p {names}", **{f"d{i}": n for i, n in enumerate(shape[1:])})


def build(nc, A):
    with ExitStack() as ctx:
        def sb(name, shape, dt=F32):
            return ctx.enter_context(nc.sbuf_tensor(name, shape, dt))

        def sem(name):
            return ctx.enter_context(nc.semaphore(name))

        psum = ctx.enter_context(nc.psum_tensor("psum", [P, 8, 512], F32))
        bank = [psum[:, i] for i in range(8)]

        xc_rows = nc.dram_tensor("xc_rows", (T, L), F32, kind="Internal").ap()
        y_slots = nc.dram_tensor("y_slots", (ET * P, L), F32, kind="Internal").ap()

        small = sb("small", [P, SMALL_W])
        const = sb("const", [P, CONST_W])
        sm = {k: small[:, v] for k, v in SM.items()}
        co = {k: const[:, v] for k, v in CO.items()}
        ident = co["ident"]

        x_rows = sb("x_rows", [P, TT, L])
        x4 = sb("x4", [P, N, NB + 2])
        wconv = sb("wconv", [P, 3, P])
        xcT_at = nc.sbuf_base
        xcT = sb("xcT", [P, S, T])
        xc_stage = sb("xc_stage", [P, 2, L])
        diag = sb("diag", [P, N, C])
        ctxrep = sb("ctxrep", [P, T])
        ctxb = sb("ctxb", [N, C])
        ones = sb("ones", [P, P])
        ones_bf = sb("ones_bf", [P, P], BF16)
        upper_bf = sb("upper_bf", [P, P], BF16)
        h1T = sb("h1T", [D, N])
        h2T = sb("h2T", [D, N])
        att = sb("att", [N, KE])
        attw = sb("attw", [N, KE + 3])
        attT = sb("attT", [KE, N])
        aggb = sb("aggb", [N, C])
        aggbrep = sb("aggbrep", [P, T])
        bd = sb("bd", [P, TT, P])

        w12_at = nc.sbuf_base
        w12 = sb("w12", [P, E, S, 2 * INTER])
        w3 = sb("w3", [INTER, E, L])
        sw12_at = nc.sbuf_base
        sw12 = sb("sw12", [P, S, 4 * INTER])
        sw3 = sb("sw3", [P, MC, L])
        b3x = sb("b3x", [E + 1, L])
        hs = sb("hs", [P, MC, T])

        al = [Region(w3[:].rearrange("p e l -> p (e l)"), (E - 2) * L)([P, N, C]),
              Region(bd[:].rearrange("p t k -> p (t k)"))([P, N, C])]

        after_conv = Region(x4[:].rearrange("p n b -> p (n b)"))
        score = sb("score", [P, TT, E])
        ra = sb("ra", [P, TT, E])
        rbuf = sb("rbuf", [P, TT, E])
        rc = sb("rc", [P, TT, E])
        masked = sb("masked", [P, TT, E])
        pick = [sb(f"pick{c}", [P, TT, E]) for c in range(TOPK)]
        gpick = [sb(f"gpick{c}", [P, TT, EG]) for c in range(TOPK)]
        gm = sb("gm", [P, TT, EG])
        gt1 = sb("gt1", [P, TT, EG])
        r1 = sb("r1", [P, TT])
        r2 = sb("r2", [P, TT])
        gate = sb("gate", [P, TOPK, TT])
        gate17 = sb("gate17", [P, TT, E + 1])
        gateT = diag[0:E + 1].rearrange("p n c -> p (n c)")
        sel_bf = sb("sel_bf", [P, TT, E], BF16)
        cntj = sb("cntj", [P, E, TT])
        ntile = sb("ntile", [P, E])
        tri_w = after_conv([P, E, E])
        tstart = sb("tstart", [P, E])
        tend = sb("tend", [P, E])
        slot_f = sb("slot_f", [P, TOPK, TT])
        slot_i = sb("slot_i", [P, TOPK, TT], I32)
        sq_i = sb("sq_i", [P, TOPK, TT], I32)
        sr_i = sb("sr_i", [P, TOPK, TT], I32)
        sq_f = sb("sq_f", [P, TOPK, TT])
        sr_f = sb("sr_f", [P, TOPK, TT])
        silu_s = after_conv([P, 2, 512])
        onehot_r = after_conv([P, TOPK, TT, P], BF16)
        onehot_q = after_conv([P, TOPK, TT, 32])
        tok_p = after_conv([P, TOPK, TT, 32], BF16)
        tok_t = after_conv([P, TOPK, TT, 32], BF16)
        tok_of_slot = sb("tok_of_slot", [P, 32], I32)
        eidw = after_conv([P, 32, E])
        eid_f = sb("eid_f", [P, 32])
        expert_of_tile = sb("expert_of_tile", [P, 32], I32)

        after_shared = Region(xcT[:].rearrange("p j t -> p (j t)"))
        spare = Region(hs[:].rearrange("p m t -> p (m t)"))
        yg = [spare([P, L]) for _ in range(4)]
        xg = [after_shared([P, L]) for _ in range(2)] + yg[2:]
        xgT = [after_shared([P, S, P]) for _ in range(2)]
        h12 = [after_shared([P, 2 * INTER]) for _ in range(2)]
        sil = [after_shared([P, INTER]) for _ in range(2)]
        hid = [after_shared([P, INTER]) for _ in range(2)]
        hidT = [after_shared([INTER, P]) for _ in range(2)]
        b12rep = [after_shared([P, 2 * INTER]) for _ in range(2)]
        y_sb = [xc_stage[:, i] for i in range(2)]

        after_ctx = Region(ctxrep[:])
        qw = after_ctx([P, QT, L // 32], I32)
        lut4 = after_ctx([P, NG, G8])
        bits = Region(x4[:].rearrange("p n b -> p (n b)"))([P, QT, L], U8)
        lut4_parts = Region(diag[:].rearrange("p n c -> p (n c)"))([P, NG, PARTS, G8], BF16)
        bits_now = [Region(sw3[:].rearrange("p m l -> p (m l)"), 4 * P + P * i)([P, L], U8) for i in range(2)]
        match = Region(wconv[:].rearrange("p d m -> p (d m)"))([P, 2, 2, P], BF16)
        rounded_words = HALVES * (2 * L + 2 * LT * P + 2 * LT * O) + 2 * P
        rounded_early = Region(nc.alloc_sbuf_tensor_at("rounded_early", [P, HALVES * 2 * 2 * P + 2 * L], F32R,
                                                       offset=sw12_at)[:])
        lut8 = [Region(sw3[:].rearrange("p m l -> p (m l)"), 2 * P * i)([P, 2, P]) for i in range(2)]
        lut8_halves = [rounded_early([P, HALVES, 2, P], F32R) for _ in range(2)]
        hot_hi = [rounded_early([P, L], F32R) for _ in range(2)]
        rounded = Region(nc.alloc_sbuf_tensor_at("rounded", [P, rounded_words], F32R, offset=w12_at)[:])
        place = rounded([P, 2 * P - G8], F32R)
        after_up = Region(w12[:].rearrange("p e j m -> p (e j m)"), rounded_words)
        hot_lo = [after_up([P, L], BF16) for _ in range(4)]
        rounded_late = Region(nc.alloc_sbuf_tensor_at("rounded_late", [P, 2 * HALVES * L], F32R, offset=xcT_at + 4 * LT * O)[:])
        prod = [region([P, HALVES, L], F32R) for region in (rounded, rounded, rounded_late, rounded_late)]
        wTh = rounded([P, HALVES, LT, O], F32R)
        wTl = rounded([P, HALVES, LT, O], F32R)
        after_down = Region(w3[:].rearrange("p e l -> p (e l)"))
        xb = after_down([P, TT, L])
        ybias = after_down([P, L])
        w_rows = after_down([P, NBLOCK, L])
        aT_halves = [rounded([P, HALVES, LT, P], F32R) for _ in range(2)]
        sq = [after_down([P, LT, P]) for _ in range(2)]
        sq_sum = [after_down([P, P]) for _ in range(2)]
        high = [after_down([P, 1], I32) for _ in range(2)]
        after_tiles = Region(xcT[:].rearrange("p j t -> p (j t)"))
        wTl_sum = after_tiles([P, LT, O])
        aT = [after_tiles([P, LT, P]) for _ in range(2)]
        ysel = [after_tiles([P, L]) for _ in range(2)]

        s_small = sem("small_loaded")
        s_const = sem("const_loaded")
        s_x4 = [sem(f"x4_loaded{i}") for i in range(4)]
        s_wconv = sem("wconv_loaded")
        s_xrows = sem("x_rows_loaded")
        s_shared = sem("shared_weights_loaded")
        s_b3 = sem("b3_loaded")
        s_w = sem("expert_weights_loaded")
        s_ones = sem("ones_ready")
        s_masks = sem("masks_ready")
        s_ctx = sem("ctx_summed")
        s_diag = sem("ctx_diag_ready")
        s_ctxrep_mm = sem("ctx_spread")
        s_ctxrep = sem("ctx_on_all_partitions")
        s_h1 = sem("att_h1_summed")
        s_h1T = sem("att_h1_ready")
        s_h2 = sem("att_h2_summed")
        s_h2T = sem("att_h2_ready")
        s_attl = sem("att_logits_summed")
        s_attm = sem("att_logits_shifted")
        s_attex = sem("att_exp_ready")
        s_att = sem("att_ready")
        s_attTp = sem("att_turned")
        s_attT = sem("attT_ready")
        s_attrep = sem("att_spread")
        s_al = sem("att_mix_ready")
        s_agg = sem("agg_summed")
        s_aggb = sem("agg_bias_spread")
        s_aggbrep = sem("aggb_on_all_partitions")
        s_bd = sem("block_diagonal_ready")
        s_conv = sem("conv_summed")
        s_xcT = sem("conv_ready")
        s_turn = sem("conv_turned")
        s_stage = sem("conv_rows_staged")
        s_xcw = [sem(f"conv_rows_written{i}") for i in range(2)]
        s_logit = sem("router_logits_summed")
        s_rm = sem("router_logits_shifted")
        s_rexp = sem("router_exp_ready")
        s_sel = sem("chosen_ready")
        s_gate = sem("gates_ready")
        s_rank = sem("ranks_summed")
        s_hots = sem("slot_onehots_ready")
        s_toks = sem("slot_tokens_summed")
        s_route = sem("routing_ready")
        s_gTp = sem("gates_turned")
        s_gT = sem("gateT_ready")
        s_sup = sem("shared_up_summed")
        s_silu = sem("shared_silu_ready")
        s_hs = sem("shared_hidden_ready")
        s_z = sem("shared_out_summed")
        s_zadd = sem("shared_out_added")
        s_gather = [sem(f"rows_gathered{i}") for i in range(4)]
        s_xTp = sem("rows_turned")
        s_xTe = sem("rows_turned_copied")
        s_b12 = [sem(f"expert_bias_loaded{i}") for i in range(2)]
        s_up = sem("expert_up_summed")
        s_hb = sem("expert_bias_added")
        s_hsilu = sem("expert_silu_ready")
        s_hg = sem("expert_hidden_ready")
        s_hTp = sem("expert_hidden_turned")
        s_hTe = sem("expert_hidden_turned_copied")
        s_down = sem("expert_down_summed")
        s_ye = sem("expert_out_copied")
        s_yw = [sem(f"expert_out_written{i}") for i in range(2)]
        s_back = [sem(f"out_rows_gathered{i}") for i in range(4)]
        s_comb = sem("out_rows_added")
        s_q = sem("packed_bits_loaded")
        s_l4 = sem("lut4_loaded")
        s_l4p = sem("lut4_split")
        s_match = sem("match_weights_ready")
        s_bits = sem("bit_chunks_ready")
        s_lut8 = [sem(f"lut8_loaded{i}") for i in range(2)]
        s_l8hi = sem("table_rounded")
        s_l8 = sem("table_halves_ready")
        s_place = sem("placing_ones_ready")
        s_now = [sem(f"bits_moved{i}") for i in range(2)]
        s_mh = sem("high_nibbles_matched")
        s_ml = sem("low_nibbles_matched")
        s_hi = sem("high_onehot_ready")
        s_lo = sem("low_onehot_ready")
        s_G = sem("table_rows_summed")
        s_prod = sem("values_chosen")
        s_wblock = sem("weight_rows_summed")
        s_wrows = sem("weight_rows_bank_free")
        s_wl = sem("low_weights_summed")
        s_wlfree = sem("low_weights_bank_free")
        s_wTp = sem("weights_turned")
        s_whi = sem("weights_rounded")
        s_wlo = sem("weight_rests_ready")
        s_aThi = sem("linear_input_rounded")
        s_aTlo = sem("linear_input_rest_ready")
        s_ybias = sem("ybias_loaded")
        s_pool = sem("pool_chain")
        s_xb = sem("residual_bias_ready")
        s_amm = sem("linear_input_summed")
        s_aT = sem("linear_input_ready")
        s_sq = sem("squares_ready")
        s_sqsum = sem("squares_added")
        s_norm = sem("norms_summed")
        s_high = sem("precision_chosen")
        s_ymm = sem("linear_summed")
        s_ylc = sem("low_result_copied")
        s_ysel = sem("result_chosen")
        s_yout = sem("result_ready")
        s_out = [sem(f"result_written{i}") for i in range(2)]
        s_v = sem("vector_chain")

        def over_tiles(eng, step, last):
            for i in range(4):
                step(0, i)
            with eng.Fori(1, 1 + TILE_LOOPS) as u:
                for i in range(4):
                    step(u, i)
            for k in range(4 * (1 + TILE_LOOPS), last + 1):
                step(k // 4, k % 4)

        def turned_bank(j):
            return bank[3 + j if j < 3 else 2]

        def shared_bank(n):
            return (0, 2, 4, 0)[n]

        z_bank = [bank[6], bank[2], bank[3], bank[7]]

        block = ctx.enter_context(nc.Block())

        @block.sync
        def _(sp):
            sp.dma_start(small[:], A["small"]).then_inc(s_small, 16)
            sp.dma_start(wconv[:], A["wconv"]).then_inc(s_wconv, 16)
            for i in range(4):
                sp.dma_start(x4[:, 8 * i:8 * i + 8, :], A["x4"][:, 8 * i:8 * i + 8, :]).then_inc(s_x4[i], 16)
            sp.dma_start(sw12[:], A["sw12"]).then_inc(s_shared, 16)
            sp.dma_start(sw3[:], A["sw3"]).then_inc(s_shared, 16)
            sp.dma_start(b3x[:], A["b3x"]).then_inc(s_b3, 16)
            sp.dma_start(x_rows[:], A["x_rows"]).then_inc(s_xrows, 16)
            for e in range(0, E, 2):
                sp.wait_ge(s_stage, e // 2 + 1)
                sp.dma_start(w12[:, e:e + 2], A["w12"][:, e:e + 2]).then_inc(s_w, 16)
                if e == E - 2:
                    sp.wait_ge(s_agg, TT)
                sp.dma_start(w3[:, e:e + 2], A["w3"][:, e:e + 2]).then_inc(s_w, 16)
                if e == 8:
                    sp.wait_ge(s_xcT, TT)
                    sp.dma_start(qw, A["q"]).then_inc(s_q, 16)
                    sp.dma_start(lut4, A["lut4"]).then_inc(s_l4, 16)
            sp.wait_ge(s_route, 1)
            sp.wait_ge(s_sup, 2 * MC)

            def move_bits(u, par):
                t = 2 * u + par
                if not isinstance(t, int) or t >= 2:
                    sp.wait_ge(s_ml, 2 * t - 2)
                sp.dma_start(bits_now[par], bits[:, bass.ds(t, 1)].rearrange("p a i -> p (a i)")).then_inc(s_now[par], 16)

            def tables(u, par):
                t = 2 * u + par
                sp.wait_ge(s_l8, t - 1)
                sp.dma_start(lut8[par], A["lut8"][bass.ds(t, 1)].rearrange("a p g m -> p (a g) m")).then_inc(s_lut8[par], 16)

            def step(u, i):
                k, kk, par = 4 * u + i, 2 * u + i // 2, i % 2
                if not isinstance(k, int) or k < ET:
                    if not isinstance(k, int) or k >= 2:
                        sp.wait_ge(s_hb, k - 1)
                    e = sp.value_load(expert_of_tile[0:1, bass.ds(k, 1)], min_val=0, max_val=E - 1)
                    sp.dma_start(b12rep[par], A["b12"][bass.ds(e, 1), :].partition_broadcast(P)).then_inc(s_b12[par], 16)
                if not isinstance(k, int) or k >= 2:
                    sp.wait_ge(s_ye, k - 1)
                    sp.dma_start(y_slots[bass.ds((k - 2) * P, P), :], y_sb[par]).then_inc(s_yw[par], 16)
                if isinstance(k, int) and k == 2:
                    sp.wait_ge(s_bits, 1)
                    for t in range(2):
                        move_bits(0, t)

            over_tiles(sp, step, ET + 1)
            sp.wait_ge(s_down, ET)
            sp.dma_start(ybias, A["ybias"].partition_broadcast(P)).then_inc(s_ybias, 16)
            with sp.Fori(1, QT // 2) as u:
                for par in range(2):
                    tables(u, par)
                    move_bits(u, par)
            for t in range(TT):
                sp.wait_ge(s_yout, t + 1)
                sp.dma_start(A["out"][P * t:P * t + P, :], ysel[t % 2]).then_inc(s_out[t % 2], 16)
            for i in range(2):
                sp.wait_ge(s_out[i], 16 * TT // 2)

        @block.gpsimd
        def _(pool):
            nc.gpsimd.memset(ones[:], 1.0).then_inc(s_ones, 1)
            nc.gpsimd.memset(ones_bf[:], 1.0).then_inc(s_ones, 1)
            nc.gpsimd.memset(gate17[:], 1.0).then_inc(s_ones, 1)
            pool.wait_ge(s_const, 16)
            nc.gpsimd.tensor_copy(upper_bf[:], co["upper"]).then_inc(s_masks, 1)
            pool.wait_ge(s_route, 2)
            pool.wait_ge(s_sup, 2 * MC)
            for i in range(2):
                pool.wait_ge(s_xcw[i], 16 * TT // 2)
            for k in range(ET):
                if k == 2:
                    pool.wait_ge(s_z, TT)
                if k >= 4:
                    pool.wait_ge(s_xTp, k - 3)
                nc.gpsimd.indirect_dma_start(xg[k % 4], None, xc_rows,
                                             bass.IndirectOffsetOnAxis(tok_of_slot[:, k:k + 1], 0)).then_inc(s_gather[k % 4], 16)
            pool.wait_ge(s_yw[0], 16 * ((ET + 1) // 2))
            pool.wait_ge(s_yw[1], 16 * (ET // 2))
            pool.wait_ge(s_down, ET)
            pool.wait_ge(s_zadd, TT)
            pool.wait_ge(s_ybias, 16)
            chain = 0

            def gather_back(n):
                t, c = n // TOPK, n % TOPK
                nc.gpsimd.indirect_dma_start(yg[n % 4], None, y_slots,
                                             bass.IndirectOffsetOnAxis(slot_i[:, c, t:t + 1], 0)).then_inc(s_back[n % 4], 16)

            for n in range(4):
                gather_back(n)
            for t in range(TT):
                for c in range(TOPK):
                    n = TOPK * t + c
                    pool.wait_ge(s_back[n % 4], 16 * (n // 4 + 1))
                    nc.gpsimd.tensor_scalar(yg[n % 4], yg[n % 4], gate[:, c, t:t + 1], None, ALU.mult).then_inc(s_pool, 1)
                    chain += 1
                    pool.wait_ge(s_pool, chain)
                    if n >= 1:
                        pool.wait_ge(s_comb, n)
                    nc.gpsimd.tensor_tensor(x_rows[:, t], x_rows[:, t], yg[n % 4], ALU.add).then_inc(s_comb, 1)
                    if n + 4 < TOPK * TT:
                        pool.wait_ge(s_comb, n + 1)
                        gather_back(n + 4)
                pool.wait_ge(s_comb, TOPK * (t + 1))
                nc.gpsimd.tensor_tensor(xb[:, t], x_rows[:, t], ybias, ALU.add).then_inc(s_xb, 1)

        @block.scalar
        def _(act):
            act.dma_start(const[:], A["const"]).then_inc(s_const, 16)
            act.wait_ge(s_small, 16)
            act.wait_ge(s_h1, 1)
            nc.scalar.activation(h1T[:], bank[6][:, 0:N], ACT.Gelu, bias=sm["b0"]).then_inc(s_h1T, 1)
            act.wait_ge(s_h2, 1)
            nc.scalar.activation(h2T[:], bank[6][:, 0:N], ACT.Gelu, bias=sm["b1"]).then_inc(s_h2T, 1)
            for h in range(2):
                act.wait_ge(s_ctxrep_mm, h + 1)
                nc.scalar.activation(ctxrep[:, 512 * h:512 * h + 512], bank[4 + 3 * h], ACT.Copy).then_inc(s_ctxrep, 1)

            def stage_rows(t):
                act.wait_ge(s_turn, t + 1)
                if t >= 2:
                    act.wait_ge(s_xcw[t % 2], 16 * (t // 2))
                nc.scalar.activation(xc_stage[:, t % 2], bank[2 + t % 2], ACT.Copy).then_inc(s_stage, 1)
                act.wait_ge(s_stage, t + 1)
                act.dma_start(xc_rows[P * t:P * t + P, :], xc_stage[:, t % 2]).then_inc(s_xcw[t % 2], 16)

            for t in range(TT):
                stage_rows(t)
                if t == 3:
                    act.wait_ge(s_attm, 1)
                    nc.scalar.activation(att[:], attw[:, 0:KE], ACT.Exp, accum_out=attw[:, KE + 1:KE + 2]).then_inc(s_attex, 1)
                if t == 4:
                    act.wait_ge(s_attTp, 1)
                    nc.scalar.activation(attT[:], bank[6][0:KE, 0:N], ACT.Copy).then_inc(s_attT, 1)
                if t == 6:
                    for h in range(2):
                        act.wait_ge(s_aggb, h + 1)
                        nc.scalar.activation(aggbrep[:, 512 * h:512 * h + 512], bank[6 + h], ACT.Copy).then_inc(s_aggbrep, 1)
            act.wait_ge(s_rm, 1)
            nc.scalar.activation(ra[:], rbuf[:], ACT.Exp).then_inc(s_rexp, 1)

            def shared_silu(n):
                act.wait_ge(s_sup, n + 1)
                if n >= 2:
                    act.wait_ge(s_hs, n - 1)
                nc.scalar.activation(silu_s[:, n % 2], bank[shared_bank(n)], ACT.Silu,
                                     bias=sm["sb1"][:, n % MC:n % MC + 1]).then_inc(s_silu, 1)

            for n in range(2 * MC):
                shared_silu(n)
            for h in range(2):
                act.wait_ge(s_gTp, h + 1)
                nc.scalar.activation(gateT[:, 512 * h:512 * h + 512], bank[2 + h][0:E + 1, :], ACT.Copy).then_inc(s_gT, 1)

            def turned_rows(kk, par):
                k = 2 * kk + par
                act.wait_ge(s_xTp, k + 1)
                if not isinstance(k, int) or k >= 2:
                    act.wait_ge(s_up, k - 1)
                nc.scalar.activation(xgT[par].rearrange("p j t -> p (j t)"), bank[par], ACT.Copy).then_inc(s_xTe, 1)

            def round_table(u, par):
                act.wait_ge(s_lut8[par], 16 * (u + 1))
                nc.scalar.activation(lut8_halves[par][:, 0], lut8[par], ACT.Copy).then_inc(s_l8hi, 1)

            def step(u, i):
                k, kk, par = 4 * u + i, 2 * u + i // 2, i % 2
                if not isinstance(k, int) or k + 1 < ET:
                    turned_rows(kk + par, 1 - par)
                if not isinstance(k, int) or k >= 2:
                    act.wait_ge(s_down, k - 1)
                    if not isinstance(k, int) or k >= 4:
                        act.wait_ge(s_yw[par], 16 * (kk - 1))
                    nc.scalar.activation(y_sb[par], bank[5 + par], ACT.Copy).then_inc(s_ye, 1)
                if not isinstance(k, int) or k < ET:
                    act.wait_ge(s_hb, k + 1)
                    if not isinstance(k, int) or k >= 2:
                        act.wait_ge(s_hg, k - 1)
                    nc.scalar.activation(sil[par], h12[par][:, 0:INTER], ACT.Silu).then_inc(s_hsilu, 1)
                if isinstance(k, int) and k == 3:
                    round_table(0, 0)
                    round_table(0, 1)

            act.wait_ge(s_z, TT)
            for t in range(2):
                act.dma_start(lut8[t], A["lut8"][t]).then_inc(s_lut8[t], 16)
            turned_rows(0, 0)
            over_tiles(act, step, ET)

            def make_onehots(r, i):
                g = BLOCK * r + i
                act.wait_ge(s_mh, g + 1)
                nc.scalar.activation(hot_hi[i % 2], bank[0], ACT.Relu, bias=co["mbias"]).then_inc(s_hi, 1)
                act.wait_ge(s_ml, g + 1)
                nc.scalar.activation(hot_lo[i % 4], bank[1], ACT.Relu, bias=co["mbias"]).then_inc(s_lo, 1)
                if i % 2 == 1 and (not isinstance(g, int) or 3 <= g < NG - 1):
                    round_table(BLOCK // 4 * r + (i + 1) // 4, (i + 1) // 2 % 2)

            def copy_rows(r):
                act.wait_ge(s_wblock, r + 1)
                nc.scalar.activation(w_rows[:, bass.ds(r, 1)].rearrange("p a l -> p (a l)"), bank[6],
                                     ACT.Copy).then_inc(s_wrows, 1)

            act.wait_ge(s_up, ET)
            make_onehots(0, 0)
            step((ET + 1) // 4, (ET + 1) % 4)
            make_onehots(0, 1)
            make_onehots(0, 2)
            with act.Fori(0, NBLOCK - 1) as r:
                for i in range(3, BLOCK + 3):
                    make_onehots(r, i)
                copy_rows(r)
            for i in range(3, BLOCK):
                make_onehots(NBLOCK - 1, i)
            copy_rows(NBLOCK - 1)

            def round_input(t):
                act.wait_ge(s_aT, t + 1)
                if t >= 2:
                    act.wait_ge(s_ymm, 2 * t - 2)
                nc.scalar.activation(aT_halves[t % 2][:, 0], aT[t % 2], ACT.Copy).then_inc(s_aThi, 1)

            round_input(0)
            act.wait_ge(s_wlfree, QT + 1)
            for j in range(LT):
                nc.scalar.activation(wTl[:, 0, j], wTl_sum[:, j], ACT.Copy).then_inc(s_whi, 1)
            for j in range(LT):
                act.wait_ge(s_wTp, j + 1)
                nc.scalar.activation(wTh[:, 0, j], turned_bank(j), ACT.Copy).then_inc(s_whi, 1)
            act.wait_ge(s_aT, 1)
            nc.scalar.activation(sq[0].rearrange("p j t -> p (j t)"), aT[0].rearrange("p j t -> p (j t)"),
                                 ACT.Square).then_inc(s_sq, 1)
            for t in range(TT):
                if t + 1 < TT:
                    round_input(t + 1)
                    if t >= 1:
                        act.wait_ge(s_sqsum, t)
                    nc.scalar.activation(sq[(t + 1) % 2].rearrange("p j t -> p (j t)"),
                                         aT[(t + 1) % 2].rearrange("p j t -> p (j t)"), ACT.Square).then_inc(s_sq, 1)
                act.wait_ge(s_ymm, 2 * t + 1)
                if t >= 2:
                    act.wait_ge(s_out[t % 2], 16 * (t // 2))
                nc.scalar.activation(ysel[t % 2], bank[6 + t % 2], ACT.Copy).then_inc(s_ylc, 1)

        @block.vector
        def _(dve):
            chain = [0]

            def link(ins):
                chain[0] += 1
                ins.then_inc(s_v, 1)
                dve.wait_ge(s_v, chain[0])

            v = nc.vector
            dve.wait_ge(s_small, 16)
            dve.wait_ge(s_const, 16)
            dve.wait_ge(s_ctx, 1)
            link(v.tensor_tensor(ctxb[:], bank[5][0:N, 0:C], sm["convb"][0:N], ALU.add))
            v.tensor_tensor(diag[0:N], bc(ctxb[:], 1, N), bc(ident[0:N, 0:N], 2, C), ALU.mult).then_inc(s_diag, 1)

            def conv_out(t):
                dve.wait_ge(s_conv, t + 1)
                if t == 0:
                    dve.wait_ge(s_ctxrep, 2)
                cr = ctxrep[:, P * t:P * t + P].rearrange("p (n c) -> p n c", n=NT)
                v.tensor_tensor(
                    xcT[:, :, P * t:P * t + P].rearrange("p j (n c) -> p n j c", n=NT),
                    bank[t % 2].rearrange("p (n j c) -> p n j c", n=NT, j=S),
                    bc(cr, 2, S), ALU.add).then_inc(s_xcT, 1)

            for t in range(4):
                conv_out(t)
            dve.wait_ge(s_attl, 1)
            link(v.tensor_tensor(attw[:, 0:KE], bank[5][0:N, 0:KE], sm["b2"][0:N], ALU.add))
            link(v.tensor_reduce(attw[:, KE:KE + 1], attw[:, 0:KE], X, ALU.max))
            v.tensor_scalar(attw[:, 0:KE], attw[:, 0:KE], attw[:, KE:KE + 1], None, ALU.subtract).then_inc(s_attm, 1)
            conv_out(4)
            dve.wait_ge(s_attex, 1)
            link(v.reciprocal(attw[:, KE + 2:KE + 3], attw[:, KE + 1:KE + 2]))
            v.tensor_scalar(att[:], att[:], attw[:, KE + 2:KE + 3], None, ALU.mult).then_inc(s_att, 1)
            conv_out(5)
            dve.wait_ge(s_attrep, 2)
            for k in range(KT):
                v.tensor_tensor(al[k], bc(bank[5][:, N * k:N * k + N], 2, C), bc(co["dmask"], 1, N),
                                ALU.mult).then_inc(s_al, 1)
            conv_out(6)
            link(v.tensor_copy(aggb[:], bank[6][0:N, 0:C]))
            v.tensor_tensor(diag[0:N], bc(aggb[:], 1, N), bc(ident[0:N, 0:N], 2, C), ALU.mult).then_inc(s_al, 1)
            conv_out(7)

            v.tensor_copy(match[:, 0].rearrange("p a m -> p (a m)"), co["mhi"]).then_inc(s_match, 1)
            v.tensor_copy(match[:, 1].rearrange("p a m -> p (a m)"), co["mlo"]).then_inc(s_match, 1)

            dve.wait_ge(s_logit, 1)
            link(v.tensor_tensor(score[:], bank[4][:, 0:TT * E].rearrange("p (t e) -> p t e", t=TT),
                                 bc(sm["rb"], 1, TT), ALU.add))
            link(v.tensor_reduce(r1[:], score[:], X, ALU.max))
            v.tensor_tensor(rbuf[:], score[:], bc(r1[:], 2, E), ALU.subtract).then_inc(s_rm, 1)

            dve.wait_ge(s_rexp, 1)
            link(v.tensor_reduce(r1[:], ra[:], X, ALU.add))
            link(v.reciprocal(r2[:], r1[:]))
            link(v.tensor_tensor(rbuf[:], ra[:], bc(r2[:], 2, E), ALU.mult))
            link(v.tensor_tensor(score[:], rbuf[:], bc(sm["rbias"], 1, TT), ALU.add))

            def first_max(out, m, n, a, b):
                link(v.tensor_reduce(r1[:], m, X, ALU.max))
                link(v.tensor_tensor(a, m, bc(r1[:], 2, n), ALU.is_equal))
                link(v.tensor_tensor(b, a, bc(co["rev"][:, 0:n], 1, TT), ALU.mult))
                link(v.tensor_reduce(r2[:], b, X, ALU.max))
                link(v.tensor_tensor(out, b, bc(r2[:], 2, n), ALU.is_equal))

            g4 = score[:].rearrange("p t (g k) -> p t g k", g=EG)
            link(v.tensor_reduce(gm[:], g4, X, ALU.max))
            first_max(gpick[0][:], gm[:], EG, ra[:, :, 0:EG], rc[:, :, 0:EG])
            link(v.scalar_tensor_tensor(gm[:], gpick[0][:], -BIG, gm[:], ALU.mult, ALU.add))
            first_max(gpick[1][:], gm[:], EG, ra[:, :, 0:EG], rc[:, :, 0:EG])
            link(v.tensor_tensor(gt1[:], gpick[0][:], gpick[1][:], ALU.add))
            link(v.tensor_scalar(gt1[:], gt1[:], BIG, -BIG, ALU.mult, ALU.add))
            link(v.tensor_tensor(masked[:].rearrange("p t (g k) -> p t g k", g=EG), g4, bc(gt1[:], 3, E // EG), ALU.add))
            first_max(pick[0][:], masked[:], E, ra[:], rc[:])
            link(v.scalar_tensor_tensor(masked[:], pick[0][:], -BIG, masked[:], ALU.mult, ALU.add))
            first_max(pick[1][:], masked[:], E, ra[:], rc[:])
            link(v.tensor_tensor(rbuf[:], pick[0][:], pick[1][:], ALU.add))
            v.tensor_copy(sel_bf[:], rbuf[:]).then_inc(s_sel, 1)
            dve.wait_ge(s_ones, 3)
            v.tensor_tensor(gate17[:, :, 0:E], rbuf[:], score[:], ALU.mult).then_inc(s_gate, 1)
            for c in range(TOPK):
                link(v.tensor_tensor(ra[:], pick[c][:], score[:], ALU.mult))
                link(v.tensor_reduce(gate[:, c], ra[:], X, ALU.add))

            def shared_hidden(n):
                half, m = n // MC, n % MC
                dve.wait_ge(s_silu, n + 1)
                v.scalar_tensor_tensor(hs[:, m, 512 * half:512 * half + 512], bank[shared_bank(n) + 1],
                                       sm["sb2"][:, m:m + 1], silu_s[:, n % 2], ALU.add, ALU.mult).then_inc(s_hs, 1)

            shared_hidden(0)
            shared_hidden(1)

            dve.wait_ge(s_rank, 2)
            link(v.tensor_tensor(cntj[:], bc(bank[7][:, TT * E:TT * E + E], 2, TT), bc(co["thr"], 1, E), ALU.is_gt))
            link(v.tensor_reduce(ntile[:], cntj[:], X, ALU.add))
            link(v.tensor_tensor(tri_w[:], bc(ntile[:], 1, E), co["tri"].rearrange("p (a b) -> p a b", a=E), ALU.mult))
            link(v.tensor_reduce(tstart[:], tri_w[:], X, ALU.add))
            link(v.tensor_tensor(tend[:], tstart[:], ntile[:], ALU.add))
            link(v.tensor_scalar(tstart[:], tstart[:], float(P), None, ALU.mult))
            link(v.tensor_tensor(ra[:], bank[7][:, 0:TT * E].rearrange("p (t e) -> p t e", t=TT),
                                 bc(tstart[:], 1, TT), ALU.add))
            for c in range(TOPK):
                link(v.tensor_tensor(rc[:], pick[c][:], ra[:], ALU.mult))
                link(v.tensor_reduce(slot_f[:, c], rc[:], X, ALU.add))
            link(v.tensor_copy(slot_i[:], slot_f[:]))
            link(v.tensor_scalar(sq_i[:], slot_i[:], 7, None, ALU.logical_shift_right))
            link(v.tensor_scalar(sr_i[:], slot_i[:], P - 1, None, ALU.bitwise_and))
            link(v.tensor_copy(sq_f[:], sq_i[:]))
            link(v.tensor_copy(sr_f[:], sr_i[:]))
            for c in range(TOPK):
                link(v.tensor_tensor(onehot_r[:, c], bc(co["iota"], 1, TT), bc(sr_f[:, c], 2, P), ALU.is_equal))
                link(v.tensor_tensor(onehot_q[:, c], bc(co["iota"][:, 0:32], 1, TT), bc(sq_f[:, c], 2, 32), ALU.is_equal))
                v.tensor_scalar(tok_p[:, c], onehot_q[:, c], co["pidx"], None, ALU.mult).then_inc(s_hots, 1)
                v.tensor_tensor(tok_t[:, c], onehot_q[:, c], bc(co["tbase"], 2, 32), ALU.mult).then_inc(s_hots, 1)
            link(v.tensor_tensor(eidw[:], bc(tend[:], 1, 32), bc(co["iota"][:, 0:32], 2, E), ALU.is_le))
            link(v.tensor_reduce(eid_f[:], eidw[:], X, ALU.add))
            v.tensor_scalar(expert_of_tile[:], eid_f[:], float(E - 1), None, ALU.min).then_inc(s_route, 1)
            dve.wait_ge(s_agg, TT)
            for t in range(TT):
                last = v.tensor_tensor(bd[:, t].rearrange("p (n c) -> p n c", n=NT),
                                       bc(bank[6][:, C * t:C * t + C], 1, NT), bc(co["blk"], 2, C), ALU.mult)
            last.then_inc(s_bd, 1)
            shared_hidden(2)
            shared_hidden(3)
            dve.wait_ge(s_toks, 1)
            v.tensor_copy(tok_of_slot[:], bank[7][:, 0:32]).then_inc(s_route, 1)

            def make_bit(t, tiles, n):
                move = (6 - n % 8, ALU.logical_shift_left) if n % 8 < 7 else (1, ALU.logical_shift_right)
                packed_bytes = qw[:, bass.ds(t, tiles)].rearrange("p t w -> p (t w)").bitcast(U8)
                packed_bytes = packed_bytes.rearrange("p (w b) -> p w b", b=4)
                out = bits[:, bass.ds(t, tiles)].rearrange("p t (w s) -> p (t w) s", s=32)
                ins = v.tensor_scalar(out[:, :, n], packed_bytes[:, :, n // 8], move[0], 0x40, move[1], ALU.bitwise_and)
                if n == 31:
                    ins.then_inc(s_bits, 1)

            def split_lut4(k):
                ins = v.tensor_copy(lut4_parts[:, :, k], lut4)
                if k == PARTS - 1:
                    ins.then_inc(s_l4p, 1)
                else:
                    link(ins)
                    link(v.tensor_tensor(lut4, lut4, lut4_parts[:, :, k], ALU.subtract))

            dve.wait_ge(s_xrows, 16)
            for t in range(TT):
                if t >= 4:
                    dve.wait_ge(s_q, 16)
                    for n in range(8 * (t - 4), 8 * (t - 4) + 8):
                        make_bit(0, BITS_FIRST, n)
                dve.wait_ge(s_z, t + 1)
                v.tensor_tensor(x_rows[:, t], x_rows[:, t], z_bank[t % 4], ALU.add).then_inc(s_zadd, 1)

            def split_table(t, par):
                dve.wait_ge(s_l8hi, t + 1)
                v.tensor_tensor(lut8_halves[par][:, 1], lut8[par], lut8_halves[par][:, 0].bitcast(F32),
                                ALU.subtract).then_inc(s_l8, 1)

            def step(u, i):
                k, kk, par = 4 * u + i, 2 * u + i // 2, i % 2
                if not isinstance(k, int) or k >= 1:
                    dve.wait_ge(s_hTp, k)
                    if not isinstance(k, int) or k >= 3:
                        dve.wait_ge(s_down, k - 2)
                    v.tensor_copy(hidT[1 - par], bank[4][:, 0:P]).then_inc(s_hTe, 1)
                if not isinstance(k, int):
                    for n in range(8 * i, 8 * i + 4):
                        make_bit(BITS_LOOP * u + BITS_FIRST - BITS_LOOP, BITS_LOOP, n)
                if not isinstance(k, int) or k < ET:
                    dve.wait_ge(s_up, k + 1)
                    dve.wait_ge(s_b12[par], 16 * (kk + 1))
                    if not isinstance(k, int) or k >= 2:
                        dve.wait_ge(s_hg, k - 1)
                    v.tensor_tensor(h12[par], bank[2 + par][:, 0:2 * INTER], b12rep[par], ALU.add).then_inc(s_hb, 1)
                    dve.wait_ge(s_hsilu, k + 1)
                    v.tensor_tensor(hid[par], sil[par], h12[par][:, INTER:2 * INTER], ALU.mult).then_inc(s_hg, 1)
                if not isinstance(k, int):
                    for n in range(8 * i + 4, 8 * i + 8):
                        make_bit(BITS_LOOP * u + BITS_FIRST - BITS_LOOP, BITS_LOOP, n)
                elif 1 <= k <= PARTS:
                    dve.wait_ge(s_l4, 16)
                    split_lut4(k - 1)
                elif k == ET - 3:
                    split_table(0, 0)
                    split_table(1, 1)

            over_tiles(dve, step, ET)

            link(v.tensor_scalar(place, co["pidx"].to_broadcast([P, 2 * P - G8]), 0.0, None, ALU.mult))
            v.tensor_copy(place[:, P - G8:P], co["ones8"]).then_inc(s_place, 1)

            def copy_weights(t):
                dve.wait_ge(s_wl, t + 1)
                v.tensor_reduce(wTl_sum[:, :, bass.ds(OI * t, OI)].rearrange("p i (g c) -> p i g c", g=2),
                                bank[7][:, 0:LT * 2 * PARTS * G8].rearrange("p (i g k c) -> p i g c k", g=2, k=PARTS, c=G8),
                                X, ALU.add).then_inc(s_wlfree, 1)

            def step(r, i):
                g = BLOCK * r + i
                t = BLOCK // 2 * r + i // 2
                dve.wait_ge(s_G, g + 1)
                v.tensor_tensor(prod[i % 4], bc(hot_lo[i % 4], 1, HALVES), psum[:, 2 + 2 * (i % 2):4 + 2 * (i % 2)],
                                ALU.mult).then_inc(s_prod, 1)
                if i % 2 == 0 and (not isinstance(g, int) or g >= 1):
                    copy_weights(t - 1)
                    if not isinstance(g, int) or t + 1 < QT:
                        split_table(t + 1, (i // 2 + 1) % 2)

            v.memset(r1[:], 0.0).then_inc(s_wrows, 1)
            v.memset(r2[:], 0.0).then_inc(s_wlfree, 1)
            step(0, 0)
            with dve.Fori(0, NBLOCK - 1) as r:
                for i in range(1, BLOCK + 1):
                    step(r, i)
            for i in range(1, BLOCK):
                step(NBLOCK - 1, i)
            copy_weights(QT - 1)

            def linear_in(t):
                dve.wait_ge(s_amm, t + 1)
                if t >= 2:
                    dve.wait_ge(s_aTlo, t - 1)
                    dve.wait_ge(s_sq, t - 1)
                v.tensor_tensor(aT[t % 2], bank[t % 2].rearrange("p (j k) -> p j k", j=LT),
                                bc(aggbrep[:, P * t:P * t + P], 1, LT), ALU.add).then_inc(s_aT, 1)
                dve.wait_ge(s_aThi, t + 1)
                v.tensor_tensor(aT_halves[t % 2][:, 1], aT[t % 2], aT_halves[t % 2][:, 0].bitcast(F32),
                                ALU.subtract).then_inc(s_aTlo, 1)

            def add_squares(t):
                dve.wait_ge(s_sq, t + 1)
                if t >= 2:
                    dve.wait_ge(s_norm, t - 1)
                v.tensor_reduce(sq_sum[t % 2], sq[t % 2].rearrange("p j t -> p t j"), X, ALU.add).then_inc(s_sqsum, 1)

            linear_in(0)
            for j in range(LT):
                dve.wait_ge(s_whi, j + 1)
                v.tensor_tensor(wTl[:, 1, j], wTl_sum[:, j], wTl[:, 0, j].bitcast(F32), ALU.subtract).then_inc(s_wlo, 1)
            for j in range(LT):
                dve.wait_ge(s_whi, LT + j + 1)
                v.tensor_tensor(wTh[:, 1, j], turned_bank(j), wTh[:, 0, j].bitcast(F32), ALU.subtract).then_inc(s_wlo, 1)
            add_squares(0)
            for t in range(TT):
                if t + 1 < TT:
                    linear_in(t + 1)
                    add_squares(t + 1)
                dve.wait_ge(s_norm, t + 1)
                v.tensor_scalar(high[t % 2], bank[5][:, 0:1], EST_SQ, None, ALU.is_gt).then_inc(s_high, 1)
                dve.wait_ge(s_ylc, t + 1)
                dve.wait_ge(s_ymm, 2 * t + 2)
                dve.wait_ge(s_high, t + 1)
                v.copy_predicated(ysel[t % 2], high[t % 2].to_broadcast([P, L]), bank[3 + t % 2]).then_inc(s_ysel, 1)
                dve.wait_ge(s_ysel, t + 1)
                dve.wait_ge(s_xb, t + 1)
                v.tensor_tensor(ysel[t % 2], ysel[t % 2], xb[:, t], ALU.add).then_inc(s_yout, 1)

        @block.tensor
        def _(pe):
            mm = nc.tensor.matmul
            pe.wait_ge(s_small, 16)
            mm(bank[5][0:N, 0:C], sm["cT"], sm["cwT"], start=True, stop=True).then_inc(s_ctx, 1)
            mm(bank[6][:, 0:N], sm["W0"], sm["cT"], start=True, stop=True).then_inc(s_h1, 1)
            pe.wait_ge(s_h1T, 1)
            mm(bank[6][:, 0:N], sm["W1"], h1T[:], start=True, stop=True).then_inc(s_h2, 1)
            pe.wait_ge(s_ones, 3)
            pe.wait_ge(s_diag, 1)
            for h in range(2):
                mm(bank[4 + 3 * h], ones[0:N, :], diag[0:N, 16 * h:16 * h + 16, :].rearrange("p n c -> p (n c)"),
                   start=True, stop=True).then_inc(s_ctxrep_mm, 1)
            pe.wait_ge(s_wconv, 16)

            def conv(t):
                pe.wait_ge(s_x4[t // 2], 16)
                if t >= 2:
                    pe.wait_ge(s_xcT, t - 1)
                for k in range(NT):
                    for d in range(3):
                        last = mm(bank[t % 2][:, P * k:P * k + P], x4[:, NT * t + k, d:d + NB], wconv[:, d],
                                  start=(d == 0), stop=(d == 2))
                last.then_inc(s_conv, 1)

            def turn(t):
                pe.wait_ge(s_xcT, t + 1)
                if t == 0:
                    pe.wait_ge(s_const, 16)
                    pe.wait_ge(s_ctxrep, 1)
                if t >= 2:
                    pe.wait_ge(s_stage, t - 1)
                for j in range(S):
                    last = nc.tensor.transpose(bank[2 + t % 2][:, P * j:P * j + P], xcT[:, j, P * t:P * t + P], ident)
                last.then_inc(s_turn, 1)
                for j in range(S):
                    last = mm(bank[4][:, E * t:E * t + E], xcT[:, j, P * t:P * t + P], sm["rw"][:, E * j:E * j + E],
                              start=(j == 0), stop=(j == S - 1))
                if t == TT - 1:
                    last.then_inc(s_logit, 1)

            def mixed(t):
                for k in range(KT):
                    last = mm(bank[6][:, C * t:C * t + C], al[k][:, NT * t:NT * t + NT, :].rearrange("p n i -> p (n i)"),
                              sm["wk"][:, C * k:C * k + C], start=(k == 0), stop=(k == KT - 1))
                last.then_inc(s_agg, 1)

            def spread_bias(h):
                mm(bank[6 + h], ones[0:N, :], diag[0:N, 16 * h:16 * h + 16, :].rearrange("p n c -> p (n c)"),
                   start=True, stop=True).then_inc(s_aggb, 1)

            for t in range(TT):
                conv(t)
                if t >= 1:
                    turn(t - 1)
                if t == 3:
                    pe.wait_ge(s_h2T, 1)
                    mm(bank[5][0:N, 0:KE], h2T[:], sm["W2"], start=True, stop=True).then_inc(s_attl, 1)
                if t == 5:
                    pe.wait_ge(s_att, 1)
                    nc.tensor.transpose(bank[6][0:KE, 0:N], att[:], ident[0:N, 0:N]).then_inc(s_attTp, 1)
                if t == 6:
                    pe.wait_ge(s_attT, 1)
                    for k in range(KT):
                        mm(bank[5][:, N * k:N * k + N], co["ksel"][0:KE, P * k:P * k + P], attT[:], start=True, stop=True)
                    last = mm(bank[6][0:N, 0:C], attT[:], sm["bk"][0:KE], start=True, stop=True)
                    last.then_inc(s_attrep, 2)

            pe.wait_ge(s_al, 3)
            spread_bias(0)
            spread_bias(1)
            turn(TT - 1)

            def shared_up(n):
                half, m = n // MC, n % MC
                if n == 0:
                    pe.wait_ge(s_shared, 32)
                if n == 1:
                    pe.wait_ge(s_stage, TT)
                if n == 3:
                    pe.wait_ge(s_hs, 1)
                for w in range(2):
                    for j in range(S):
                        t = 2 * (MC * n + w) + j // 2 - 2
                        if j % 2 == 0 and 0 <= t < TT:
                            if t == 0:
                                pe.wait_ge(s_aggbrep, 1)
                            mixed(t)
                        last = mm(bank[shared_bank(n) + w], sw12[:, j, 256 * w + P * m:256 * w + P * m + P],
                                  xcT[:, j, 512 * half:512 * half + 512], start=(j == 0), stop=(j == S - 1))
                last.then_inc(s_sup, 1)

            def shared_down(t):
                if t == 0:
                    pe.wait_ge(s_gT, 2)
                    pe.wait_ge(s_bd, 1)
                if t == 3:
                    pe.wait_ge(s_route, 2)
                if t >= 4:
                    pe.wait_ge(s_hs, 4)
                    pe.wait_ge(s_zadd, t - 3)
                for m in range(MC):
                    mm(z_bank[t % 4], hs[:, m, P * t:P * t + P], sw3[:, m], start=(m == 0), stop=False)
                mm(z_bank[t % 4], gateT[:, P * t:P * t + P], b3x[:], start=False, stop=True).then_inc(s_z, 1)

            shared_up(0)
            shared_up(1)
            pe.wait_ge(s_sel, 1)
            pe.wait_ge(s_masks, 1)
            pe.wait_ge(s_aggbrep, 2)
            sel = sel_bf[:].rearrange("p t e -> p (t e)")
            mm(bank[7][:, 0:TT * E], upper_bf[:], sel, start=True, stop=False)
            for t in range(1, TT):
                last = mm(bank[7][:, t * E:TT * E], ones_bf[:], sel[:, 0:(TT - t) * E], start=False, stop=(t == TT - 1))
            last.then_inc(s_rank, 1)
            for t in range(TT):
                last = mm(bank[7][:, TT * E:TT * E + E], ones_bf[:], sel[:, t * E:t * E + E], start=(t == 0), stop=(t == TT - 1))
            last.then_inc(s_rank, 1)
            shared_up(2)
            shared_up(3)
            pe.wait_ge(s_gate, 1)
            pe.wait_ge(s_hs, 2)
            for h in range(2):
                for t in range(4 * h, 4 * h + 4):
                    last = nc.tensor.transpose(bank[2 + h][0:E + 1, P * (t % 4):P * (t % 4) + P], gate17[:, t], ident)
                last.then_inc(s_gTp, 1)
            pe.wait_ge(s_hots, 4)
            n = 0
            for c in range(TOPK):
                for t in range(TT):
                    for part in (tok_p, tok_t):
                        last = mm(bank[7][:, 0:32], onehot_r[:, c, t], part[:, c, t],
                                  start=(n == 0), stop=(n == 2 * TOPK * TT - 1))
                        n += 1
            last.then_inc(s_toks, 1)
            pe.wait_ge(s_b3, 16)
            for t in range(TT):
                shared_down(t)

            pe.wait_ge(s_w, 16 * E)

            def turn_rows(u, i):
                k, par = 4 * u + i, i % 2
                pe.wait_ge(s_gather[i], 16 * (u + 1))
                if not isinstance(k, int) or k >= 2:
                    pe.wait_ge(s_xTe, k - 1)
                for j in range(S):
                    last = nc.tensor.transpose(bank[par][:, P * j:P * j + P], xg[i][:, P * j:P * j + P], ident)
                last.then_inc(s_xTp, 1)

            now = [pe.alloc_register(f"expert{i}") for i in range(4)]
            before = [pe.alloc_register(f"expert_before{i}") for i in range(2)]
            expert = [None] * 4

            def step(u, i):
                k, kk, par = 4 * u + i, 2 * u + i // 2, i % 2
                if i == 0:
                    if not isinstance(k, int) or k >= 4:
                        for old, new in zip(before, now[2:]):
                            pe.reg_mov(old, new)
                    if not isinstance(k, int) or k < ET:
                        pe.load(now, expert_of_tile[0:1, bass.ds(4 * u, 4)])
                if not isinstance(k, int) or k >= 2:
                    e_down = pe.snap(before[i], min_val=0, max_val=E - 1) if i < 2 else expert[i - 2]
                if not isinstance(k, int) or k < ET:
                    e_up = expert[i] = pe.snap(now[i], min_val=0, max_val=E - 1)
                if not isinstance(k, int) or k + 1 < ET:
                    turn_rows(u + (i + 1) // 4, (i + 1) % 4)
                if not isinstance(k, int) or k >= 2:
                    pe.wait_ge(s_hTe, k - 1)
                    if not isinstance(k, int) or k >= 4:
                        pe.wait_ge(s_ye, k - 3)
                    mm(bank[5 + par], hidT[par], w3[:, bass.ds(e_down, 1), :].rearrange("p a l -> p (a l)"),
                       start=True, stop=True).then_inc(s_down, 1)
                if not isinstance(k, int) or k < ET:
                    pe.wait_ge(s_xTe, k + 1)
                    if not isinstance(k, int) or k >= 2:
                        pe.wait_ge(s_hb, k - 1)
                for j in range(S):
                    if j == 2 and (not isinstance(k, int) or 1 <= k <= ET):
                        pe.wait_ge(s_hg, k)
                        nc.tensor.transpose(bank[4][:, 0:P], hid[1 - par], ident).then_inc(s_hTp, 1)
                    if not isinstance(k, int) or k < ET:
                        last = mm(bank[2 + par][:, 0:2 * INTER], xgT[par][:, j],
                                  w12[:, bass.ds(e_up, 1), j, :].rearrange("p a m -> p (a m)"),
                                  start=(j == 0), stop=(j == S - 1))
                if not isinstance(k, int) or k < ET:
                    last.then_inc(s_up, 1)

            turn_rows(0, 0)
            pe.wait_ge(s_zadd, TT)
            over_tiles(pe, step, ET)
            last_down = lambda: step((ET + 1) // 4, (ET + 1) % 4)

            def match_high(j, par):
                mm(bank[0], match[:, 0, par], bits_now[j].bitcast(F8), start=True, stop=True).then_inc(s_mh, 1)

            def match_low(j, par):
                mm(bank[1], match[:, 1, par], bits_now[j].bitcast(F8), start=True, stop=True).then_inc(s_ml, 1)

            def look_up(t, i):
                if i % 2 == 0:
                    pe.wait_ge(s_l8, t + 1)
                for h in range(HALVES):
                    last = mm(bank[2 + 2 * (i % 2) + h], lut8_halves[i // 2 % 2][:, h, i % 2], hot_hi[i % 2],
                              start=True, stop=True)
                last.then_inc(s_G, 1)

            def turn_low(r, i):
                if i % 2 == 0:
                    pe.wait_ge(s_wlfree, BLOCK // 2 * r + i // 2 + 1)
                for j in range(LT):
                    at = PARTS * G8 * (2 * j + i % 2)
                    last = mm(bank[7][:, at:at + PARTS * G8], hot_lo[i % 4][:, P * j:P * j + P],
                              lut4_parts[:, bass.ds(BLOCK * r + i, 1)].rearrange("p a k c -> p (a k c)"), start=True, stop=True)
                if i % 2 == 1:
                    last.then_inc(s_wl, 1)

            def dequantise(r, i):
                g = BLOCK * r + i
                ahead = lambda n: not isinstance(g, int) or g + n < NG
                if ahead(2):
                    pe.wait_ge(s_hi, g + 3)
                if ahead(3):
                    t = (i + 3) // 2
                    if i % 2 == 1:
                        pe.wait_ge(s_now[t % 2], 16 * (BLOCK // 4 * r + t // 2 + 1))
                    pe.nop(nofuse=True)
                    match_high(t % 2, (i + 1) % 2)
                if ahead(2):
                    pe.wait_ge(s_lo, g + 3)
                if ahead(3):
                    pe.nop(nofuse=True)
                    match_low(t % 2, (i + 1) % 2)
                pe.wait_ge(s_prod, g + 1)
                if ahead(2):
                    look_up(BLOCK // 2 * r + (i + 2) // 2, (i + 2) % BLOCK)
                if i == 0:
                    pe.wait_ge(s_wrows, r + 1)
                for h in range(HALVES):
                    last = mm(bank[6], place[:, P - G8 - G8 * i:2 * P - G8 - G8 * i], prod[i % 4][:, h],
                              start=(i == 0 and h == 0), stop=(i == BLOCK - 1 and h == HALVES - 1))
                if i == BLOCK - 1:
                    last.then_inc(s_wblock, 1)
                if ahead(1):
                    turn_low(r, i + 1)

            pe.wait_ge(s_match, 2)
            pe.wait_ge(s_l4p, 1)
            pe.wait_ge(s_now[0], 16)
            match_high(0, 0)
            match_low(0, 0)
            last_down()
            for g in (1, 2):
                pe.wait_ge(s_hi, g)
                if g == 2:
                    pe.wait_ge(s_now[1], 16)
                pe.nop(nofuse=True)
                match_high(g // 2, g % 2)
                pe.wait_ge(s_lo, g)
                pe.nop(nofuse=True)
                match_low(g // 2, g % 2)
                if g == 2:
                    pe.wait_ge(s_ye, ET)
                look_up(0, g - 1)
            turn_low(0, 0)
            pe.wait_ge(s_place, 1)
            with pe.Fori(0, NBLOCK - 1) as r:
                for i in range(BLOCK):
                    dequantise(r, i)
            for i in range(BLOCK):
                dequantise(NBLOCK - 1, i)

            def linear_in(t):
                pe.wait_ge(s_comb, TOPK * (t + 1))
                if t >= 2:
                    pe.wait_ge(s_aT, t - 1)
                for j in range(LT):
                    last = mm(bank[t % 2][:, P * j:P * j + P], x_rows[:, t, P * j:P * j + P], bd[:, t], start=True, stop=True)
                last.then_inc(s_amm, 1)

            linear_in(0)
            linear_in(1)
            pe.wait_ge(s_wrows, NBLOCK + 1)
            for j in range(LT):
                for r in range(NBLOCK):
                    last = nc.tensor.transpose(turned_bank(j)[:, P * r:P * r + P], w_rows[:, r, P * j:P * j + P], ident)
                last.then_inc(s_wTp, 1)

            def norms(t):
                pe.wait_ge(s_sqsum, t + 1)
                if t >= 1:
                    pe.wait_ge(s_high, t)
                mm(bank[5][:, 0:1], sq_sum[t % 2], ones[:, 0:1], start=True, stop=True).then_inc(s_norm, 1)

            for t in range(TT):
                if 1 <= t < TT - 1:
                    linear_in(t + 1)
                pe.wait_ge(s_aTlo, t + 1)
                if t >= 2:
                    pe.wait_ge(s_ylc, t - 1)
                    pe.wait_ge(s_ysel, t - 1)
                for b, w, ready in ((6, wTl, 0), (3, wTh, LT)):
                    terms = [(j, ha, hw) for j in range(LT) for ha, hw in ((1, 0), (0, 1), (0, 0))]
                    for n, (j, ha, hw) in enumerate(terms):
                        if t == 0 and n % 3 == 0:
                            pe.wait_ge(s_wlo, ready + j + 1)
                        last = mm(bank[b + t % 2], aT_halves[t % 2][:, ha, j], w[:, hw, j],
                                  start=(n == 0), stop=(n == len(terms) - 1))
                    last.then_inc(s_ymm, 1)
                    if b == 6 and t > 0:
                        norms(t)
                if t == 0:
                    norms(0)


def conv_weights(w):
    out = np.zeros((S, C, 3, S, C), w.dtype)
    pad, per = TAPS // 2, C // GROUPS
    for o in range(C):
        g = o // per
        for j in range(S):
            for k in range(TAPS):
                rel = j + k - pad
                out[rel % S, g * per:(g + 1) * per, rel // S + 1, j, o] = w[o, :, k]
    return out.reshape(P, 3, P)


def packed(table, parts, dtype=np.float32):
    at, width = spans(table)
    out = np.zeros((P, width), dtype)
    for name, a in parts.items():
        a = a.reshape(a.shape[0], -1)
        out[:a.shape[0], at[name].start:at[name].start + a.shape[1]] = a
    return out


def constants():
    p = np.arange(P)
    bits = lambda x, k: x >> k & 1
    match = np.zeros((2, P, 2, P), np.float32)
    for half in range(2):
        for plane in range(4):
            for par in range(2):
                for o in range(G8):
                    row = (4 * half + plane) * OI + par * G8 + o
                    match[half, row, par, 16 * o:16 * o + 16] = np.where(bits(np.arange(16), plane), 0.5, -0.5)
    ksel = np.zeros((KE, KT, KE // KT, C), np.float32)
    for k in range(KE):
        ksel[k, k // (KE // KT), k % (KE // KT)] = 1
    ones = np.array([bin(x).count("1") for x in range(16)])
    return packed(CONST, {
        "ident": np.eye(P), "iota": np.tile(p, (P, 1)), "rev": np.tile(E - np.arange(E), (P, 1)),
        "thr": np.tile(P * np.arange(TT), (P, 1)), "tri": np.tile(np.tri(E, k=-1).reshape(-1), (P, 1)),
        "blk": p[:, None] // C == np.arange(NT), "dmask": p[:, None] % C == np.arange(C), "pidx": p[:, None],
        "tbase": np.tile(P * np.arange(TT), (P, 1)), "ksel": ksel, "upper": p[:, None] < p,
        "mlo": match[0], "mhi": match[1], "mbias": 1 - ones[p % 16][:, None], "ones8": p[:, None] // 16 == np.arange(G8)})


def layout(i):
    a = {k: np.ascontiguousarray(v) for k, v in i.items()}
    rep = lambda v, n=P: np.broadcast_to(v, (n,) + v.shape)
    x4 = np.zeros((S, C, N, NB + 2), a["x"].dtype)
    x4[..., 1:NB + 1] = a["x"].reshape(N, C, NB, S).transpose(3, 1, 0, 2)
    blocks = lambda w: w.reshape(w.shape[:-2] + (NB, S, w.shape[-1]))
    ew12 = np.concatenate([blocks(a["L0_ffn_ew1"]), blocks(a["L0_ffn_ew2"])], -1)
    sw12 = np.concatenate([blocks(a["L0_ffn_sw1"]), blocks(a["L0_ffn_sw2"])], -1)
    q = a["L1_ffn_qweight"]
    lut8 = np.zeros((NG, G8, 16, G8, 16), a["L1_ffn_lut8"].dtype)
    lut4 = np.zeros((G8, 16, NG, G8), a["L1_ffn_lut4"].dtype)
    l8 = a["L1_ffn_lut8"].reshape(NG, G8, 16, 16)
    l4 = a["L1_ffn_lut4"].reshape(NG, G8, 16)
    for o in range(G8):
        lut8[:, o, :, o, :] = l8[:, o]
        lut4[o, :, :, o] = l4[:, o].T
    small = packed(SMALL, {
        "cT": a["cond_128"].T, "cwT": a["L0_cond_c_weight"].T, "W0": a["L1_cond_W0"], "W1": a["L1_cond_W1"],
        "W2": a["L1_cond_W2"], "b0": a["L1_cond_b0"][:, None], "b1": a["L1_cond_b1"][:, None],
        "sb1": a["L0_ffn_sb1"].reshape(MC, P).T, "sb2": a["L0_ffn_sb2"].reshape(MC, P).T,
        "wk": a["L1_cond_weight"][..., 0].reshape(KT, KE // KT, C, C).transpose(1, 3, 0, 2).reshape(P, KT, C),
        "rw": blocks(a["L0_ffn_router_w"]), "convb": rep(a["fside_S_0"], N), "b2": rep(a["L1_cond_b2"], N),
        "bk": a["L1_cond_bias_k"], "rb": rep(a["L0_ffn_router_b"]), "rbias": rep(a["L0_ffn_router_bias"])})
    return {
        "small": small, "const": constants(), "x4": x4.reshape(P, N, NB + 2), "wconv": conv_weights(a["L0_cond_weight"]),
        "x_rows": a["x"].reshape(TT, P, L).transpose(1, 0, 2), "w12": ew12.transpose(1, 0, 2, 3),
        "w3": a["L0_ffn_ew3"].transpose(1, 0, 2), "sw12": sw12, "sw3": a["L0_ffn_sw3"].reshape(MC, P, L).transpose(1, 0, 2),
        "b3x": np.concatenate([a["L0_ffn_eb3"], a["L0_ffn_sb3"][None]]),
        "b12": np.concatenate([a["L0_ffn_eb1"], a["L0_ffn_eb2"]], -1),
        "q": q.reshape(8, QT, OI, L // 32).transpose(0, 2, 1, 3).reshape(P, QT, L // 32),
        "lut8": lut8.reshape(QT, 2, P, P).transpose(0, 2, 1, 3), "lut4": lut4.reshape(P, NG, G8), "ybias": a["L1_ffn_bias"],
    }


def kernel(**inputs):
    import concourse.bacc as bacc
    from concourse.bass_utils import run_bass_kernel_spmd

    nc = bacc.Bacc("TRN2", target_bir_lowering=False, num_devices=1)
    arrays, A = {}, {}
    for name, a in layout(inputs).items():
        a = np.ascontiguousarray(a)
        arrays[f"in_{name}"] = a
        A[name] = nc.dram_tensor(f"in_{name}", a.shape, mybir.dt.from_np(a.dtype), kind="ExternalInput").ap()
    A["out"] = nc.dram_tensor("out", (T, L), F32, kind="ExternalOutput").ap()
    build(nc, A)
    r = run_bass_kernel_spmd(nc, [arrays], core_ids=[0])
    return r.results[0]["out"].reshape(N, C, L)
```
